# Optimizing a Trainium2 kernel written in Bass

```python
import numpy as np
import jax
import jax.numpy as jnp

def _softmax(x, axis=-1):
    return jax.nn.softmax(x, axis=axis)
def _gelu(x):
    return jax.nn.gelu(x, approximate=True)
def _silu(x):
    return jax.nn.silu(x)
def _sigmoid(x):
    return jax.nn.sigmoid(x)
def _layernorm(x, axis=-1, eps=1e-5):
    m = jnp.mean(x, axis=axis, keepdims=True)
    v = jnp.var(x, axis=axis, keepdims=True)
    return (x - m) / jnp.sqrt(v + eps)
def _scatter_add(tgt, idx, src, axis=0):
    return tgt.at[idx].add(src)
def _segment_sum(src, seg, n):
    return jax.ops.segment_sum(src, seg, n)

kernel_name = 'mk_adj_resnorm_d1_adj_256_921910'

def setup_inputs(seed: int = 0):
    np.random.seed(seed)
    _w = jnp.asarray
    def _rec_inputs():
        import jax
        import jax.numpy as jnp
        _gk = jax.random.key(seed)
        x = -0.0002928 + 1 * jax.random.normal(jax.random.fold_in(_gk, 1), (16, 1024, 256), jnp.float32)
        _w = (1.0 + jnp.arange(1024, dtype=jnp.float32)) ** -0.5
        _w = _w / _w.mean()
        _pij = jnp.clip(0.0078125 * _w[:, None] * _w[None, :], 0.0, 1.0)
        _a = jax.random.uniform(jax.random.fold_in(_gk, 2), (1024, 1024)) < _pij
        adj = _a.astype(jnp.int32)
        return x, adj
    x, adj = _rec_inputs()
    def _L0_gnn_setup():
        import jax, jax.numpy as jnp
        import numpy as np
        ALPHA = 0.2
        NEG_INF = -9000000000000000.0

        def _gat(inp, adj_mask, W, a):
            h = jnp.matmul(inp, W)
            F_ = h.shape[-1]
            f1 = jnp.matmul(h, a[:F_, 0])
            f2 = jnp.matmul(h, a[F_:, 0])
            e = jax.nn.leaky_relu(f1[:, :, None] + f2[:, None, :], ALPHA)
            if adj_mask is not None:
                e = jnp.where(adj_mask[None, :, :] > 0, e, NEG_INF)
            att = jax.nn.softmax(e, axis=2)
            h_prime = jnp.einsum('bij,bjf->bif', att, h)
            return jax.nn.elu(h_prime)
        key = jax.random.key(seed)
        ks = jax.random.split(key, 10)
        B, N, Fin, H, O = (16, 1024, 256, 512, 256)

        def xavier(k, shape):
            fan_in, fan_out = (shape[0], shape[-1])
            bound = 1.414 * np.sqrt(6.0 / (fan_in + fan_out))
            return jax.random.uniform(k, shape, jnp.float32, -bound, bound)
        return {'x': jax.random.normal(ks[0], (B, N, Fin), jnp.float32), 'adj': jax.random.randint(ks[1], (N, N), 0, 2, jnp.int32), 'mlp1_w': xavier(ks[2], (Fin, H)), 'mlp1_b': jnp.zeros((H,), jnp.float32), 'mlp2_w': xavier(ks[3], (H, O)), 'mlp2_b': jnp.zeros((O,), jnp.float32), 'W_fc': xavier(ks[4], (H, H)), 'a_fc': xavier(ks[5], (2 * H, 1)), 'W_hand': xavier(ks[6], (O, O)), 'a_hand': xavier(ks[7], (2 * O, 1))}
    _L0_gnn_all = _L0_gnn_setup()
    _L0_gnn_in = {k: v for k, v in _L0_gnn_all.items() if k in ('mlp1_w', 'mlp1_b', 'mlp2_w', 'mlp2_b', 'W_fc', 'a_fc', 'W_hand', 'a_hand', )}
    del _L0_gnn_all

    return {
        "x": x,
        "adj": adj,
        "L0_gnn_mlp1_w": _L0_gnn_in["mlp1_w"],
        "L0_gnn_mlp1_b": _L0_gnn_in["mlp1_b"],
        "L0_gnn_mlp2_w": _L0_gnn_in["mlp2_w"],
        "L0_gnn_mlp2_b": _L0_gnn_in["mlp2_b"],
        "L0_gnn_W_fc": _L0_gnn_in["W_fc"],
        "L0_gnn_a_fc": _L0_gnn_in["a_fc"],
        "L0_gnn_W_hand": _L0_gnn_in["W_hand"],
        "L0_gnn_a_hand": _L0_gnn_in["a_hand"],
    }

def reference(x, adj, L0_gnn_mlp1_w, L0_gnn_mlp1_b, L0_gnn_mlp2_w, L0_gnn_mlp2_b, L0_gnn_W_fc, L0_gnn_a_fc, L0_gnn_W_hand, L0_gnn_a_hand):
    import jax
    import jax.numpy as jnp
    def _L0_gnn_ref(x, adj, mlp1_w, mlp1_b, mlp2_w, mlp2_b, W_fc, a_fc, W_hand, a_hand):
        import jax, jax.numpy as jnp
        import numpy as np
        ALPHA = 0.2
        NEG_INF = -9000000000000000.0

        def _gat(inp, adj_mask, W, a):
            h = jnp.matmul(inp, W)
            F_ = h.shape[-1]
            f1 = jnp.matmul(h, a[:F_, 0])
            f2 = jnp.matmul(h, a[F_:, 0])
            e = jax.nn.leaky_relu(f1[:, :, None] + f2[:, None, :], ALPHA)
            if adj_mask is not None:
                e = jnp.where(adj_mask[None, :, :] > 0, e, NEG_INF)
            att = jax.nn.softmax(e, axis=2)
            h_prime = jnp.einsum('bij,bjf->bif', att, h)
            return jax.nn.elu(h_prime)
        out = jax.nn.relu(jnp.matmul(x, mlp1_w) + mlp1_b)
        residual = out
        out = _gat(jax.nn.relu(out), None, W_fc, a_fc)
        out = jax.nn.elu(out) + residual
        out = jax.nn.relu(jnp.matmul(out, mlp2_w) + mlp2_b)
        residual = out
        out = _gat(jax.nn.relu(out), adj, W_hand, a_hand)
        out = jax.nn.elu(out) + residual
        return jax.nn.relu(out)

    x = _layernorm(x + _L0_gnn_ref(x, adj, L0_gnn_mlp1_w, L0_gnn_mlp1_b, L0_gnn_mlp2_w, L0_gnn_mlp2_b, L0_gnn_W_fc, L0_gnn_a_fc, L0_gnn_W_hand, L0_gnn_a_hand), axis=-1)
    return x


_drawn_inputs = setup_inputs


def setup_inputs(seed=0):
    import zlib

    import numpy as np

    out = dict(_drawn_inputs(seed))
    spreads = {'L0_gnn_mlp1_b': (0.0, 0.1), 'L0_gnn_mlp2_b': (0.0, 0.1)}
    factors = {}
    for name, (base, spread) in spreads.items():
        noise = np.random.default_rng([zlib.crc32(name.encode()), seed]).standard_normal(out[name].shape)
        drawn = base * np.exp(spread * noise) if base else spread * noise
        out[name] = jnp.asarray(drawn.astype(out[name].dtype))
    for name, factor in factors.items():
        out[name] = (out[name] * factor).astype(out[name].dtype)
    return out
```

```python
from contextlib import ExitStack

import concourse.bass as bass
from concourse import mybir

ALU = mybir.AluOpType
ACT = mybir.ActivationFunctionType
AX_X = mybir.AxisListType.X
F32 = mybir.dt.float32
F32R = mybir.dt.float32r
BF16 = mybir.dt.bfloat16
U8 = mybir.dt.uint8
I32 = mybir.dt.int32
RMAX = bass.bass_isa.ReduceOp.max

P = 128
HALF = 512
ALPHA = 0.2
EPS = 1e-5
SHRINK = 2.0 ** -60
GROW = 2.0 ** 60
NO_NEIGHBOUR = -1e17


def gnn_layer_kernel(nc, xT, x, adj, adjT, w1, b1, w2, b2, wf, af, wh, ah, keep_dram, out):
    B = xT.shape[0] // (2 * P)
    H = w1.shape[1]
    F = w1.shape[0]
    O = w2.shape[1]
    N = adj.shape[0]
    NT = N // P
    KF, KH, KO = F // P, H // P, O // P
    TH = NT // 2
    NP_ = 2 * NT
    RING = 4

    with ExitStack() as ctx:
        def sb(name, shape, dt):
            return ctx.enter_context(nc.sbuf_tensor(name, shape, dt))

        def sem(name):
            return ctx.enter_context(nc.semaphore(name))

        w1h = sb("w1h", [P, KF, H], F32R)
        w1l = sb("w1l", [P, KF, H], F32R)
        wfh = sb("wfh", [P, KH, H], F32R)
        wfl = sb("wfl", [P, KH, H], F32R)
        w2h = sb("w2h", [P, KH, O], F32R)
        w2l = sb("w2l", [P, KH, O], F32R)
        whh = sb("whh", [P, KO, O], F32R)
        whl = sb("whl", [P, KO, O], F32R)
        b1c = sb("b1c", [P, KH], F32)
        b2c = sb("b2c", [P, KO], F32)
        afr = sb("afr", [P, 2, H], F32)
        ahr = sb("ahr", [P, 2, O], F32)
        noT = sb("noT", [P, NT, N], U8)
        noD = sb("noD", [P, 2, N], U8)
        ident = sb("ident", [P, P], F32)
        identr = sb("identr", [16, 16], F32R)
        ones = sb("ones", [P, 1], F32)
        minus1 = sb("minus1", [P, 1], F32)
        powh = sb("powh", [P, 2], F32)
        epsc = sb("epsc", [P, 2], F32)
        xf = sb("xf", [P, KF, HALF], F32)
        xh = sb("xh", [P, KF, HALF], F32R)
        xl = sb("xl", [P, KF, HALF], F32R)
        o1f = sb("o1f", [P, KH, N], F32)
        o1h = sb("o1h", [P, KH, HALF], F32R)
        o1l = sb("o1l", [P, KH, HALF], F32R)
        gh = sb("gh", [P, KH * HALF], F32R)
        gl = sb("gl", [P, KH * HALF], F32R)
        h1h = sb("h1h", [P, NT, H], F32R)
        h1l = sb("h1l", [P, NT, H], F32R)
        ph = sb("ph", [P, RING, HALF], F32R)
        pl = sb("pl", [P, RING, HALF], F32R)
        o2f = sb("o2f", [P, KO, N], F32)
        pf = sb("pf", [P, 2, HALF], F32)
        acc = sb("acc", [P, HALF], F32)
        rz = sb("rz", [P, HALF], F32)
        arow = sb("arow", [P, HALF], F32)
        tb = sb("tb", [P, 2, HALF], F32)
        yb = sb("yb", [P, 2, HALF], F32)
        eb = sb("eb", [P, 2, HALF], F32)
        vb = sb("vb", [P, 2, 2 * F], F32)
        brow = sb("brow", [P, N], F32)
        r1row = sb("r1row", [P, HALF], F32)
        r2row = sb("r2row", [P, HALF], F32)
        junk = sb("junk", [P, N], BF16)
        prod = sb("prod", [P, H], BF16)
        f1c = sb("f1c", [P, NT], F32)
        f2c = sb("f2c", [P, NT], F32)
        fmx = sb("fmx", [P, 1], F32)
        fall = sb("fall", [P, 1], F32)
        nfa = sb("nfa", [P, 1], F32)
        nfb = sb("nfb", [P, 1], F32)
        sc = sb("sc", [P, NT], F32)
        uc = sb("uc", [P, NT], F32)
        vc = sb("vc", [P, NT], F32)
        bc = sb("bc", [P, NT], F32)
        g1c = sb("g1c", [P, NT], F32)
        g2c = sb("g2c", [P, NT], F32)
        g2s = sb("g2s", [P, NT], F32)
        g2a = sb("g2a", [P, NT], F32)
        mx = sb("mx", [P, NT], F32)
        mxc = sb("mxc", [P, NT], F32)
        emp = sb("emp", [P, NT], F32)
        lg = sb("lg", [P, NT], F32)
        mc = sb("mc", [P, NT], F32)
        r1t = sb("r1t", [P, NT], F32)
        r2t = sb("r2t", [P, NT], F32)
        rc = sb("rc", [P, 2 * NT], F32)
        rTh = sb("rTh", [2 * NT, P], F32R)
        rTl = sb("rTl", [2 * NT, P], F32R)
        f2Th, bTh, bTl = rTh[0:NT, :], rTh[0:NT, :], rTl[0:NT, :]
        bst = sb("bst", [P, 2, 6], F32)
        bmv = sb("bmv", [P, 2, 2], F32)
        rst = sb("rst", [P, 2], F32)
        rsd = sb("rsd", [P, 2], F32)

        gview_h = gh[:, :].rearrange("p (k n) -> p k n", k=KH)
        gview_l = gl[:, :].rearrange("p (k n) -> p k n", k=KH)
        h2h = gh[:, :].rearrange("p (t n) -> p t n", t=NT)
        h2l = gl[:, :].rearrange("p (t n) -> p t n", t=NT)
        o2h = ph[:, :, :].rearrange("p (k a) n -> p k (a n)", k=KO)
        o2l = pl[:, :, :].rearrange("p (k a) n -> p k (a n)", k=KO)
        wst = o1f[:, :, :].rearrange("p k n -> p (k n)")
        ast = o2f[:, :, :].bitcast(I32)

        bank = [ctx.enter_context(nc.psum_tensor(f"bank{i}", [P, HALF], F32)) for i in range(6)]
        row2 = ctx.enter_context(nc.psum_tensor("row2", [P, 2, HALF], F32))
        bank += [row2[:, 0, :], row2[:, 1, :]]

        names = """
        ld_w ld_b ld_a ld_adj0 ld_adj1 st_keep ld_x0 ld_keep0 ld_keep1 ld_xn0 ld_xn1 st_out0 st_out1
        const_ready ident0
        wh_ready wl_ready noT_ready noD_ready
        x_hi x_lo o1_f o1_hi o1_lo h1_hi h1_lo h1_f h1_fj
        col_max all_max shift_ready uvb_ready bT_hi bT_lo brow_ready
        p1_f p1_hi p1_lo p1_lo2 acc1 rz1 y1 m1 e1a e1 r1 g1 g1_hi g1_lo
        o2_f o2_hi o2_lo h2_hi h2_lo h2_f h2_fj g2s_ready f2T_ready row_max
        rstep rT_hi rT_lo rrow_ready
        a2 t2 t2m p2_f p2_hi p2_lo p2_lo2 acc2 rz2 y2 m2 e2a e2 r2 w2_done
        v_ready st_ready mv_ready ve_ready rs_ready o_ready
        pe_mlp1 pe_h1 pe_p1 pe_z1 pe_mlp2 pe_h2 pe_f2T pe_f2row pe_rT pe_rrow pe_p2 pe_z2 pe_bT pe_brow pe_tr
        """.split()
        S = {n: sem(n) for n in names}

        block = ctx.enter_context(nc.Block())

        def f(ap):
            return ap.bitcast(F32)

        @block.sync
        def _(sp):
            rows = [(w1, KF * H), (wf, KH * H), (w2, KH * O), (wh, KO * O)]
            sp.dma_start(b1c[:, :], b1).then_inc(S["ld_b"], 16)
            sp.dma_start(b2c[:, :], b2).then_inc(S["ld_b"], 16)
            sp.dma_start(afr[:, :, :].rearrange("p a n -> p (a n)"), af.partition_broadcast(P)).then_inc(S["ld_a"], 16)
            sp.dma_start(ahr[:, :, :].rearrange("p a n -> p (a n)"), ah.partition_broadcast(P)).then_inc(S["ld_a"], 16)
            for n, (w, size) in enumerate(rows):
                k = size // (HALF * (w.shape[1] // HALF if w.shape[1] >= HALF else 1))
                if n >= 1:
                    sp.wait_ge(S["wl_ready"], n)
                kk = w.shape[0] // P
                sp.dma_start(wst[:, 0:size].rearrange("p (k n) -> p k n", k=kk),
                             w.rearrange("(k p) n -> p k n", p=P)).then_inc(S["ld_w"], 16)
            for t in range(2 * NT):
                if t >= 2:
                    sp.wait_ge(S["noT_ready"] if t % 2 == 0 else S["noD_ready"], t // 2)
                src = adjT if t % 2 == 0 else adj
                sp.dma_start(ast[:, t % 2, :], src[(t // 2) * P:(t // 2 + 1) * P, :])\
                    .then_inc(S["ld_adj0"] if t % 2 == 0 else S["ld_adj1"], 16)
                if t % 2 == 1:
                    sp.wait_ge(S["noD_ready"], t // 2 + 1)
                    sp.dma_start(keep_dram[(t // 2) * P:(t // 2 + 1) * P, :], noD[:, (t // 2) % 2, :])\
                        .then_inc(S["st_keep"], 16)
            sp.wait_ge(S["st_keep"], 16 * NT)

            def load_x(b, h, first):
                if not first:
                    sp.wait_ge(S["x_lo"], 2 * b + h)
                    sp.wait_ge(S["x_hi"], 2 * b + h)
                sp.dma_start(xf[:, :, :].rearrange("p k n -> p (k n)"), xT[bass.ts(2 * b + h, P), :])\
                    .then_inc(S["ld_x0"], 16)

            def load_masks(b, first):
                for t in range(NT):
                    if not (first and t < 2):
                        sp.wait_ge(S["row_max"], NT * b + t - 1)
                    sp.dma_start(noD[:, t % 2, :], keep_dram[t * P:(t + 1) * P, :])\
                        .then_inc(S["ld_keep0"] if t % 2 == 0 else S["ld_keep1"], 16)

            def load_chunk(b, c, first):
                if not (first and c < 2):
                    sp.wait_ge(S["st_out0"] if c % 2 == 0 else S["st_out1"], 32 * b + 16 * (c // 2))
                sp.dma_start(vb[:, c % 2, :], x[bass.ts(4 * b + c, P), :])\
                    .then_inc(S["ld_xn0"] if c % 2 == 0 else S["ld_xn1"], 16)

            def store_chunk(b, c):
                sp.wait_ge(S["o_ready"], 8 * b + 2 * c + 2)
                sp.dma_start(out[bass.ts(4 * b + c, P), :], vb[:, c % 2, :])\
                    .then_inc(S["st_out0"] if c % 2 == 0 else S["st_out1"], 16)

            def body(b, first, last):
                if not last:
                    load_x(b + 1, 0, False)
                    load_x(b + 1, 1, False)
                load_masks(b, first)
                load_chunk(b, 0, first)
                load_chunk(b, 1, first)
                store_chunk(b, 0)
                load_chunk(b, 2, False)
                store_chunk(b, 1)
                load_chunk(b, 3, False)
                store_chunk(b, 2)
                store_chunk(b, 3)

            load_x(0, 0, True)
            load_x(0, 1, False)
            body(0, True, False)
            with sp.Fori(1, B - 1) as b:
                body(b, False, False)
            body(B - 1, False, True)
            sp.wait_ge(S["st_out0"], 32 * B)
            sp.wait_ge(S["st_out1"], 32 * B)

        @block.tensor
        def _(pe):
            def mm3(dst, ah_, al_, bh_, bl_, start, stop):
                nc.tensor.matmul(dst, ah_, bh_, start=start, stop=False)
                nc.tensor.matmul(dst, ah_, bl_, start=False, stop=False)
                return nc.tensor.matmul(dst, al_, bh_, start=False, stop=stop)

            def mlp1(b, h, first):
                pe.wait_ge(S["x_hi"], 2 * b + h + 1)
                pe.wait_ge(S["x_lo"], 2 * b + h + 1)
                for m in range(KH):
                    if m >= 2:
                        pe.wait_ge(S["o1_hi"], 8 * b + 4 * h + m - 1)
                    elif h == 0 and not first:
                        pe.wait_ge(S["o2_f"], 4 * b - 2)
                    elif h == 1 and not first:
                        pe.wait_ge(S["y1"], 8 * b)
                    dst = bank[(2, 4)[h] + m % 2][:, :]
                    for k in range(KF):
                        w = slice(m * P, (m + 1) * P)
                        mm = mm3(dst, w1h[:, k, w], w1l[:, k, w], xh[:, k, :], xl[:, k, :], k == 0, k == KF - 1)
                    mm.then_inc(S["pe_mlp1"], 1)

            def proj1(b, h, first, qs=range(4)):
                for q in qs:
                    if q == 0:
                        pe.wait_ge(S["o1_hi"], 8 * b + 4 * h + 4)
                        pe.wait_ge(S["o1_lo"], 8 * b + 4 * h + 4)
                    if q >= 2:
                        pe.wait_ge(S["h1_f"], 8 * b + 4 * h + q - 1)
                    elif h == 0 and not first:
                        pe.wait_ge(S["rz1"], 2 * b)
                    dst = bank[(6, 4)[h] + q % 2][:, :] if h else bank[6 + q % 2]
                    n = slice(q * P, (q + 1) * P)
                    for k in range(KH):
                        mm = mm3(dst, o1h[:, k, n], o1l[:, k, n], wfh[:, k, :], wfl[:, k, :], k == 0, k == KH - 1)
                    mm.then_inc(S["pe_h1"], 1)

            def agg1(b, h, js, first):
                banks = (0, 1, 2, 3) if h == 0 else (4, 5, 0, 1)
                for j in js:
                    n = NT * h + j
                    pe.wait_ge(S["p1_hi"], NP_ * b + n + 1)
                    if h == 0:
                        pe.wait_ge(S["p1_lo"], NT * b + j + 1)
                    else:
                        pe.wait_ge(S["p1_lo2"], NT * b + j + 1)
                    for m in range(KH):
                        if j == 0 and h == 0 and m == 0 and not first:
                            pe.wait_ge(S["v_ready"], 8 * b - 4)
                        if j == 0 and h == 0 and m == 2:
                            pe.wait_ge(S["brow_ready"], 2 * b + 2)
                        if j == 0 and h == 1 and m == 0 and not first:
                            pe.wait_ge(S["v_ready"], 8 * b)
                        if j == 0 and h == 1 and m >= 2:
                            pe.wait_ge(S["y1"], 8 * b + m - 1)
                        w = slice(m * P, (m + 1) * P)
                        mm = mm3(bank[banks[m]][:, :], h1h[:, j, w], h1l[:, j, w],
                                 ph[:, n % RING, :], pl[:, n % RING, :], j == 0, j == NT - 1)
                    mm.then_inc(S["pe_p1"], 1)

            def z1(b, h, first):
                pe.wait_ge(S["acc1"], NP_ * b + NT * h + NT)
                if not first:
                    pe.wait_ge(S["rz2"], 2 * b - 1 + h)
                nc.tensor.matmul(bank[6 + h], ones[:, 0:1].to_broadcast([P, P]), acc[:, :], start=True, stop=True).then_inc(S["pe_z1"], 1)

            def mlp2(b, h, last):
                pe.wait_ge(S["g1_hi"], 8 * b + 4 * h + 4)
                pe.wait_ge(S["g1_lo"], 8 * b + 4 * h + 4)
                if h == 0:
                    pe.wait_ge(S["y1"], 8 * b + 4)
                elif last:
                    pe.wait_ge(S["o2_f"], 4 * b + 2)
                else:
                    pe.wait_ge(S["o1_hi"], 8 * b + 12)
                for m in range(KO):
                    w = slice(m * P, (m + 1) * P)
                    for k in range(KH):
                        mm = mm3(bank[2 + m][:, :], w2h[:, k, w], w2l[:, k, w], gview_h[:, k, :], gview_l[:, k, :],
                                 k == 0, k == KH - 1)
                    mm.then_inc(S["pe_mlp2"], 1)

            def proj2(b):
                pe.wait_ge(S["o2_hi"], 4 * b + 4)
                pe.wait_ge(S["o2_lo"], 4 * b + 4)
                for t in range(NT):
                    if t < 2:
                        pe.wait_ge(S["y1"], 8 * b + 8)
                    else:
                        pe.wait_ge(S["h2_f"], NT * b + t - 1)
                    n = slice(t * P, (t + 1) * P)
                    for k in range(KO):
                        mm = mm3(bank[t % 2][:, 0:O], o2h[:, k, n], o2l[:, k, n], whh[:, k, :], whl[:, k, :],
                                 k == 0, k == KO - 1)
                    mm.then_inc(S["pe_h2"], 1)

            def spread(dst, rows_hi, rows_lo, c0, K):
                for q in range(4):
                    one = identr[0:K, c0 + q:c0 + q + 1].to_broadcast([K, P])
                    d = dst[:, q * P:(q + 1) * P]
                    mm = nc.tensor.matmul(d, one, rows_hi, start=True, stop=rows_lo is None)
                    if rows_lo is not None:
                        mm = nc.tensor.matmul(d, one, rows_lo, start=False, stop=True)
                return mm

            def f2_transpose(b):
                pe.wait_ge(S["h2_f"], NT * b + NT)
                pe.wait_ge(S["o2_f"], 4 * b + 4)
                nc.tensor.transpose(bank[2][0:NT, 0:P], g2c[:, :], ident[:, :]).then_inc(S["pe_f2T"], 1)

            def f2_spread(b, last):
                pe.wait_ge(S["f2T_ready"], b + 1)
                if last:
                    pe.wait_ge(S["rz1"], 2 * b + 2)
                else:
                    pe.wait_ge(S["h1_f"], 8 * b + 12)
                spread(bank[6], f2Th[:, :], None, 0, NT)
                spread(bank[7], f2Th[:, :], None, 4, NT).then_inc(S["pe_f2row"], 1)

            def r_transpose(b):
                pe.wait_ge(S["rstep"], 8 * b + 8)
                nc.tensor.transpose(bank[2][0:2 * NT, 0:P], rc[:, :], ident[:, :]).then_inc(S["pe_rT"], 1)

            def r_spread(b, h):
                if h == 0:
                    pe.wait_ge(S["rT_hi"], b + 1)
                    pe.wait_ge(S["rT_lo"], b + 1)
                else:
                    pe.wait_ge(S["rrow_ready"], 4 * b + 2)
                spread(bank[3][:, :], rTh[:, :], rTl[:, :], 4 * h, 2 * NT)
                spread(bank[2][:, :], rTh[:, :], rTl[:, :], NT + 4 * h, 2 * NT).then_inc(S["pe_rrow"], 1)

            def agg2(b, h, js, last):
                for j in js:
                    n = NT * h + j
                    pe.wait_ge(S["p2_hi"], NP_ * b + n + 1)
                    pe.wait_ge(S["p2_lo"] if n % 2 == 0 else S["p2_lo2"], NT * b + n // 2 + 1)
                    if j == 0 and h == 1:
                        if last:
                            pe.wait_ge(S["y1"], 8 * b + 8)
                        else:
                            pe.wait_ge(S["h1_f"], 8 * b + 16)
                    for m in range(KO):
                        w = slice(m * P, (m + 1) * P)
                        mm = mm3(bank[(0, 4)[h] + m][:, :], h2h[:, j, w], h2l[:, j, w],
                                 ph[:, n % RING, :], pl[:, n % RING, :], j == 0, j == NT - 1)
                    mm.then_inc(S["pe_p2"], 1)

            def z2(b, h):
                pe.wait_ge(S["acc2"], NP_ * b + NT * h + NT)
                pe.wait_ge(S["row_max"], NT * b + NT)
                nc.tensor.matmul(bank[6 + h], ones[:, 0:1].to_broadcast([P, P]), acc[:, :], start=True, stop=True).then_inc(S["pe_z2"], 1)

            def b_spread(b, first):
                pe.wait_ge(S["uvb_ready"], b + 1)
                if not first:
                    pe.wait_ge(S["rrow_ready"], 4 * b)
                nc.tensor.transpose(bank[3][0:NT, 0:P], bc[:, :], ident[:, :]).then_inc(S["pe_bT"], 1)
                pe.wait_ge(S["bT_hi"], b + 1)
                pe.wait_ge(S["bT_lo"], b + 1)
                spread(bank[2][:, :], bTh[:, :], bTl[:, :], 0, NT)
                spread(bank[3][:, :], bTh[:, :], bTl[:, :], 4, NT).then_inc(S["pe_brow"], 1)

            def transposes(b, h):
                pe.wait_ge(S["w2_done"], 4 * b + 2 * h + 2)
                for c in range(2):
                    for q in range(2):
                        t = 4 * h + 2 * c + q
                        for m in range(KO):
                            mm = nc.tensor.transpose(bank[(0, 4)[h] + c][:, q * O + m * P:q * O + (m + 1) * P],
                                                     o2f[:, m, t * P:(t + 1) * P], ident[:, :])
                    mm.then_inc(S["pe_tr"], 1)

            def body(b, first, last):
                agg1(b, 0, range(NT), first)
                z1(b, 0, first)
                agg1(b, 1, range(6), first)
                mlp2(b, 0, last)
                agg1(b, 1, range(6, NT), first)
                z1(b, 1, first)
                if not last:
                    mlp1(b + 1, 0, False)
                    proj1(b + 1, 0, False)
                mlp2(b, 1, last)
                if not last:
                    mlp1(b + 1, 1, False)
                proj2(b)
                f2_transpose(b)
                if not last:
                    proj1(b + 1, 1, False, range(1))
                f2_spread(b, last)
                if not last:
                    proj1(b + 1, 1, False, range(1, 4))
                r_transpose(b)
                r_spread(b, 0)
                agg2(b, 0, range(2), last)
                r_spread(b, 1)
                agg2(b, 0, range(2, NT), last)
                z2(b, 0)
                agg2(b, 1, range(2), last)
                if not last:
                    b_spread(b + 1, False)
                agg2(b, 1, range(2, NT), last)
                z2(b, 1)
                transposes(b, 0)
                transposes(b, 1)

            pe.wait_ge(S["const_ready"], 5)
            pe.wait_ge(S["wl_ready"], 4)
            pe.wait_ge(S["wh_ready"], 4)
            mlp1(0, 0, True)
            proj1(0, 0, True)
            mlp1(0, 1, True)
            proj1(0, 1, True)
            b_spread(0, True)
            body(0, True, False)
            with pe.Fori(1, B - 1) as b:
                body(b, False, False)
            body(B - 1, False, True)

        @block.vector
        def _(dve):
            def x_hi(b, h, first):
                dve.wait_ge(S["ld_x0"], 32 * b + 16 * h + 16)
                if not first:
                    dve.wait_ge(S["pe_mlp1"], 8 * b + 4 * h)
                dve.tensor_copy(xh[:, :, :], xf[:, :, :]).then_inc(S["x_hi"], 1)

            def h1_evac(b, t, first):
                src = bank[6 + t % 2] if t < 4 else bank[4 + t % 2][:, :]
                dve.wait_ge(S["h1_hi"], NT * b + t + 1)
                dve.tensor_tensor(h1l[:, t, :], src, f(h1h[:, t, :]), ALU.subtract).then_inc(S["h1_lo"], 1)
                dve.wait_ge(S["h1_f"], NT * b + t)
                if t == 4 and not first:
                    dve.wait_ge(S["h2_f"], NT * b)
                dve.tensor_tensor_reduce(prod[:, 0:H], src, afr[:, 0, :], 1.0, 0.0, ALU.mult, ALU.add,
                                         f1c[:, t:t + 1]).then_inc(S["h1_fj"], 1)
                dve.wait_ge(S["h1_fj"], NT * b + t + 1)
                dve.tensor_tensor_reduce(prod[:, 0:H], src, afr[:, 1, :], 1.0, 0.0, ALU.mult, ALU.add,
                                         f2c[:, t:t + 1]).then_inc(S["h1_f"], 1)

            def shifts(b):
                dve.wait_ge(S["h1_f"], NT * b + NT)
                dve.reduce_max(fmx[:, :], f2c[:, :], AX_X).then_inc(S["col_max"], 1)

            def shifts_rest(b):
                dve.wait_ge(S["all_max"], b + 1)
                dve.tensor_scalar(nfa[:, :], fall[:, :], -1.0, None, ALU.mult).then_inc(S["shift_ready"], 1)
                dve.tensor_scalar(nfb[:, :], fall[:, :], -ALPHA, None, ALU.mult).then_inc(S["shift_ready"], 1)
                dve.tensor_scalar(sc[:, :], f1c[:, :], fall[:, 0:1], 0.0, ALU.add, ALU.max)\
                    .then_inc(S["shift_ready"], 1)

            def b_parts(b):
                dve.wait_ge(S["pe_bT"], b + 1)
                dve.tensor_copy(bTh[:, :], bank[3][0:NT, 0:P]).then_inc(S["bT_hi"], 1)
                dve.wait_ge(S["bT_hi"], b + 1)
                dve.tensor_tensor(bTl[:, :], bank[3][0:NT, 0:P], f(bTh[:, :]), ALU.subtract)\
                    .then_inc(S["bT_lo"], 1)

            def p1_tile(b, n, first):
                j = n % NT
                if n == 0:
                    dve.wait_ge(S["brow_ready"], 2 * b + 2)
                    if not first:
                        dve.wait_ge(S["acc2"], NP_ * b)
                        dve.wait_ge(S["p2_lo2"], NT * b)
                        dve.wait_ge(S["p2_lo"], NT * b)
                        dve.wait_ge(S["p2_hi"], NP_ * b)
                if n >= 2:
                    dve.wait_ge(S["p1_hi"], NP_ * b + n - 1)
                    dve.wait_ge(S["acc1"], NP_ * b + n - 1)
                    if n - 2 < NT:
                        dve.wait_ge(S["p1_lo"], NT * b + n - 1)
                h = n // NT
                dve.tensor_scalar(pf[:, n % 2, :], brow[:, h * HALF:(h + 1) * HALF], vc[:, j:j + 1], uc[:, j:j + 1],
                                  ALU.mult, ALU.max).then_inc(S["p1_f"], 1)

            def p1_low(b, n):
                dve.wait_ge(S["p1_hi"], NP_ * b + n + 1)
                dve.wait_ge(S["pe_p1"], NP_ * b + n - RING + 1)
                dve.tensor_tensor(pl[:, n % RING, :], pf[:, n % 2, :], f(ph[:, n % RING, :]), ALU.subtract)\
                    .then_inc(S["p1_lo2"], 1)

            def recip1(b, h):
                dve.wait_ge(S["pe_z1"], 2 * b + h + 1)
                dve.wait_ge(S["y1"], 8 * b + 4 * h)
                dve.reciprocal(rz[:, :], bank[6 + h]).then_inc(S["rz1"], 1)
                dve.wait_ge(S["rz1"], 2 * b + h + 1)
                dve.wait_ge(S["pe_p1"], NP_ * b + NT * h + NT)

            def y_tile1(b, p, first):
                h, m = p // 4, p % 4
                src = bank[((0, 1, 2, 3), (4, 5, 0, 1))[h][m]][:, :]
                if p >= 2:
                    dve.wait_ge(S["g1_lo"], 8 * b + p - 1)
                elif not first:
                    dve.wait_ge(S["w2_done"], 4 * b)
                dve.tensor_tensor(yb[:, p % 2, :], src, rz[:, :], ALU.mult).then_inc(S["y1"], 1)
                dve.wait_ge(S["y1"], 8 * b + p + 1)
                dve.tensor_scalar(eb[:, p % 2, :], yb[:, p % 2, :], 0.0, None, ALU.min).then_inc(S["m1"], 1)

            def g_tile1(b, p):
                h, m = p // 4, p % 4
                dve.scalar_tensor_tensor(yb[:, p % 2, :], yb[:, p % 2, :], 0.0, o1f[:, m, h * HALF:(h + 1) * HALF],
                                         ALU.max, ALU.add).then_inc(S["r1"], 1)
                dve.wait_ge(S["r1"], 8 * b + p + 1)
                dve.wait_ge(S["e1"], 8 * b + p + 1)
                dve.scalar_tensor_tensor(yb[:, p % 2, :], eb[:, p % 2, :], -1.0, yb[:, p % 2, :],
                                         ALU.add, ALU.add).then_inc(S["g1"], 1)

            def h2_evac(b, t, last):
                src = bank[t % 2][:, 0:O]
                dve.wait_ge(S["h2_hi"], NT * b + t + 1)
                dve.tensor_tensor(h2l[:, t, :], src, f(h2h[:, t, :]), ALU.subtract).then_inc(S["h2_lo"], 1)
                if t == 0:
                    dve.wait_ge(S["h1_f"], NT * b + (8 if last else 12))
                else:
                    dve.wait_ge(S["h2_f"], NT * b + t)
                dve.tensor_tensor_reduce(prod[:, 0:O], src, ahr[:, 0, :], 1.0, 0.0, ALU.mult, ALU.add,
                                         g1c[:, t:t + 1]).then_inc(S["h2_fj"], 1)
                dve.wait_ge(S["h2_fj"], NT * b + t + 1)
                dve.tensor_tensor_reduce(prod[:, 0:O], src, ahr[:, 1, :], 1.0, 0.0, ALU.mult, ALU.add,
                                         g2c[:, t:t + 1]).then_inc(S["h2_f"], 1)

            def f2_parts(b):
                dve.wait_ge(S["h2_f"], NT * b + NT)
                dve.tensor_scalar(g2a[:, :], g2c[:, :], SHRINK * ALPHA, None, ALU.mult).then_inc(S["g2s_ready"], 1)
                dve.wait_ge(S["pe_f2T"], b + 1)
                dve.tensor_scalar(f2Th[:, :], bank[2][0:NT, 0:P], SHRINK, None, ALU.mult).then_inc(S["f2T_ready"], 1)

            def max_tile(b, t):
                if t == 0:
                    dve.wait_ge(S["pe_f2row"], b + 1)
                dve.wait_ge(S["ld_keep0"] if t % 2 == 0 else S["ld_keep1"], 16 * (NT // 2) * b + 16 * (t // 2) + 16)
                dve.wait_ge(S["row_max"], NT * b + t)
                dve.tensor_scalar(g2s[:, t:t + 1], g2c[:, t:t + 1], SHRINK, None, ALU.mult)\
                    .then_inc(S["g2s_ready"], 1)
                dve.tensor_tensor_reduce(junk[:, :], row2[:, :, :].rearrange("p a n -> p (a n)"), noD[:, t % 2, :],
                                         GROW, -3e38, ALU.subtract, ALU.max, mx[:, t:t + 1]).then_inc(S["row_max"], 1)

            def r_columns(b):
                R = S["rstep"]
                dve.wait_ge(S["row_max"], NT * b + NT)
                dve.tensor_scalar(emp[:, :], mx[:, :], NO_NEIGHBOUR, None, ALU.is_lt).then_inc(R, 1)
                dve.scalar_tensor_tensor(mxc[:, :], mx[:, :], NO_NEIGHBOUR, mx[:, :], ALU.is_ge, ALU.mult)\
                    .then_inc(R, 1)
                dve.wait_ge(R, 8 * b + 2)
                dve.tensor_tensor(lg[:, :], g1c[:, :], mxc[:, :], ALU.add).then_inc(R, 1)
                dve.wait_ge(R, 8 * b + 3)
                dve.scalar_tensor_tensor(mc[:, :], lg[:, :], ALPHA, lg[:, :], ALU.mult, ALU.max).then_inc(R, 1)
                dve.wait_ge(R, 8 * b + 4)
                dve.tensor_tensor(r1t[:, :], g1c[:, :], mc[:, :], ALU.subtract).then_inc(R, 1)
                dve.scalar_tensor_tensor(r2t[:, :], g1c[:, :], ALPHA, mc[:, :], ALU.mult, ALU.subtract)\
                    .then_inc(R, 1)
                dve.wait_ge(R, 8 * b + 6)
                dve.scalar_tensor_tensor(rc[:, 0:NT], r1t[:, :], SHRINK, emp[:, :], ALU.mult, ALU.add)\
                    .then_inc(R, 1)
                dve.scalar_tensor_tensor(rc[:, NT:2 * NT], r2t[:, :], SHRINK, emp[:, :], ALU.mult, ALU.add)\
                    .then_inc(R, 1)

            def r_parts(b):
                dve.wait_ge(S["pe_rT"], b + 1)
                src = bank[2][0:2 * NT, 0:P]
                dve.tensor_copy(rTh[:, :], src).then_inc(S["rT_hi"], 1)
                dve.wait_ge(S["rT_hi"], b + 1)
                dve.tensor_tensor(rTl[:, :], src, f(rTh[:, :]), ALU.subtract).then_inc(S["rT_lo"], 1)

            def t_tile(b, n, first):
                h, j = n // NT, n % NT
                dve.wait_ge(S["a2"], NP_ * b + n + 1)
                if n % NT == 0:
                    dve.wait_ge(S["rrow_ready"], 4 * b + 2 * h + 2)
                if n >= 2 or not first:
                    dve.wait_ge(S["p2_f"], NP_ * b + n - 1)
                dve.scalar_tensor_tensor(tb[:, n % 2, :], r1row[:, :], g2s[:, j:j + 1], arow[:, :],
                                         ALU.add, ALU.max).then_inc(S["t2"], 1)
                dve.wait_ge(S["t2"], NP_ * b + n + 1)
                dve.tensor_tensor(tb[:, n % 2, :], tb[:, n % 2, :], noT[:, j, h * HALF:(h + 1) * HALF],
                                  ALU.subtract).then_inc(S["t2m"], 1)

            def p2_low(b, n):
                dve.wait_ge(S["p2_hi"], NP_ * b + n + 1)
                dve.tensor_tensor(pl[:, n % RING, :], pf[:, n % 2, :], f(ph[:, n % RING, :]), ALU.subtract)\
                    .then_inc(S["p2_lo"], 1)

            def recip2(b, h):
                dve.wait_ge(S["pe_z2"], 2 * b + h + 1)
                dve.wait_ge(S["y2"], 4 * b + 2 * h)
                dve.wait_ge(S["y1"], 8 * b + 8)
                dve.reciprocal(rz[:, :], bank[6 + h]).then_inc(S["rz2"], 1)
                dve.wait_ge(S["rz2"], 2 * b + h + 1)
                dve.wait_ge(S["pe_p2"], NP_ * b + NT * h + NT)

            def y_tile2(b, p):
                h, m = p // 2, p % 2
                if p == 0:
                    dve.wait_ge(S["g1_lo"], 8 * b + 8)
                    dve.wait_ge(S["g1_hi"], 8 * b + 8)
                elif p >= 2:
                    dve.wait_ge(S["w2_done"], 4 * b + p - 1)
                dve.tensor_tensor(yb[:, p % 2, :], bank[(0, 4)[h] + m][:, :], rz[:, :], ALU.mult)\
                    .then_inc(S["y2"], 1)
                dve.wait_ge(S["y2"], 4 * b + p + 1)
                dve.tensor_scalar(eb[:, p % 2, :], yb[:, p % 2, :], 0.0, None, ALU.min).then_inc(S["m2"], 1)

            def w_tile2(b, p):
                h, m = p // 2, p % 2
                o2 = o2f[:, m, h * HALF:(h + 1) * HALF]
                dve.scalar_tensor_tensor(yb[:, p % 2, :], yb[:, p % 2, :], 0.0, o2,
                                         ALU.max, ALU.add).then_inc(S["r2"], 1)
                dve.wait_ge(S["r2"], 4 * b + p + 1)
                dve.wait_ge(S["e2"], 4 * b + p + 1)
                dve.scalar_tensor_tensor(o2, eb[:, p % 2, :], -1.0, yb[:, p % 2, :],
                                         ALU.add, ALU.add).then_inc(S["w2_done"], 1)

            def norm_chunk(b, c, first):
                h = c // 2
                dve.wait_ge(S["pe_tr"], 4 * b + c + 1)
                dve.wait_ge(S["ld_xn0"] if c % 2 == 0 else S["ld_xn1"], 32 * b + 16 * (c // 2) + 16)
                v = [vb[:, c % 2, q * F:(q + 1) * F] for q in range(2)]
                src = bank[(0, 4)[h] + c % 2]
                for q in range(2):
                    dve.scalar_tensor_tensor(v[q], src[:, q * O:(q + 1) * O], 0.0, v[q], ALU.max, ALU.add)\
                        .then_inc(S["v_ready"], 1)
                for q in range(2):
                    dve.wait_ge(S["v_ready"], 8 * b + 2 * c + q + 1)
                    if not (first and c == 0):
                        dve.wait_ge(S["mv_ready"], 8 * b + 2 * c)
                    dve.bn_stats(bst[:, q, :], v[q]).then_inc(S["st_ready"], 1)
                for q in range(2):
                    dve.wait_ge(S["const_ready"], 5)
                    dve.wait_ge(S["st_ready"], 8 * b + 2 * c + q + 1)
                    if not (first and c == 0):
                        dve.wait_ge(S["o_ready"], 8 * b + 2 * c)
                    dve.bn_aggr(bmv[:, q, :], bst[:, q, :]).then_inc(S["mv_ready"], 1)

            def norm_out(b, c):
                dve.wait_ge(S["rs_ready"], 4 * b + c + 1)
                for q in range(2):
                    v = vb[:, c % 2, q * F:(q + 1) * F]
                    dve.tensor_scalar(v, v, bmv[:, q, 0:1], rsd[:, q:q + 1], ALU.subtract, ALU.mult)\
                        .then_inc(S["o_ready"], 1)

            def body(b, first, last):
                if not last:
                    x_hi(b + 1, 0, False)
                for n in range(RING, 8):
                    p1_tile(b, n, first)
                p1_tile(b, 8, first)
                p1_tile(b, 9, first)
                recip1(b, 0)
                y_tile1(b, 0, first)
                y_tile1(b, 1, first)
                p1_low(b, 8)
                p1_low(b, 9)
                g_tile1(b, 0)
                p1_tile(b, 10, first)
                g_tile1(b, 1)
                p1_low(b, 10)
                y_tile1(b, 2, first)
                p1_tile(b, 11, first)
                y_tile1(b, 3, first)
                p1_low(b, 11)
                g_tile1(b, 2)
                p1_tile(b, 12, first)
                g_tile1(b, 3)
                p1_low(b, 12)
                for n in range(13, NP_):
                    p1_tile(b, n, first)
                    p1_low(b, n)
                recip1(b, 1)
                for p in (4, 6):
                    y_tile1(b, p, first)
                    y_tile1(b, p + 1, first)
                    g_tile1(b, p)
                    g_tile1(b, p + 1)
                    if p == 4 and not last:
                        h1_evac(b + 1, 0, False)
                if not last:
                    for t in range(1, 4):
                        h1_evac(b + 1, t, False)
                    x_hi(b + 1, 1, False)
                for t in range(NT):
                    h2_evac(b, t, last)
                f2_parts(b)
                for t in range(NT):
                    if not last and t % 2 == 1 and t < 7:
                        h1_evac(b + 1, 4 + t // 2, False)
                    max_tile(b, t)
                r_columns(b)
                if not last:
                    h1_evac(b + 1, 7, False)
                r_parts(b)
                if not last:
                    shifts(b + 1)
                t_tile(b, 0, first)
                t_tile(b, 1, first)
                p2_low(b, 0)
                for n in range(2, 8):
                    t_tile(b, n, first)
                    if n % 2 == 0:
                        p2_low(b, n)
                    if n == 3 and not last:
                        shifts_rest(b + 1)
                t_tile(b, 8, first)
                t_tile(b, 9, first)
                p2_low(b, 8)
                if not last:
                    b_parts(b + 1)
                recip2(b, 0)
                y_tile2(b, 0)
                y_tile2(b, 1)
                for n in range(10, 16):
                    t_tile(b, n, first)
                    if n % 2 == 0:
                        p2_low(b, n)
                    if n == 11:
                        w_tile2(b, 0)
                    if n == 13:
                        w_tile2(b, 1)
                recip2(b, 1)
                y_tile2(b, 2)
                y_tile2(b, 3)
                if not last:
                    p1_tile(b + 1, 0, False)
                    p1_tile(b + 1, 1, False)
                w_tile2(b, 2)
                w_tile2(b, 3)
                norm_chunk(b, 0, first)
                norm_out(b, 0)
                norm_chunk(b, 1, first)
                if not last:
                    p1_tile(b + 1, 2, False)
                norm_out(b, 1)
                norm_chunk(b, 2, first)
                if not last:
                    p1_tile(b + 1, 3, False)
                norm_out(b, 2)
                norm_chunk(b, 3, first)
                norm_out(b, 3)

            dve.memset(minus1[:, :], -1.0).then_inc(S["const_ready"], 1)
            dve.memset(ones[:, :], 1.0).then_inc(S["const_ready"], 1)
            dve.memset(powh[:, :], -0.5).then_inc(S["const_ready"], 1)
            for n, (hi, lo) in enumerate(((w1h, w1l), (wfh, wfl), (w2h, w2l), (whh, whl))):
                hi_, lo_ = (t[:, :, :].rearrange("p k n -> p (k n)") for t in (hi, lo))
                src = wst[:, 0:hi_.shape[1]]
                dve.wait_ge(S["ld_w"], 16 * n + 16)
                dve.tensor_copy(hi_, src).then_inc(S["wh_ready"], 1)
                dve.wait_ge(S["wh_ready"], n + 1)
                dve.tensor_tensor(lo_, src, f(hi_), ALU.subtract).then_inc(S["wl_ready"], 1)
            dve.wait_ge(S["ident0"], 2)
            dve.tensor_copy(identr[:, :], ident[0:16, 0:16]).then_inc(S["const_ready"], 1)
            for t in range(NT):
                dve.wait_ge(S["ld_adj0"], 16 * t + 16)
                dve.tensor_scalar(noT[:, t, :], ast[:, 0, :], 0, None, ALU.is_le).then_inc(S["noT_ready"], 1)
                dve.wait_ge(S["ld_adj1"], 16 * t + 16)
                if t >= 2:
                    dve.wait_ge(S["st_keep"], 16 * (t - 1))
                dve.tensor_scalar(noD[:, t % 2, :], ast[:, 1, :], 0, None, ALU.is_le).then_inc(S["noD_ready"], 1)
            dve.wait_ge(S["ld_a"], 32)
            x_hi(0, 0, True)
            for t in range(4):
                h1_evac(0, t, True)
            x_hi(0, 1, False)
            for t in range(4, 8):
                h1_evac(0, t, True)
            shifts(0)
            shifts_rest(0)
            b_parts(0)
            for n in range(RING):
                p1_tile(0, n, True)
            body(0, True, False)
            with dve.Fori(1, B - 1) as b:
                body(b, False, False)
            body(B - 1, False, True)

        @block.scalar
        def _(act):
            def o1_evac(b, p, first):
                h, m = p // 4, p % 4
                src = bank[(2, 4)[h] + m % 2][:, :]
                act.wait_ge(S["pe_mlp1"], 8 * b + p + 1)
                if m == 0 and not first:
                    act.wait_ge(S["g1"], 8 * b - 4 + 4 * h)
                act.activation(o1f[:, m, h * HALF:(h + 1) * HALF], src, ACT.Relu, bias=b1c[:, m:m + 1])\
                    .then_inc(S["o1_f"], 1)
                if m == 0 and not (first and h == 0):
                    act.wait_ge(S["pe_h1"], 8 * b + 4 * h)
                act.activation(o1h[:, m, :], src, ACT.Relu, bias=b1c[:, m:m + 1]).then_inc(S["o1_hi"], 1)

            def h1_hi(b, t, first):
                src = bank[6 + t % 2] if t < 4 else bank[4 + t % 2][:, :]
                act.wait_ge(S["pe_h1"], NT * b + t + 1)
                if t == 0 and not first:
                    act.wait_ge(S["pe_p1"], NP_ * b)
                act.activation(h1h[:, t, :], src, ACT.Copy).then_inc(S["h1_hi"], 1)

            def uvb(b, first):
                act.wait_ge(S["shift_ready"], 3 * b + 3)
                if not first:
                    act.wait_ge(S["p1_f"], NP_ * b)
                    act.wait_ge(S["pe_bT"], b)
                act.activation(uc[:, :], f2c[:, :], ACT.Exp, bias=nfa[:, 0:1])
                act.activation(vc[:, :], f2c[:, :], ACT.Exp, bias=nfb[:, 0:1], scale=ALPHA)
                act.activation(bc[:, :], sc[:, :], ACT.Exp, scale=ALPHA - 1.0).then_inc(S["uvb_ready"], 1)

            def brow_evac(b):
                act.wait_ge(S["pe_brow"], b + 1)
                act.activation(brow[:, 0:HALF], bank[2][:, :], ACT.Copy).then_inc(S["brow_ready"], 1)
                act.activation(brow[:, HALF:N], bank[3][:, :], ACT.Copy).then_inc(S["brow_ready"], 1)

            def p1_hi(b, n, first):
                act.wait_ge(S["p1_f"], NP_ * b + n + 1)
                if n >= RING or not first:
                    act.wait_ge(*((S["pe_p1"], NP_ * b + n - RING + 1) if n >= RING
                                  else (S["pe_p2"], NP_ * b - RING + n + 1)))
                act.activation(ph[:, n % RING, :], pf[:, n % 2, :], ACT.Copy).then_inc(S["p1_hi"], 1)

            def e_tile1(b, p):
                act.wait_ge(S["m1"], 8 * b + p + 1)
                act.activation(eb[:, p % 2, :], eb[:, p % 2, :], ACT.Exp).then_inc(S["e1a"], 1)
                act.wait_ge(S["e1a"], 8 * b + p + 1)
                act.activation(eb[:, p % 2, :], eb[:, p % 2, :], ACT.Exp, bias=minus1[:, 0:1]).then_inc(S["e1"], 1)

            def g_hi(b, p, first):
                h, m = p // 4, p % 4
                act.wait_ge(S["g1"], 8 * b + p + 1)
                if p == 0 and not first:
                    act.wait_ge(S["pe_p2"], NP_ * b)
                if p == 4:
                    act.wait_ge(S["pe_mlp2"], 4 * b + 2)
                act.activation(gview_h[:, m, :], yb[:, p % 2, :], ACT.Copy).then_inc(S["g1_hi"], 1)

            def o2_f(b, p, first):
                h, m = p // 2, p % 2
                act.wait_ge(S["pe_mlp2"], 4 * b + p + 1)
                if p == 0 and not first:
                    act.wait_ge(S["pe_tr"], 4 * b)
                act.activation(o2f[:, m, h * HALF:(h + 1) * HALF], bank[2 + m][:, :], ACT.Relu,
                               bias=b2c[:, m:m + 1]).then_inc(S["o2_f"], 1)

            def o2_hi(b, p):
                h, m = p // 2, p % 2
                act.wait_ge(S["o2_f"], 4 * b + p + 1)
                act.wait_ge(S["pe_p1"], NP_ * b + NP_)
                n = slice(h * HALF, (h + 1) * HALF)
                act.activation(o2h[:, m, n], o2f[:, m, n], ACT.Copy).then_inc(S["o2_hi"], 1)

            def h2_hi(b, t):
                act.wait_ge(S["pe_h2"], NT * b + t + 1)
                if t == 0:
                    act.wait_ge(S["pe_mlp2"], 4 * b + 4)
                act.activation(h2h[:, t, :], bank[t % 2][:, 0:O], ACT.Copy).then_inc(S["h2_hi"], 1)

            def rrow(b, h, first):
                act.wait_ge(S["pe_rrow"], 2 * b + h + 1)
                if h == 1 or not first:
                    act.wait_ge(S["t2"], NP_ * b + NT * h)
                act.activation(r1row[:, :], bank[3][:, :], ACT.Copy).then_inc(S["rrow_ready"], 1)
                act.activation(r2row[:, :], bank[2][:, :], ACT.Copy).then_inc(S["rrow_ready"], 1)

            def a_tile(b, n, first):
                h, j = n // NT, n % NT
                if n == 0:
                    act.wait_ge(S["g2s_ready"], 9 * b + 9)
                if j == 0:
                    act.wait_ge(S["rrow_ready"], 4 * b + 2 * h + 2)
                if n >= 1 or not first:
                    act.wait_ge(S["t2"], NP_ * b + n)
                act.activation(arow[:, :], r2row[:, :], ACT.Identity, bias=g2a[:, j:j + 1]).then_inc(S["a2"], 1)

            def exp_tile(b, n, first):
                act.wait_ge(S["t2m"], NP_ * b + n + 1)
                if n < 2:
                    act.wait_ge(S["acc1"], NP_ * b + NP_)
                    act.wait_ge(S["p1_lo2"], NT * b + NT)
                else:
                    act.wait_ge(S["acc2"], NP_ * b + n - 1)
                    act.wait_ge(S["p2_lo"] if n % 2 == 0 else S["p2_lo2"], NT * b + n // 2)
                act.activation(pf[:, n % 2, :], tb[:, n % 2, :], ACT.Exp, scale=GROW).then_inc(S["p2_f"], 1)
                if n < RING:
                    act.wait_ge(S["pe_h2"], NT * b + NT)
                else:
                    act.wait_ge(S["pe_p2"], NP_ * b + n - RING + 1)
                act.wait_ge(S["p2_f"], NP_ * b + n + 1)
                act.activation(ph[:, n % RING, :], pf[:, n % 2, :], ACT.Copy).then_inc(S["p2_hi"], 1)

            def e_tile2(b, p):
                act.wait_ge(S["m2"], 4 * b + p + 1)
                act.activation(eb[:, p % 2, :], eb[:, p % 2, :], ACT.Exp).then_inc(S["e2a"], 1)
                act.wait_ge(S["e2a"], 4 * b + p + 1)
                act.activation(eb[:, p % 2, :], eb[:, p % 2, :], ACT.Exp, bias=minus1[:, 0:1]).then_inc(S["e2"], 1)

            def body(b, first, last):
                for n in range(RING, 10):
                    p1_hi(b, n, first)
                e_tile1(b, 0)
                e_tile1(b, 1)
                g_hi(b, 0, first)
                p1_hi(b, 10, first)
                g_hi(b, 1, first)
                e_tile1(b, 2)
                p1_hi(b, 11, first)
                e_tile1(b, 3)
                g_hi(b, 2, first)
                p1_hi(b, 12, first)
                g_hi(b, 3, first)
                p1_hi(b, 13, first)
                o2_f(b, 0, first)
                o2_f(b, 1, first)
                for n in range(14, NP_):
                    p1_hi(b, n, first)
                for p in (4, 6):
                    e_tile1(b, p)
                    e_tile1(b, p + 1)
                    g_hi(b, p, first)
                    g_hi(b, p + 1, first)
                    if not last:
                        if p == 4:
                            for m in range(4):
                                o1_evac(b + 1, m, False)
                            h1_hi(b + 1, 0, False)
                if not last:
                    for t in range(1, 4):
                        h1_hi(b + 1, t, False)
                o2_hi(b, 0)
                o2_hi(b, 1)
                for p in (2, 3):
                    o2_f(b, p, first)
                    o2_hi(b, p)
                if not last:
                    for m in range(4, 8):
                        o1_evac(b + 1, m, False)
                for t in range(NT):
                    h2_hi(b, t)
                if not last:
                    for t in range(4, 8):
                        h1_hi(b + 1, t, False)
                rrow(b, 0, first)
                a_tile(b, 0, first)
                for n in range(NT):
                    if n < NT - 1:
                        a_tile(b, n + 1, first)
                    elif n == NT - 1:
                        rrow(b, 1, first)
                        a_tile(b, n + 1, first)
                    exp_tile(b, n, first)
                    if n == 4 and not last:
                        uvb(b + 1, False)
                a_tile(b, 9, first)
                exp_tile(b, 8, first)
                if not last:
                    a_tile(b, 10, first)
                    exp_tile(b, 9, first)
                    brow_evac(b + 1)
                else:
                    a_tile(b, 10, first)
                    exp_tile(b, 9, first)
                e_tile2(b, 0)
                e_tile2(b, 1)
                for n in range(10, NP_):
                    if n < NP_ - 1:
                        a_tile(b, n + 1, first)
                    exp_tile(b, n, first)
                e_tile2(b, 2)
                e_tile2(b, 3)
                if not last:
                    for n in range(RING):
                        p1_hi(b + 1, n, False)

            act.wait_ge(S["ld_b"], 32)
            act.wait_ge(S["const_ready"], 5)
            act.wait_ge(S["wl_ready"], 4)
            for m in range(4):
                o1_evac(0, m, True)
            for t in range(4):
                h1_hi(0, t, True)
            for m in range(4, 8):
                o1_evac(0, m, True)
            for t in range(4, 8):
                h1_hi(0, t, True)
            uvb(0, True)
            brow_evac(0)
            for n in range(RING):
                p1_hi(0, n, True)
            act.wait_ge(S["noT_ready"], NT)
            act.wait_ge(S["noD_ready"], NT)
            body(0, True, False)
            with act.Fori(1, B - 1) as b:
                body(b, False, False)
            body(B - 1, False, True)

        @block.gpsimd
        def _(pool):
            def sub(out_, a, b_, s):
                pool.tensor_tensor(out_, a, b_, ALU.subtract).then_inc(S[s], 1)

            def x_lo(b, h):
                pool.wait_ge(S["x_hi"], 2 * b + h + 1)
                sub(xl[:, :, :], xf[:, :, :], f(xh[:, :, :]), "x_lo")

            def o1_lo(b, p):
                h, m = p // 4, p % 4
                pool.wait_ge(S["o1_hi"], 8 * b + p + 1)
                sub(o1l[:, m, :], o1f[:, m, h * HALF:(h + 1) * HALF], f(o1h[:, m, :]), "o1_lo")

            def all_max(b):
                if isinstance(b, int) and b == 0:
                    pool.wait_ge(S["col_max"], 1)
                pool.partition_all_reduce(fall[:, :], fmx[:, :], P, RMAX).then_inc(S["all_max"], 1)

            def p1_low(b, n):
                pool.wait_ge(S["p1_hi"], NP_ * b + n + 1)
                sub(pl[:, n % RING, :], pf[:, n % 2, :], f(ph[:, n % RING, :]), "p1_lo")

            def acc1(b, n, first):
                h, j = n // NT, n % NT
                if j == 0:
                    return
                pool.wait_ge(S["p1_f"], NP_ * b + n + 1)
                if j == 1:
                    if h == 1:
                        pool.wait_ge(S["pe_z1"], 2 * b + 1)
                    elif not first:
                        pool.wait_ge(S["pe_z2"], 2 * b)
                    pool.tensor_tensor(acc[:, :], pf[:, 0, :], pf[:, 1, :], ALU.add).then_inc(S["acc1"], 2)
                else:
                    pool.wait_ge(S["acc1"], NP_ * b + n)
                    pool.tensor_tensor(acc[:, :], acc[:, :], pf[:, n % 2, :], ALU.add).then_inc(S["acc1"], 1)

            def g_lo(b, p):
                m = p % 4
                pool.wait_ge(S["g1_hi"], 8 * b + p + 1)
                sub(gview_l[:, m, :], yb[:, p % 2, :], f(gview_h[:, m, :]), "g1_lo")

            def o2_lo(b, p):
                h, m = p // 2, p % 2
                pool.wait_ge(S["o2_hi"], 4 * b + p + 1)
                n = slice(h * HALF, (h + 1) * HALF)
                sub(o2l[:, m, n], o2f[:, m, n], f(o2h[:, m, n]), "o2_lo")

            def acc2(b, n, last):
                h, j = n // NT, n % NT
                if j == 0:
                    return
                pool.wait_ge(S["p2_f"], NP_ * b + n + 1)
                if j == 1:
                    if h == 1:
                        pool.wait_ge(S["pe_z2"], 2 * b + 1)
                    else:
                        if not last:
                            pool.wait_ge(S["col_max"], b + 2)
                        pool.wait_ge(S["pe_z1"], 2 * b + 2)
                    pool.tensor_tensor(acc[:, :], pf[:, 0, :], pf[:, 1, :], ALU.add).then_inc(S["acc2"], 2)
                else:
                    pool.wait_ge(S["acc2"], NP_ * b + n)
                    pool.tensor_tensor(acc[:, :], acc[:, :], pf[:, n % 2, :], ALU.add).then_inc(S["acc2"], 1)

            def p2_low(b, n):
                pool.wait_ge(S["p2_hi"], NP_ * b + n + 1)
                sub(pl[:, n % RING, :], pf[:, n % 2, :], f(ph[:, n % RING, :]), "p2_lo2")

            def rstd(b, c):
                pool.wait_ge(S["mv_ready"], 8 * b + 2 * c + 2)
                pool.tensor_tensor(rst[:, :], bmv[:, :, 1], epsc[:, :], ALU.add).then_inc(S["ve_ready"], 1)
                pool.wait_ge(S["ve_ready"], 4 * b + c + 1)
                pool.tensor_tensor(rsd[:, :], rst[:, :], powh[:, 0:2], ALU.pow).then_inc(S["rs_ready"], 1)

            def body(b, first, last):
                if not last:
                    x_lo(b + 1, 0)
                for n in range(RING, 8):
                    p1_low(b, n)
                    acc1(b, n, first)
                for n in range(8, NP_):
                    acc1(b, n, first)
                    if 9 <= n < 13:
                        g_lo(b, n - 9)
                for p in range(4, 6):
                    g_lo(b, p)
                if not last:
                    for m in range(4):
                        o1_lo(b + 1, m)
                for p in range(6, 8):
                    g_lo(b, p)
                if not last:
                    x_lo(b + 1, 1)
                for p in range(4):
                    o2_lo(b, p)
                if not last:
                    for m in range(4, 8):
                        o1_lo(b + 1, m)
                for n in range(NP_):
                    acc2(b, n, last)
                    if n == 1 and not last:
                        all_max(b + 1)
                    if n % 2 == 1:
                        p2_low(b, n)
                if not last:
                    p1_low(b + 1, 0)
                    acc1(b + 1, 0, False)
                    p1_low(b + 1, 1)
                    acc1(b + 1, 1, False)
                rstd(b, 0)
                rstd(b, 1)
                if not last:
                    p1_low(b + 1, 2)
                    acc1(b + 1, 2, False)
                rstd(b, 2)
                if not last:
                    p1_low(b + 1, 3)
                    acc1(b + 1, 3, False)
                rstd(b, 3)

            pool.memset(ident[:, :], 0.0).then_inc(S["ident0"], 1)
            pool.wait_ge(S["ident0"], 1)
            pool.affine_select(out=ident[:, :], in_=ident[:, :], compare_op=ALU.not_equal, fill=1.0, base=0,
                               pattern=[[-1, P]], channel_multiplier=1).then_inc(S["ident0"], 1)
            pool.wait_ge(S["ident0"], 2)
            pool.memset(epsc[:, :], EPS).then_inc(S["const_ready"], 1)
            pool.wait_ge(S["const_ready"], 5)
            x_lo(0, 0)
            for m in range(4):
                o1_lo(0, m)
            x_lo(0, 1)
            for m in range(4, 8):
                o1_lo(0, m)
            all_max(0)
            for n in range(RING):
                p1_low(0, n)
                acc1(0, n, True)
            body(0, True, False)
            with pool.Fori(1, B - 1) as b:
                body(b, False, False)
            body(B - 1, False, True)


def kernel(x, adj, L0_gnn_mlp1_w, L0_gnn_mlp1_b, L0_gnn_mlp2_w, L0_gnn_mlp2_b, L0_gnn_W_fc, L0_gnn_a_fc,
           L0_gnn_W_hand, L0_gnn_a_hand):
    import numpy as np
    import concourse.bacc as bacc
    from concourse.bass_utils import run_bass_kernel_spmd as run

    x = np.asarray(x)
    B, N, F = x.shape
    H, O = L0_gnn_mlp1_w.shape[1], L0_gnn_mlp2_w.shape[1]
    half, p = N // 2, 128
    c = np.ascontiguousarray
    arrays = {
        "xT": c(x.reshape(B, 2, half, F // p, p).transpose(0, 1, 4, 3, 2).reshape(B * 2 * p, -1)),
        "x": c(x.reshape(B, 4, 2, p, F).transpose(0, 1, 3, 2, 4).reshape(B * 4 * p, -1)),
        "adj": c(np.asarray(adj)),
        "adjT": c(np.asarray(adj).T),
        "w1": c(np.asarray(L0_gnn_mlp1_w)),
        "b1": c(np.asarray(L0_gnn_mlp1_b).reshape(H // p, p).T),
        "w2": c(np.asarray(L0_gnn_mlp2_w)),
        "b2": c(np.asarray(L0_gnn_mlp2_b).reshape(O // p, p).T),
        "wf": c(np.asarray(L0_gnn_W_fc)),
        "af": c(np.asarray(L0_gnn_a_fc).reshape(-1)),
        "wh": c(np.asarray(L0_gnn_W_hand)),
        "ah": c(np.asarray(L0_gnn_a_hand).reshape(-1)),
    }
    nc = bacc.Bacc("TRN2", target_bir_lowering=False, num_devices=1)
    aps = {n: nc.dram_tensor(f"in_{n}", a.shape, mybir.dt.from_np(a.dtype), kind="ExternalInput").ap()
           for n, a in arrays.items()}
    keep = nc.dram_tensor("no_edge", (N, N), U8).ap()
    out = nc.dram_tensor("out", (B * 4 * p, 2 * F), F32, kind="ExternalOutput").ap()
    gnn_layer_kernel(nc, aps["xT"], aps["x"], aps["adj"], aps["adjT"], aps["w1"], aps["b1"], aps["w2"], aps["b2"],
                     aps["wf"], aps["af"], aps["wh"], aps["ah"], keep, out)
    r = run(nc, [{f"in_{n}": a for n, a in arrays.items()}], core_ids=[0])
    return r.results[0]["out"].reshape(B, 4, p, 2, F).transpose(0, 1, 3, 2, 4).reshape(B, N, F)
```

```python
from contextlib import ExitStack

import concourse.bass as bass
from concourse import mybir

ALU = mybir.AluOpType
ACT = mybir.ActivationFunctionType
AX_X = mybir.AxisListType.X
F32 = mybir.dt.float32
F32R = mybir.dt.float32r
BF16 = mybir.dt.bfloat16
U8 = mybir.dt.uint8
I32 = mybir.dt.int32
RMAX = bass.bass_isa.ReduceOp.max

P = 128
HALF = 512
ALPHA = 0.2
EPS = 1e-5
SHRINK = 2.0 ** -60
GROW = 2.0 ** 60
NO_NEIGHBOUR = -1e17


def gnn_layer_kernel(nc, xT, x, adj, adjT, w1, b1, w2, b2, wf, af, wh, ah, keep_dram, out):
    B = xT.shape[0] // (2 * P)
    H = w1.shape[1]
    F = w1.shape[0]
    O = w2.shape[1]
    N = adj.shape[0]
    NT = N // P
    KF, KH, KO = F // P, H // P, O // P
    TH = NT // 2
    NP_ = 2 * NT
    RING = 4
    WPARTS = 7

    with ExitStack() as ctx:
        def sb(name, shape, dt):
            return ctx.enter_context(nc.sbuf_tensor(name, shape, dt))

        def sem(name):
            return ctx.enter_context(nc.semaphore(name))

        w1h = sb("w1h", [P, KF, H], F32R)
        w1l = sb("w1l", [P, KF, H], F32R)
        wfh = sb("wfh", [P, KH, H + 2], F32R)
        wfl = sb("wfl", [P, KH, H + 2], F32R)
        w2h = sb("w2h", [P, KH, O], F32R)
        w2l = sb("w2l", [P, KH, O], F32R)
        whh = sb("whh", [P, KO, O + 2], F32R)
        whl = sb("whl", [P, KO, O + 2], F32R)
        b1c = sb("b1c", [P, KH], F32)
        b2c = sb("b2c", [P, KO], F32)
        wa = sb("wa", [P, KH, 2], F32)
        noT = sb("noT", [P, NT, N], U8)
        noD = sb("noD", [P, 2, N], U8)
        ident = sb("ident", [P, P], F32)
        identr = sb("identr", [16, 16], F32R)
        ones = sb("ones", [P, 1], F32)
        minus1 = sb("minus1", [P, 1], F32)
        powh = sb("powh", [P, 2], F32)
        epsc = sb("epsc", [P, 2], F32)
        xf = sb("xf", [P, KF, HALF], F32)
        xh = sb("xh", [P, KF, HALF], F32R)
        xl = sb("xl", [P, KF, HALF], F32R)
        o1f = sb("o1f", [P, KH, N], F32)
        o1h = sb("o1h", [P, KH, HALF], F32R)
        o1l = sb("o1l", [P, KH, HALF], F32R)
        gh = sb("gh", [P, KH * HALF], F32R)
        gl = sb("gl", [P, KH * HALF], F32R)
        h1h = sb("h1h", [P, NT, H], F32R)
        h1l = sb("h1l", [P, NT, H], F32R)
        ph = sb("ph", [P, RING, HALF], F32R)
        pl = sb("pl", [P, RING, HALF], F32R)
        o2f = sb("o2f", [P, KO, N], F32)
        pf = sb("pf", [P, 2, HALF], F32)
        acc = sb("acc", [P, 2, HALF], F32)
        rz = sb("rz", [P, HALF], F32)
        arow = sb("arow", [P, 2, HALF], F32)
        tb = sb("tb", [P, 2, HALF], F32)
        yb = sb("yb", [P, 2, HALF], F32)
        eb = sb("eb", [P, 2, HALF], F32)
        vb = sb("vb", [P, 2, 2 * F], F32)
        brow = sb("brow", [P, N], F32)
        r1row = sb("r1row", [P, HALF], F32)
        r2row = sb("r2row", [P, HALF], F32)
        junk = sb("junk", [P, N], BF16)
        fc = sb("fc", [P, 2, NT], F32)
        f1c, f2c = fc[:, 0, :], fc[:, 1, :]
        fmx = sb("fmx", [P, 1], F32)
        fall = sb("fall", [P, 1], F32)
        nfa = sb("nfa", [P, 1], F32)
        nfb = sb("nfb", [P, 1], F32)
        sc = sb("sc", [P, NT], F32)
        uc = sb("uc", [P, NT], F32)
        vc = sb("vc", [P, NT], F32)
        bc = sb("bc", [P, NT], F32)
        gc = sb("gc", [P, 2, NT], F32)
        g1c, g2c = gc[:, 0, :], gc[:, 1, :]
        g2s = sb("g2s", [P, NT], F32)
        g2a = sb("g2a", [P, NT], F32)
        mx = sb("mx", [P, NT], F32)
        mxc = sb("mxc", [P, NT], F32)
        emp = sb("emp", [P, NT], F32)
        lg = sb("lg", [P, NT], F32)
        mc = sb("mc", [P, NT], F32)
        r1t = sb("r1t", [P, NT], F32)
        r2t = sb("r2t", [P, NT], F32)
        rc = sb("rc", [P, 2 * NT], F32)
        rTh = sb("rTh", [2 * NT, P], F32R)
        rTl = sb("rTl", [2 * NT, P], F32R)
        f2Th, bTh, bTl = rTh[0:NT, :], rTh[0:NT, :], rTl[0:NT, :]
        rzc = sb("rzc", [P, 4], F32)
        zTh = sb("zTh", [4, P], F32R)
        zTl = sb("zTl", [4, P], F32R)
        bst = sb("bst", [P, 2, 6], F32)
        bmv = sb("bmv", [P, 2, 2], F32)
        rst = sb("rst", [P, 2], F32)
        rsd = sb("rsd", [P, 2], F32)

        gview_h = gh[:, :].rearrange("p (k n) -> p k n", k=KH)
        gview_l = gl[:, :].rearrange("p (k n) -> p k n", k=KH)
        h2h = gh[:, :].rearrange("p (t n) -> p t n", t=NT)
        h2l = gl[:, :].rearrange("p (t n) -> p t n", t=NT)
        o2h = ph[:, :, :].rearrange("p (k a) n -> p k (a n)", k=KO)
        o2l = pl[:, :, :].rearrange("p (k a) n -> p k (a n)", k=KO)
        afr = pf[:, :, :]
        ahr = tb[:, 0, :].rearrange("p (a n) -> p a n", a=2)
        wst = o1f[:, :, :].rearrange("p k n -> p (k n)")
        ast = o2f[:, :, :].bitcast(I32)

        pair = [ctx.enter_context(nc.psum_tensor(f"pair{i}", [P, 2, HALF], F32)) for i in range(4)]
        bank = [pair[i // 2][:, i % 2, :] for i in range(8)]
        row2 = pair[3]

        names = """
        ld_w ld_b ld_a ld_adj0 ld_adj1 st_keep ld_x0 ld_keep0 ld_keep1 ld_xn0 ld_xn1 st_out0 st_out1
        const_ready ident0 wh_ready wl_ready wa_ready noT_ready noD_ready
        x_hi x_lo o1_f o1_hi o1_lo h1_hi h1_lo h1_f
        col_max all_max shift_ready uvb_ready bT_hi bT_lo brow_ready
        p1_f p1_hi p1_lo p1_lo2 acc1 y1 m1 e1a e1 r1 g1 g1_hi g1_lo
        z_rec z_hi z_lo rz_ready pe_zc pe_zT pe_zr
        o2_f o2_hi o2_lo h2_hi h2_lo h2_f g2s_ready f2T_ready row_max
        rstep rT_hi rT_lo rrow_ready
        a2 t2 t2m p2_f p2_hi p2_lo p2_lo2 acc2 y2 m2 e2a e2 r2 w2_done
        v_ready st_ready mv_ready ve_ready rs_ready o_ready
        pe_mlp1 pe_h1 pe_p1 pe_mlp2 pe_h2 pe_f2T pe_f2row pe_rT pe_rrow pe_p2 pe_bT pe_brow pe_tr
        """.split()
        S = {n: sem(n) for n in names}

        block = ctx.enter_context(nc.Block())

        def f(ap):
            return ap.bitcast(F32)

        @block.sync
        def _(sp):
            rows = [(w1, KF * H), (wf, KH * H), (w2, KH * O), (wh, KO * O)]
            sp.dma_start(b1c[:, :], b1).then_inc(S["ld_b"], 16)
            sp.dma_start(b2c[:, :], b2).then_inc(S["ld_b"], 16)
            sp.dma_start(pf[:, :, :].rearrange("p a n -> p (a n)"), af.partition_broadcast(P)).then_inc(S["ld_a"], 16)
            sp.dma_start(tb[:, 0, :], ah.partition_broadcast(P)).then_inc(S["ld_a"], 16)
            for n, (w, size) in enumerate(rows):
                k = size // (HALF * (w.shape[1] // HALF if w.shape[1] >= HALF else 1))
                if n >= 1:
                    sp.wait_ge(S["wl_ready"], (1, 4, 5)[n - 1])
                kk = w.shape[0] // P
                sp.dma_start(wst[:, 0:size].rearrange("p (k n) -> p k n", k=kk),
                             w.rearrange("(k p) n -> p k n", p=P)).then_inc(S["ld_w"], 16)
            for t in range(2 * NT):
                if t >= 2:
                    sp.wait_ge(S["noT_ready"] if t % 2 == 0 else S["noD_ready"], t // 2)
                src = adjT if t % 2 == 0 else adj
                sp.dma_start(ast[:, t % 2, :], src[(t // 2) * P:(t // 2 + 1) * P, :])\
                    .then_inc(S["ld_adj0"] if t % 2 == 0 else S["ld_adj1"], 16)
                if t % 2 == 1:
                    sp.wait_ge(S["noD_ready"], t // 2 + 1)
                    sp.dma_start(keep_dram[(t // 2) * P:(t // 2 + 1) * P, :], noD[:, (t // 2) % 2, :])\
                        .then_inc(S["st_keep"], 16)
            sp.wait_ge(S["st_keep"], 16 * NT)

            def load_x(b, h, first):
                if not first:
                    sp.wait_ge(S["x_lo"], 2 * b + h)
                    sp.wait_ge(S["x_hi"], 2 * b + h)
                sp.dma_start(xf[:, :, :].rearrange("p k n -> p (k n)"), xT[bass.ts(2 * b + h, P), :])\
                    .then_inc(S["ld_x0"], 16)

            def load_masks(b, first):
                for t in range(NT):
                    if not (first and t < 2):
                        sp.wait_ge(S["row_max"], NT * b + t - 1)
                    sp.dma_start(noD[:, t % 2, :], keep_dram[t * P:(t + 1) * P, :])\
                        .then_inc(S["ld_keep0"] if t % 2 == 0 else S["ld_keep1"], 16)

            def load_chunk(b, c, first):
                if not (first and c < 2):
                    sp.wait_ge(S["st_out0"] if c % 2 == 0 else S["st_out1"], 32 * b + 16 * (c // 2))
                sp.dma_start(vb[:, c % 2, :], x[bass.ts(4 * b + c, P), :])\
                    .then_inc(S["ld_xn0"] if c % 2 == 0 else S["ld_xn1"], 16)

            def store_chunk(b, c):
                sp.wait_ge(S["o_ready"], 8 * b + 2 * c + 2)
                sp.dma_start(out[bass.ts(4 * b + c, P), :], vb[:, c % 2, :])\
                    .then_inc(S["st_out0"] if c % 2 == 0 else S["st_out1"], 16)

            def chunks(b, first):
                load_chunk(b, 0, first)
                load_chunk(b, 1, first)
                store_chunk(b, 0)
                load_chunk(b, 2, False)
                store_chunk(b, 1)
                load_chunk(b, 3, False)
                store_chunk(b, 2)
                store_chunk(b, 3)

            def body(b, first, last):
                if not first:
                    chunks(b - 1, isinstance(b, int) and b == 1)
                if not last:
                    load_x(b + 1, 1, False)
                load_masks(b, first)
                if not last and not (isinstance(b, int) and b == B - 2):
                    load_x(b + 2, 0, False)

            load_x(0, 0, True)
            load_x(0, 1, False)
            load_x(1, 0, False)
            body(0, True, False)
            body(1, False, False)
            with sp.Fori(2, B - 2) as b:
                body(b, False, False)
            body(B - 2, False, False)
            body(B - 1, False, True)
            chunks(B - 1, False)
            sp.wait_ge(S["st_out0"], 32 * B)
            sp.wait_ge(S["st_out1"], 32 * B)

        @block.tensor
        def _(pe):
            def mm3(dst, ah_, al_, bh_, bl_, start, stop):
                nc.tensor.matmul(dst, ah_, bh_, start=start, stop=False)
                nc.tensor.matmul(dst, ah_, bl_, start=False, stop=False)
                return nc.tensor.matmul(dst, al_, bh_, start=False, stop=stop)

            def mlp1(b, h, first, ms=range(4)):
                if 0 in ms:
                    pe.wait_ge(S["x_hi"], 2 * b + h + 1)
                    pe.wait_ge(S["x_lo"], 2 * b + h + 1)
                for m in ms:
                    if m >= 2:
                        pe.wait_ge(S["o1_hi"], 8 * b + 4 * h + m - 1)
                    elif h == 1:
                        pe.wait_ge(S["h1_f"], 8 * b + 4)
                    elif not first:
                        pe.wait_ge(S["o2_f"], 4 * b - 2)
                    dst = bank[(2, 4)[h] + m % 2]
                    w = slice(m * P, (m + 1) * P)
                    for k in range(KF):
                        mm = mm3(dst, w1h[:, k, w], w1l[:, k, w], xh[:, k, :], xl[:, k, :], k == 0, k == KF - 1)
                    mm.then_inc(S["pe_mlp1"], 1)

            def proj1(b, h, first, qs):
                for q in qs:
                    if q == 0:
                        pe.wait_ge(S["o1_hi"], 8 * b + 4 * h + 4)
                        pe.wait_ge(S["o1_lo"], 8 * b + 4 * h + 4)
                    if q >= 2:
                        pe.wait_ge(S["h1_f"], 8 * b + 4 * h + q - 1)
                    elif q == 0 and not first:
                        if h == 0:
                            pe.wait_ge(S["y1"], 8 * b - 1)
                        else:
                            pe.wait_ge(S["h2_f"], 8 * b)
                    pr = pair[((3, 2), (1, 2))[h][q % 2]]
                    n = slice(q * P, (q + 1) * P)
                    for part, dst in ((slice(0, O + 2), pr[:, 0, 0:O + 2]), (slice(O + 2, H + 2), pr[:, 1, 0:O])):
                        for k in range(KH):
                            mm = mm3(dst, o1h[:, k, n], o1l[:, k, n], wfh[:, k, part], wfl[:, k, part],
                                     k == 0, k == KH - 1)
                    mm.then_inc(S["pe_h1"], 1)

            def agg1(b, h, j, ms, first):
                n = NT * h + j
                if 0 in ms:
                    pe.wait_ge(S["p1_hi"], NP_ * b + n + 1)
                    pe.wait_ge(S["p1_lo"] if h == 0 else S["p1_lo2"], NT * b + j + 1)
                for m in ms:
                    if j == 0 and h == 0 and m == 0:
                        pe.wait_ge(S["brow_ready"], 2 * b + 2)
                        pe.wait_ge(S["h1_f"], 8 * b + 8)
                        if not first:
                            pe.wait_ge(S["rz_ready"], 4 * b - 1)
                    if j == 0 and h == 1 and m == 0 and not first:
                        pe.wait_ge(S["v_ready"], 8 * b)
                    if j == 0 and h == 1 and m == 3:
                        pe.wait_ge(S["y1"], 8 * b + 1)
                    w = slice(m * P, (m + 1) * P)
                    mm = mm3(bank[((0, 1, 2, 3), (4, 5, 6, 0))[h][m]], h1h[:, j, w], h1l[:, j, w],
                             ph[:, n % RING, :], pl[:, n % RING, :], j == 0, j == NT - 1)
                if 3 in ms:
                    mm.then_inc(S["pe_p1"], 1)

            def z_columns(b, i):
                n = NP_ * b + NT * (i % 2) + NT
                pe.wait_ge(S["acc1"] if i < 2 else S["acc2"], n)
                if i == 1:
                    pe.wait_ge(S["rz_ready"], 4 * b + 1)
                if i == 0 and not (isinstance(b, int) and b == 0):
                    pe.wait_ge(S["rz_ready"], 4 * b)
                if i == 3:
                    pe.wait_ge(S["y2"], 4 * b + 2)
                for q in range(4):
                    mm = nc.tensor.matmul(bank[(7, 7, 2, 7)[i]][:, q:q + 1], acc[:, i % 2, q * P:(q + 1) * P],
                                          ones[:, :], start=True, stop=True)
                mm.then_inc(S["pe_zc"], 1)

            def z_transpose(b, i):
                pe.wait_ge(S["z_rec"], 4 * b + i + 1)
                nc.tensor.transpose(bank[(7, 7, 2, 7)[i]][0:4, 0:P], rzc[:, :], ident[:, :]).then_inc(S["pe_zT"], 1)

            def z_spread(b, i):
                pe.wait_ge(S["z_hi"], 4 * b + i + 1)
                pe.wait_ge(S["z_lo"], 4 * b + i + 1)
                spread(bank[(7, 7, 2, 7)[i]], zTh[:, :], zTl[:, :], 0, 4).then_inc(S["pe_zr"], 1)

            def mlp2(b, h, last):
                pe.wait_ge(S["g1_hi"], 8 * b + 4 * h + 4)
                pe.wait_ge(S["g1_lo"], 8 * b + 4 * h + 4)
                if h == 0:
                    pe.wait_ge(S["y1"], 8 * b + 4)
                elif last:
                    pe.wait_ge(S["o2_f"], 4 * b + 2)
                else:
                    pe.wait_ge(S["o1_hi"], 8 * b + 12)
                for m in range(KO):
                    w = slice(m * P, (m + 1) * P)
                    for k in range(KH):
                        mm = mm3(bank[2 + m], w2h[:, k, w], w2l[:, k, w], gview_h[:, k, :], gview_l[:, k, :],
                                 k == 0, k == KH - 1)
                    mm.then_inc(S["pe_mlp2"], 1)

            def proj2(b):
                pe.wait_ge(S["o2_hi"], 4 * b + 4)
                pe.wait_ge(S["o2_lo"], 4 * b + 4)
                pe.wait_ge(S["y1"], 8 * b + 8)
                for t in range(NT):
                    if t >= 4:
                        pe.wait_ge(S["h2_f"], NT * b + t - 3)
                    n = slice(t * P, (t + 1) * P)
                    for k in range(KO):
                        mm = mm3(bank[t % 4][:, 0:O + 2], o2h[:, k, n], o2l[:, k, n], whh[:, k, :], whl[:, k, :],
                                 k == 0, k == KO - 1)
                    mm.then_inc(S["pe_h2"], 1)

            def spread(dst, rows_hi, rows_lo, c0, K):
                for q in range(4):
                    one = identr[0:K, c0 + q:c0 + q + 1].to_broadcast([K, P])
                    d = dst[:, q * P:(q + 1) * P]
                    mm = nc.tensor.matmul(d, one, rows_hi, start=True, stop=rows_lo is None)
                    if rows_lo is not None:
                        mm = nc.tensor.matmul(d, one, rows_lo, start=False, stop=True)
                return mm

            def f2_transpose(b):
                pe.wait_ge(S["h2_f"], NT * b + NT)
                nc.tensor.transpose(bank[0][0:NT, 0:P], g2c, ident[:, :]).then_inc(S["pe_f2T"], 1)

            def f2_spread(b, last):
                pe.wait_ge(S["f2T_ready"], b + 1)
                if last:
                    pe.wait_ge(S["y1"], 8 * b + 8)
                else:
                    pe.wait_ge(S["h1_f"], 8 * b + 11)
                spread(bank[6], f2Th[:, :], None, 0, NT)
                spread(bank[7], f2Th[:, :], None, 4, NT).then_inc(S["pe_f2row"], 1)

            def r_transpose(b):
                pe.wait_ge(S["rstep"], 8 * b + 8)
                nc.tensor.transpose(bank[0][0:2 * NT, 0:P], rc[:, :], ident[:, :]).then_inc(S["pe_rT"], 1)

            def r_spread(b, h):
                if h == 0:
                    pe.wait_ge(S["rT_hi"], b + 1)
                    pe.wait_ge(S["rT_lo"], b + 1)
                else:
                    pe.wait_ge(S["rrow_ready"], 4 * b + 2)
                spread(bank[0], rTh[:, :], rTl[:, :], 4 * h, 2 * NT)
                spread(bank[1], rTh[:, :], rTl[:, :], NT + 4 * h, 2 * NT).then_inc(S["pe_rrow"], 1)

            def agg2(b, h, js, last):
                for j in js:
                    n = NT * h + j
                    pe.wait_ge(S["p2_hi"], NP_ * b + n + 1)
                    pe.wait_ge(S["p2_lo"] if n % 2 == 0 else S["p2_lo2"], NT * b + n // 2 + 1)
                    if j == 0 and h == 0:
                        pe.wait_ge(S["row_max"], NT * b + NT)
                    if j == 0 and h == 1:
                        if last:
                            pe.wait_ge(S["y1"], 8 * b + 8)
                        else:
                            pe.wait_ge(S["h1_f"], 8 * b + 16)
                    for m in range(KO):
                        w = slice(m * P, (m + 1) * P)
                        mm = mm3(bank[(6, 4)[h] + m], h2h[:, j, w], h2l[:, j, w],
                                 ph[:, n % RING, :], pl[:, n % RING, :], j == 0, j == NT - 1)
                    mm.then_inc(S["pe_p2"], 1)

            def b_transpose(b, first):
                pe.wait_ge(S["uvb_ready"], b + 1)
                pe.wait_ge(S["h1_f"], NT * b + NT)
                nc.tensor.transpose(bank[3][0:NT, 0:P], bc[:, :], ident[:, :]).then_inc(S["pe_bT"], 1)

            def b_spread(b, first):
                if not first:
                    pe.wait_ge(S["rrow_ready"], 4 * b)
                pe.wait_ge(S["bT_hi"], b + 1)
                pe.wait_ge(S["bT_lo"], b + 1)
                spread(bank[0], bTh[:, :], bTl[:, :], 0, NT)
                spread(bank[1], bTh[:, :], bTl[:, :], 4, NT).then_inc(S["pe_brow"], 1)

            def transpose_chunk(b, c):
                pe.wait_ge(S["w2_done"], 4 * b + 2 * (c // 2) + 2)
                if c == 1:
                    pe.wait_ge(S["v_ready"], 8 * b + 2)
                for q in range(2):
                    t = 2 * c + q
                    for m in range(KO):
                        mm = nc.tensor.transpose(bank[(6, 6, 4, 5)[c]][:, q * O + m * P:q * O + (m + 1) * P],
                                                 o2f[:, m, t * P:(t + 1) * P], ident[:, :])
                mm.then_inc(S["pe_tr"], 1)

            def body(b, first, last):
                for j in range(NT):
                    agg1(b, 0, j, (0, 1), first)
                    if not first and j == 1:
                        z_transpose(b - 1, 3)
                    agg1(b, 0, j, (2, 3), first)
                    if not first:
                        if j == 0:
                            z_columns(b - 1, 3)
                        if j == 1:
                            z_spread(b - 1, 3)
                        if j >= 2 and j < 6:
                            transpose_chunk(b - 1, j - 2)
                agg1(b, 1, 0, (0, 1, 2), first)
                z_columns(b, 0)
                agg1(b, 1, 1, (0,), first)
                z_transpose(b, 0)
                agg1(b, 1, 1, (1, 2), first)
                z_spread(b, 0)
                agg1(b, 1, 2, (0, 1, 2), first)
                for j in range(3):
                    agg1(b, 1, j, (3,), first)
                for j in range(3, 6):
                    agg1(b, 1, j, (0, 1, 2, 3), first)
                mlp2(b, 0, last)
                for j in range(6, NT):
                    agg1(b, 1, j, (0, 1, 2, 3), first)
                if not last:
                    mlp1(b + 1, 0, False, (0, 1))
                z_columns(b, 1)
                if not last:
                    mlp1(b + 1, 0, False, (2,))
                z_transpose(b, 1)
                if not last:
                    mlp1(b + 1, 0, False, (3,))
                z_spread(b, 1)
                if not last:
                    proj1(b + 1, 0, False, range(0, 4))
                mlp2(b, 1, last)
                if not last:
                    mlp1(b + 1, 1, False)
                proj2(b)
                f2_transpose(b)
                if not last:
                    proj1(b + 1, 1, False, (0,))
                f2_spread(b, last)
                if not last:
                    proj1(b + 1, 1, False, (1, 2))
                r_transpose(b)
                if not last:
                    proj1(b + 1, 1, False, (3,))
                r_spread(b, 0)
                agg2(b, 0, range(2), last)
                r_spread(b, 1)
                agg2(b, 0, range(2, NT), last)
                agg2(b, 1, (0,), last)
                z_columns(b, 2)
                agg2(b, 1, (1,), last)
                z_transpose(b, 2)
                if not last:
                    b_transpose(b + 1, False)
                agg2(b, 1, (2,), last)
                z_spread(b, 2)
                if not last:
                    b_spread(b + 1, False)
                agg2(b, 1, (3,), last)
                agg2(b, 1, range(4, NT), last)

            pe.wait_ge(S["const_ready"], 5)
            pe.wait_ge(S["wl_ready"], WPARTS)
            pe.wait_ge(S["wh_ready"], WPARTS)
            mlp1(0, 0, True)
            proj1(0, 0, True, range(4))
            mlp1(0, 1, True)
            proj1(0, 1, True, range(4))
            b_transpose(0, True)
            b_spread(0, True)
            body(0, True, False)
            with pe.Fori(1, B - 1) as b:
                body(b, False, False)
            body(B - 1, False, True)
            z_columns(B - 1, 3)
            z_transpose(B - 1, 3)
            z_spread(B - 1, 3)
            for c in range(4):
                transpose_chunk(B - 1, c)

        @block.vector
        def _(dve):
            def x_hi(b, h, first):
                dve.wait_ge(S["ld_x0"], 32 * b + 16 * h + 16)
                if not first:
                    dve.wait_ge(S["pe_mlp1"], 8 * b + 4 * h)
                dve.tensor_copy(xh[:, :, :], xf[:, :, :]).then_inc(S["x_hi"], 1)

            def h1_evac(b, t):
                pr = pair[((3, 2), (1, 2))[t // 4][t % 2]]
                dve.wait_ge(S["h1_hi"], NT * b + t + 1)
                dve.tensor_tensor(h1l[:, t, :].rearrange("p (a n) -> p a n", a=2), pr[:, :, 0:O],
                                  f(h1h[:, t, :]).rearrange("p (a n) -> p a n", a=2), ALU.subtract)\
                    .then_inc(S["h1_lo"], 1)
                dve.tensor_copy(fc[:, :, t], pr[:, 0, O:O + 2]).then_inc(S["h1_f"], 1)

            def shifts(b):
                dve.wait_ge(S["h1_f"], NT * b + NT)
                dve.reduce_max(fmx[:, :], f2c, AX_X).then_inc(S["col_max"], 1)

            def shifts_rest(b):
                dve.wait_ge(S["all_max"], b + 1)
                dve.tensor_scalar(nfa[:, :], fall[:, :], -1.0, None, ALU.mult).then_inc(S["shift_ready"], 1)
                dve.tensor_scalar(nfb[:, :], fall[:, :], -ALPHA, None, ALU.mult).then_inc(S["shift_ready"], 1)
                dve.tensor_scalar(sc[:, :], f1c, fall[:, 0:1], 0.0, ALU.add, ALU.max)\
                    .then_inc(S["shift_ready"], 1)

            def b_parts(b):
                dve.wait_ge(S["pe_bT"], b + 1)
                dve.tensor_copy(bTh[:, :], bank[3][0:NT, 0:P]).then_inc(S["bT_hi"], 1)
                dve.wait_ge(S["bT_hi"], b + 1)
                dve.tensor_tensor(bTl[:, :], bank[3][0:NT, 0:P], f(bTh[:, :]), ALU.subtract)\
                    .then_inc(S["bT_lo"], 1)

            def p1_tile(b, n, first):
                j = n % NT
                if n == 0:
                    dve.wait_ge(S["brow_ready"], 2 * b + 2)
                    if not first:
                        dve.wait_ge(S["acc2"], NP_ * b)
                        dve.wait_ge(S["p2_lo2"], NT * b)
                        dve.wait_ge(S["p2_lo"], NT * b)
                        dve.wait_ge(S["p2_hi"], NP_ * b)
                if n >= 2:
                    dve.wait_ge(S["p1_hi"], NP_ * b + n - 1)
                    dve.wait_ge(S["acc1"], NP_ * b + n - 1)
                    if n - 2 < NT:
                        dve.wait_ge(S["p1_lo"], NT * b + n - 1)
                h = n // NT
                dve.tensor_scalar(pf[:, n % 2, :], brow[:, h * HALF:(h + 1) * HALF], vc[:, j:j + 1], uc[:, j:j + 1],
                                  ALU.mult, ALU.max).then_inc(S["p1_f"], 1)

            def p1_low(b, n):
                dve.wait_ge(S["p1_hi"], NP_ * b + n + 1)
                dve.wait_ge(S["pe_p1"], NP_ * b + n - RING + 1)
                dve.tensor_tensor(pl[:, n % RING, :], pf[:, n % 2, :], f(ph[:, n % RING, :]), ALU.subtract)\
                    .then_inc(S["p1_lo2"], 1)

            def z_recip(b, i, first):
                dve.wait_ge(S["pe_zc"], 4 * b + i + 1)
                if not (first and i == 0):
                    dve.wait_ge(S["pe_zT"], 4 * b + i)
                dve.reciprocal(rzc[:, :], bank[(7, 7, 2, 7)[i]][:, 0:4]).then_inc(S["z_rec"], 1)

            def z_parts(b, i, first):
                src = bank[(7, 7, 2, 7)[i]][0:4, 0:P]
                dve.wait_ge(S["pe_zT"], 4 * b + i + 1)
                if not (first and i == 0):
                    dve.wait_ge(S["pe_zr"], 4 * b + i)
                dve.tensor_copy(zTh[:, :], src).then_inc(S["z_hi"], 1)
                dve.wait_ge(S["z_hi"], 4 * b + i + 1)
                dve.tensor_tensor(zTl[:, :], src, f(zTh[:, :]), ALU.subtract).then_inc(S["z_lo"], 1)

            def y_tile1(b, p, first):
                h, m = p // 4, p % 4
                if m == 0:
                    dve.wait_ge(S["rz_ready"], 4 * b + h + 1)
                    dve.wait_ge(S["pe_p1"], NP_ * b + NT * h + NT)
                if p >= 2:
                    dve.wait_ge(S["g1_lo"], 8 * b + p - 1)
                elif not first:
                    dve.wait_ge(S["w2_done"], 4 * b)
                dve.tensor_tensor(yb[:, p % 2, :], bank[((0, 1, 2, 3), (4, 5, 6, 0))[h][m]], rz[:, :], ALU.mult)\
                    .then_inc(S["y1"], 1)
                dve.wait_ge(S["y1"], 8 * b + p + 1)
                dve.tensor_scalar(eb[:, p % 2, :], yb[:, p % 2, :], 0.0, None, ALU.min).then_inc(S["m1"], 1)

            def g_tile1(b, p):
                h, m = p // 4, p % 4
                dve.scalar_tensor_tensor(yb[:, p % 2, :], yb[:, p % 2, :], 0.0, o1f[:, m, h * HALF:(h + 1) * HALF],
                                         ALU.max, ALU.add).then_inc(S["r1"], 1)
                dve.wait_ge(S["r1"], 8 * b + p + 1)
                dve.wait_ge(S["e1"], 8 * b + p + 1)
                dve.scalar_tensor_tensor(yb[:, p % 2, :], eb[:, p % 2, :], -1.0, yb[:, p % 2, :],
                                         ALU.add, ALU.add).then_inc(S["g1"], 1)

            def h2_evac(b, t):
                src = bank[t % 4]
                dve.wait_ge(S["h2_hi"], NT * b + t + 1)
                dve.tensor_tensor(h2l[:, t, :], src[:, 0:O], f(h2h[:, t, :]), ALU.subtract).then_inc(S["h2_lo"], 1)
                dve.tensor_copy(gc[:, :, t], src[:, O:O + 2]).then_inc(S["h2_f"], 1)

            def f2_parts(b):
                dve.wait_ge(S["h2_f"], NT * b + NT)
                dve.tensor_scalar(g2a[:, :], g2c, SHRINK * ALPHA, None, ALU.mult).then_inc(S["g2s_ready"], 1)
                dve.wait_ge(S["pe_f2T"], b + 1)
                dve.tensor_scalar(f2Th[:, :], bank[0][0:NT, 0:P], SHRINK, None, ALU.mult).then_inc(S["f2T_ready"], 1)

            def max_tile(b, t):
                if t == 0:
                    dve.wait_ge(S["pe_f2row"], b + 1)
                dve.wait_ge(S["ld_keep0"] if t % 2 == 0 else S["ld_keep1"], 16 * (NT // 2) * b + 16 * (t // 2) + 16)
                dve.wait_ge(S["row_max"], NT * b + t)
                dve.tensor_scalar(g2s[:, t:t + 1], g2c[:, t:t + 1], SHRINK, None, ALU.mult)\
                    .then_inc(S["g2s_ready"], 1)
                dve.tensor_tensor_reduce(junk[:, :], row2[:, :, :].rearrange("p a n -> p (a n)"), noD[:, t % 2, :],
                                         GROW, -3e38, ALU.subtract, ALU.max, mx[:, t:t + 1]).then_inc(S["row_max"], 1)

            def r_columns(b):
                R = S["rstep"]
                dve.wait_ge(S["row_max"], NT * b + NT)
                dve.tensor_scalar(emp[:, :], mx[:, :], NO_NEIGHBOUR, None, ALU.is_lt).then_inc(R, 1)
                dve.scalar_tensor_tensor(mxc[:, :], mx[:, :], NO_NEIGHBOUR, mx[:, :], ALU.is_ge, ALU.mult)\
                    .then_inc(R, 1)
                dve.wait_ge(R, 8 * b + 2)
                dve.tensor_tensor(lg[:, :], g1c, mxc[:, :], ALU.add).then_inc(R, 1)
                dve.wait_ge(R, 8 * b + 3)
                dve.scalar_tensor_tensor(mc[:, :], lg[:, :], ALPHA, lg[:, :], ALU.mult, ALU.max).then_inc(R, 1)
                dve.wait_ge(R, 8 * b + 4)
                dve.tensor_tensor(r1t[:, :], g1c, mc[:, :], ALU.subtract).then_inc(R, 1)
                dve.scalar_tensor_tensor(r2t[:, :], g1c, ALPHA, mc[:, :], ALU.mult, ALU.subtract)\
                    .then_inc(R, 1)
                dve.wait_ge(R, 8 * b + 6)
                dve.scalar_tensor_tensor(rc[:, 0:NT], r1t[:, :], SHRINK, emp[:, :], ALU.mult, ALU.add)\
                    .then_inc(R, 1)
                dve.scalar_tensor_tensor(rc[:, NT:2 * NT], r2t[:, :], SHRINK, emp[:, :], ALU.mult, ALU.add)\
                    .then_inc(R, 1)

            def r_parts(b):
                dve.wait_ge(S["pe_rT"], b + 1)
                src = bank[0][0:2 * NT, 0:P]
                dve.tensor_copy(rTh[:, :], src).then_inc(S["rT_hi"], 1)
                dve.wait_ge(S["rT_hi"], b + 1)
                dve.tensor_tensor(rTl[:, :], src, f(rTh[:, :]), ALU.subtract).then_inc(S["rT_lo"], 1)

            def t_tile(b, n, first):
                h, j = n // NT, n % NT
                dve.wait_ge(S["a2"], NP_ * b + n + 1)
                if n >= 2 or not first:
                    dve.wait_ge(S["p2_f"], NP_ * b + n - 1)
                dve.scalar_tensor_tensor(tb[:, n % 2, :], r1row[:, :], g2s[:, j:j + 1], arow[:, n % 2, :],
                                         ALU.add, ALU.max).then_inc(S["t2"], 1)

            def mask_tile(b, n):
                h, j = n // NT, n % NT
                dve.wait_ge(S["t2"], NP_ * b + n + 1)
                dve.tensor_tensor(tb[:, n % 2, :], tb[:, n % 2, :], noT[:, j, h * HALF:(h + 1) * HALF],
                                  ALU.subtract).then_inc(S["t2m"], 1)

            def p2_low(b, n):
                dve.wait_ge(S["p2_hi"], NP_ * b + n + 1)
                dve.tensor_tensor(pl[:, n % RING, :], pf[:, n % 2, :], f(ph[:, n % RING, :]), ALU.subtract)\
                    .then_inc(S["p2_lo"], 1)

            def p2_step(b, n, first):
                t_tile(b, n, first)
                if n >= 2 and n % 2 == 0:
                    p2_low(b, n - 2)
                mask_tile(b, n)

            def y_tile2(b, p):
                h, m = p // 2, p % 2
                if m == 0:
                    dve.wait_ge(S["rz_ready"], 4 * b + 3 + h)
                    dve.wait_ge(S["pe_p2"], NP_ * b + NT * h + NT)
                if p == 0:
                    dve.wait_ge(S["g1_lo"], 8 * b + 8)
                    dve.wait_ge(S["g1_hi"], 8 * b + 8)
                elif p >= 2:
                    dve.wait_ge(S["w2_done"], 4 * b + p - 1)
                dve.tensor_tensor(yb[:, p % 2, :], bank[(6, 4)[h] + m], rz[:, :], ALU.mult)\
                    .then_inc(S["y2"], 1)
                dve.wait_ge(S["y2"], 4 * b + p + 1)
                dve.tensor_scalar(eb[:, p % 2, :], yb[:, p % 2, :], 0.0, None, ALU.min).then_inc(S["m2"], 1)

            def w_tile2(b, p):
                h, m = p // 2, p % 2
                o2 = o2f[:, m, h * HALF:(h + 1) * HALF]
                dve.scalar_tensor_tensor(yb[:, p % 2, :], yb[:, p % 2, :], 0.0, o2,
                                         ALU.max, ALU.add).then_inc(S["r2"], 1)
                dve.wait_ge(S["r2"], 4 * b + p + 1)
                dve.wait_ge(S["e2"], 4 * b + p + 1)
                dve.scalar_tensor_tensor(o2, eb[:, p % 2, :], -1.0, yb[:, p % 2, :],
                                         ALU.add, ALU.add).then_inc(S["w2_done"], 1)

            def norm_in(b, c, first):
                dve.wait_ge(S["pe_tr"], 4 * b + c + 1)
                dve.wait_ge(S["ld_xn0"] if c % 2 == 0 else S["ld_xn1"], 32 * b + 16 * (c // 2) + 16)
                v = [vb[:, c % 2, q * F:(q + 1) * F] for q in range(2)]
                src = bank[(6, 6, 4, 5)[c]]
                for q in range(2):
                    dve.scalar_tensor_tensor(v[q], src[:, q * O:(q + 1) * O], 0.0, v[q], ALU.max, ALU.add)\
                        .then_inc(S["v_ready"], 1)
                for q in range(2):
                    dve.wait_ge(S["v_ready"], 8 * b + 2 * c + q + 1)
                    if not (first and c == 0):
                        dve.wait_ge(S["mv_ready"], 8 * b + 2 * c)
                    dve.bn_stats(bst[:, q, :], v[q]).then_inc(S["st_ready"], 1)
                for q in range(2):
                    dve.wait_ge(S["const_ready"], 5)
                    dve.wait_ge(S["st_ready"], 8 * b + 2 * c + q + 1)
                    if not (first and c == 0):
                        dve.wait_ge(S["o_ready"], 8 * b + 2 * c)
                    dve.bn_aggr(bmv[:, q, :], bst[:, q, :]).then_inc(S["mv_ready"], 1)

            def norm_out(b, c):
                dve.wait_ge(S["rs_ready"], 4 * b + c + 1)
                for q in range(2):
                    v = vb[:, c % 2, q * F:(q + 1) * F]
                    dve.tensor_scalar(v, v, bmv[:, q, 0:1], rsd[:, q:q + 1], ALU.subtract, ALU.mult)\
                        .then_inc(S["o_ready"], 1)

            def body(b, first, last):
                if first:
                    for n in range(RING, 10):
                        p1_tile(b, n, first)
                else:
                    second = isinstance(b, int) and b == 1
                    z_recip(b - 1, 3, False)
                    p1_tile(b, 4, first)
                    z_parts(b - 1, 3, False)
                    y_tile2(b - 1, 2)
                    y_tile2(b - 1, 3)
                    p1_tile(b, 5, first)
                    w_tile2(b - 1, 2)
                    w_tile2(b - 1, 3)
                    norm_in(b - 1, 0, second)
                    p1_tile(b, 6, first)
                    norm_out(b - 1, 0)
                    norm_in(b - 1, 1, second)
                    p1_tile(b, 7, first)
                    norm_out(b - 1, 1)
                    norm_in(b - 1, 2, second)
                    p1_tile(b, 8, first)
                    norm_out(b - 1, 2)
                    norm_in(b - 1, 3, second)
                    p1_tile(b, 9, first)
                    norm_out(b - 1, 3)
                p1_low(b, 8)
                p1_low(b, 9)
                z_recip(b, 0, first)
                p1_tile(b, 10, first)
                z_parts(b, 0, first)
                p1_low(b, 10)
                y_tile1(b, 0, first)
                y_tile1(b, 1, first)
                p1_tile(b, 11, first)
                g_tile1(b, 0)
                p1_low(b, 11)
                g_tile1(b, 1)
                p1_tile(b, 12, first)
                y_tile1(b, 2, first)
                p1_low(b, 12)
                y_tile1(b, 3, first)
                p1_tile(b, 13, first)
                g_tile1(b, 2)
                p1_low(b, 13)
                g_tile1(b, 3)
                for n in range(14, NP_):
                    p1_tile(b, n, first)
                    p1_low(b, n)
                if not last:
                    x_hi(b + 1, 0, False)
                z_recip(b, 1, first)
                z_parts(b, 1, first)
                y_tile1(b, 4, first)
                y_tile1(b, 5, first)
                g_tile1(b, 4)
                g_tile1(b, 5)
                y_tile1(b, 6, first)
                y_tile1(b, 7, first)
                if not last:
                    h1_evac(b + 1, 0)
                g_tile1(b, 6)
                if not last:
                    h1_evac(b + 1, 1)
                g_tile1(b, 7)
                if not last:
                    h1_evac(b + 1, 2)
                    x_hi(b + 1, 1, False)
                    h1_evac(b + 1, 3)
                for t in range(NT):
                    h2_evac(b, t)
                f2_parts(b)
                if not last:
                    h1_evac(b + 1, 4)
                for t in range(NT):
                    if not last and t in (2, 5):
                        h1_evac(b + 1, 5 if t == 2 else 6)
                    max_tile(b, t)
                r_columns(b)
                if not last:
                    h1_evac(b + 1, 7)
                r_parts(b)
                if not last:
                    shifts(b + 1)
                for n in range(10):
                    p2_step(b, n, first)
                    if n == 4 and not last:
                        shifts_rest(b + 1)
                p2_step(b, 10, first)
                z_recip(b, 2, first)
                p2_step(b, 11, first)
                z_parts(b, 2, first)
                if not last:
                    b_parts(b + 1)
                p2_step(b, 12, first)
                y_tile2(b, 0)
                p2_step(b, 13, first)
                y_tile2(b, 1)
                p2_step(b, 14, first)
                w_tile2(b, 0)
                p2_step(b, 15, first)
                w_tile2(b, 1)
                p2_low(b, 14)
                if not last:
                    for n in range(RING):
                        p1_tile(b + 1, n, False)

            dve.memset(minus1[:, :], -1.0).then_inc(S["const_ready"], 1)
            dve.memset(ones[:, :], 1.0).then_inc(S["const_ready"], 1)
            dve.memset(powh[:, :], -0.5).then_inc(S["const_ready"], 1)
            dve.wait_ge(S["ld_a"], 32)
            halves = {1: [(slice(0, O), slice(0, O)), (slice(O + 2, H + 2), slice(O, H))],
                      3: [(slice(0, O), slice(0, O))]}
            made = 0
            parts = 0
            for n, (hi, lo, K, W) in enumerate(((w1h, w1l, KF, H), (wfh, wfl, KH, H), (w2h, w2l, KH, O),
                                                (whh, whl, KO, O))):
                src = wst[:, 0:K * W].rearrange("p (k n) -> p k n", k=K)
                dve.wait_ge(S["ld_w"], 16 * n + 16)
                if n in (1, 3):
                    row = (afr, ahr)[n // 2]
                    for k in range(K):
                        for a in range(2):
                            if made >= 1:
                                dve.wait_ge(S["wa_ready"], made)
                            dve.tensor_tensor_reduce(junk[:, 0:W], src[:, k, :], row[:, a, :], 1.0, 0.0, ALU.mult,
                                                     ALU.add, wa[:, k, a:a + 1]).then_inc(S["wa_ready"], 1)
                            made += 1
                    dve.wait_ge(S["wa_ready"], made)
                    parts += 1
                    dve.tensor_copy(hi[:, :, O:O + 2], wa[:, 0:K, :]).then_inc(S["wh_ready"], 1)
                    dve.wait_ge(S["wh_ready"], parts)
                    dve.tensor_tensor(lo[:, :, O:O + 2], wa[:, 0:K, :], f(hi[:, :, O:O + 2]), ALU.subtract)\
                        .then_inc(S["wl_ready"], 1)
                    dve.wait_ge(S["wl_ready"], parts)
                for to, of in halves.get(n, [(slice(0, W), slice(0, W))]):
                    parts += 1
                    dve.tensor_copy(hi[:, :, to], src[:, :, of]).then_inc(S["wh_ready"], 1)
                    dve.wait_ge(S["wh_ready"], parts)
                    dve.tensor_tensor(lo[:, :, to], src[:, :, of], f(hi[:, :, to]), ALU.subtract)\
                        .then_inc(S["wl_ready"], 1)
            dve.wait_ge(S["ident0"], 2)
            dve.tensor_copy(identr[:, :], ident[0:16, 0:16]).then_inc(S["const_ready"], 1)
            for t in range(NT):
                dve.wait_ge(S["ld_adj0"], 16 * t + 16)
                dve.tensor_scalar(noT[:, t, :], ast[:, 0, :], 0, None, ALU.is_le).then_inc(S["noT_ready"], 1)
                dve.wait_ge(S["ld_adj1"], 16 * t + 16)
                if t >= 2:
                    dve.wait_ge(S["st_keep"], 16 * (t - 1))
                dve.tensor_scalar(noD[:, t % 2, :], ast[:, 1, :], 0, None, ALU.is_le).then_inc(S["noD_ready"], 1)
            x_hi(0, 0, True)
            for t in range(4):
                h1_evac(0, t)
            x_hi(0, 1, False)
            for t in range(4, 8):
                h1_evac(0, t)
            shifts(0)
            shifts_rest(0)
            b_parts(0)
            for n in range(RING):
                p1_tile(0, n, True)
            body(0, True, False)
            body(1, False, False)
            with dve.Fori(2, B - 1) as b:
                body(b, False, False)
            body(B - 1, False, True)
            z_recip(B - 1, 3, False)
            z_parts(B - 1, 3, False)
            y_tile2(B - 1, 2)
            y_tile2(B - 1, 3)
            w_tile2(B - 1, 2)
            w_tile2(B - 1, 3)
            for c in range(4):
                norm_in(B - 1, c, False)
                norm_out(B - 1, c)

        @block.scalar
        def _(act):
            def o1_evac(b, p, first):
                h, m = p // 4, p % 4
                src = bank[(2, 4)[h] + m % 2]
                act.wait_ge(S["pe_mlp1"], 8 * b + p + 1)
                if m == 0 and not first:
                    act.wait_ge(S["g1"], 8 * b - 4 + 4 * h)
                act.activation(o1f[:, m, h * HALF:(h + 1) * HALF], src, ACT.Relu, bias=b1c[:, m:m + 1])\
                    .then_inc(S["o1_f"], 1)
                if m == 0 and not (first and h == 0):
                    act.wait_ge(S["pe_h1"], 8 * b + 4 * h)
                act.activation(o1h[:, m, :], src, ACT.Relu, bias=b1c[:, m:m + 1]).then_inc(S["o1_hi"], 1)

            def h1_hi(b, t, first):
                pr = pair[((3, 2), (1, 2))[t // 4][t % 2]]
                act.wait_ge(S["pe_h1"], NT * b + t + 1)
                if t == 0 and not first:
                    act.wait_ge(S["pe_p1"], NP_ * b)
                act.activation(h1h[:, t, :].rearrange("p (a n) -> p a n", a=2), pr[:, :, 0:O], ACT.Copy)\
                    .then_inc(S["h1_hi"], 1)

            def uvb(b, first):
                act.wait_ge(S["shift_ready"], 3 * b + 3)
                if not first:
                    act.wait_ge(S["p1_f"], NP_ * b)
                    act.wait_ge(S["pe_bT"], b)
                act.activation(uc[:, :], f2c, ACT.Exp, bias=nfa[:, 0:1])
                act.activation(vc[:, :], f2c, ACT.Exp, bias=nfb[:, 0:1], scale=ALPHA)
                act.activation(bc[:, :], sc[:, :], ACT.Exp, scale=ALPHA - 1.0).then_inc(S["uvb_ready"], 1)

            def brow_evac(b):
                act.wait_ge(S["pe_brow"], b + 1)
                act.activation(brow[:, 0:HALF], bank[0], ACT.Copy).then_inc(S["brow_ready"], 1)
                act.activation(brow[:, HALF:N], bank[1], ACT.Copy).then_inc(S["brow_ready"], 1)

            def p1_hi(b, n, first):
                act.wait_ge(S["p1_f"], NP_ * b + n + 1)
                if n >= RING:
                    act.wait_ge(S["pe_p1"], NP_ * b + n - RING + 1)
                elif not first:
                    act.wait_ge(S["pe_p2"], NP_ * b - RING + n + 1)
                act.activation(ph[:, n % RING, :], pf[:, n % 2, :], ACT.Copy).then_inc(S["p1_hi"], 1)

            def rz_evac(b, i, first):
                act.wait_ge(S["pe_zr"], 4 * b + i + 1)
                if i == 0 and not first:
                    act.wait_ge(S["y2"], 4 * b)
                elif i == 1:
                    act.wait_ge(S["y1"], 8 * b + 4)
                elif i == 2:
                    act.wait_ge(S["y1"], 8 * b + 8)
                elif i == 3:
                    act.wait_ge(S["y2"], 4 * b + 2)
                act.activation(rz[:, :], bank[(7, 7, 2, 7)[i]], ACT.Copy).then_inc(S["rz_ready"], 1)

            def e_tile1(b, p):
                act.wait_ge(S["m1"], 8 * b + p + 1)
                act.activation(eb[:, p % 2, :], eb[:, p % 2, :], ACT.Exp).then_inc(S["e1a"], 1)
                act.wait_ge(S["e1a"], 8 * b + p + 1)
                act.activation(eb[:, p % 2, :], eb[:, p % 2, :], ACT.Exp, bias=minus1[:, 0:1]).then_inc(S["e1"], 1)

            def g_hi(b, p, first):
                h, m = p // 4, p % 4
                act.wait_ge(S["g1"], 8 * b + p + 1)
                if p == 0 and not first:
                    act.wait_ge(S["pe_p2"], NP_ * b)
                if p == 4:
                    act.wait_ge(S["pe_mlp2"], 4 * b + 2)
                act.activation(gview_h[:, m, :], yb[:, p % 2, :], ACT.Copy).then_inc(S["g1_hi"], 1)

            def o2_f(b, p, first):
                h, m = p // 2, p % 2
                act.wait_ge(S["pe_mlp2"], 4 * b + p + 1)
                if p == 0 and not first:
                    act.wait_ge(S["pe_tr"], 4 * b)
                act.activation(o2f[:, m, h * HALF:(h + 1) * HALF], bank[2 + m], ACT.Relu,
                               bias=b2c[:, m:m + 1]).then_inc(S["o2_f"], 1)

            def o2_hi(b, p):
                h, m = p // 2, p % 2
                act.wait_ge(S["o2_f"], 4 * b + p + 1)
                act.wait_ge(S["pe_p1"], NP_ * b + NP_)
                n = slice(h * HALF, (h + 1) * HALF)
                act.activation(o2h[:, m, n], o2f[:, m, n], ACT.Copy).then_inc(S["o2_hi"], 1)

            def h2_hi(b, t):
                act.wait_ge(S["pe_h2"], NT * b + t + 1)
                if t == 0:
                    act.wait_ge(S["pe_mlp2"], 4 * b + 4)
                act.activation(h2h[:, t, :], bank[t % 4][:, 0:O], ACT.Copy).then_inc(S["h2_hi"], 1)

            def rrow(b, h, first):
                act.wait_ge(S["pe_rrow"], 2 * b + h + 1)
                if h == 1 or not first:
                    act.wait_ge(S["t2"], NP_ * b + NT * h)
                act.activation(r1row[:, :], bank[0], ACT.Copy).then_inc(S["rrow_ready"], 1)
                act.activation(r2row[:, :], bank[1], ACT.Copy).then_inc(S["rrow_ready"], 1)

            def a_tile(b, n, first):
                h, j = n // NT, n % NT
                if n == 0:
                    act.wait_ge(S["g2s_ready"], 9 * b + 9)
                if j == 0:
                    act.wait_ge(S["rrow_ready"], 4 * b + 2 * h + 2)
                if n >= 2 or not first:
                    act.wait_ge(S["t2"], NP_ * b + n - 1)
                act.activation(arow[:, n % 2, :], r2row[:, :], ACT.Identity, bias=g2a[:, j:j + 1])\
                    .then_inc(S["a2"], 1)

            def exp_tile(b, n, first):
                act.wait_ge(S["t2m"], NP_ * b + n + 1)
                if n < 2:
                    act.wait_ge(S["acc1"], NP_ * b + NP_)
                    act.wait_ge(S["p1_lo2"], NT * b + NT)
                else:
                    act.wait_ge(S["acc2"], NP_ * b + n - 1)
                    act.wait_ge(S["p2_lo"] if n % 2 == 0 else S["p2_lo2"], NT * b + n // 2)
                act.activation(pf[:, n % 2, :], tb[:, n % 2, :], ACT.Exp, scale=GROW).then_inc(S["p2_f"], 1)

            def p2_hi(b, n):
                if n < RING:
                    act.wait_ge(S["pe_h2"], NT * b + NT)
                else:
                    act.wait_ge(S["pe_p2"], NP_ * b + n - RING + 1)
                act.wait_ge(S["p2_f"], NP_ * b + n + 1)
                act.activation(ph[:, n % RING, :], pf[:, n % 2, :], ACT.Copy).then_inc(S["p2_hi"], 1)

            def p2_step(b, n, first):
                exp_tile(b, n, first)
                if n + 2 < NP_:
                    if n + 2 == NT:
                        rrow(b, 1, first)
                    a_tile(b, n + 2, first)
                p2_hi(b, n)

            def e_tile2(b, p):
                act.wait_ge(S["m2"], 4 * b + p + 1)
                act.activation(eb[:, p % 2, :], eb[:, p % 2, :], ACT.Exp).then_inc(S["e2a"], 1)
                act.wait_ge(S["e2a"], 4 * b + p + 1)
                act.activation(eb[:, p % 2, :], eb[:, p % 2, :], ACT.Exp, bias=minus1[:, 0:1]).then_inc(S["e2"], 1)

            def body(b, first, last):
                p1_hi(b, 4, first)
                if not first:
                    rz_evac(b - 1, 3, False)
                    e_tile2(b - 1, 2)
                    e_tile2(b - 1, 3)
                for n in range(5, 10):
                    p1_hi(b, n, first)
                p1_hi(b, 10, first)
                rz_evac(b, 0, first)
                e_tile1(b, 0)
                e_tile1(b, 1)
                p1_hi(b, 11, first)
                g_hi(b, 0, first)
                g_hi(b, 1, first)
                p1_hi(b, 12, first)
                e_tile1(b, 2)
                e_tile1(b, 3)
                p1_hi(b, 13, first)
                g_hi(b, 2, first)
                g_hi(b, 3, first)
                p1_hi(b, 14, first)
                o2_f(b, 0, first)
                o2_f(b, 1, first)
                p1_hi(b, 15, first)
                if not last:
                    o1_evac(b + 1, 0, False)
                    o1_evac(b + 1, 1, False)
                    o1_evac(b + 1, 2, False)
                rz_evac(b, 1, first)
                if not last:
                    o1_evac(b + 1, 3, False)
                e_tile1(b, 4)
                e_tile1(b, 5)
                g_hi(b, 4, first)
                g_hi(b, 5, first)
                if not last:
                    h1_hi(b + 1, 0, False)
                e_tile1(b, 6)
                e_tile1(b, 7)
                if not last:
                    h1_hi(b + 1, 1, False)
                g_hi(b, 6, first)
                g_hi(b, 7, first)
                if not last:
                    h1_hi(b + 1, 2, False)
                    h1_hi(b + 1, 3, False)
                o2_hi(b, 0)
                o2_hi(b, 1)
                for p in (2, 3):
                    o2_f(b, p, first)
                for p in (2, 3):
                    o2_hi(b, p)
                if not last:
                    for m in range(4, 8):
                        o1_evac(b + 1, m, False)
                for t in range(NT):
                    h2_hi(b, t)
                if not last:
                    for t in range(4, 8):
                        h1_hi(b + 1, t, False)
                rrow(b, 0, first)
                a_tile(b, 0, first)
                a_tile(b, 1, first)
                for n in range(11):
                    p2_step(b, n, first)
                    if n == 5 and not last:
                        uvb(b + 1, False)
                p2_step(b, 11, first)
                rz_evac(b, 2, first)
                p2_step(b, 12, first)
                if not last:
                    brow_evac(b + 1)
                p2_step(b, 13, first)
                e_tile2(b, 0)
                p2_step(b, 14, first)
                e_tile2(b, 1)
                p2_step(b, 15, first)
                if not last:
                    for n in range(RING):
                        p1_hi(b + 1, n, False)

            act.wait_ge(S["ld_b"], 32)
            act.wait_ge(S["const_ready"], 5)
            act.wait_ge(S["wl_ready"], WPARTS)
            for m in range(4):
                o1_evac(0, m, True)
            for t in range(4):
                h1_hi(0, t, True)
            for m in range(4, 8):
                o1_evac(0, m, True)
            for t in range(4, 8):
                h1_hi(0, t, True)
            uvb(0, True)
            brow_evac(0)
            for n in range(RING):
                p1_hi(0, n, True)
            act.wait_ge(S["noT_ready"], NT)
            act.wait_ge(S["noD_ready"], NT)
            body(0, True, False)
            with act.Fori(1, B - 1) as b:
                body(b, False, False)
            body(B - 1, False, True)
            rz_evac(B - 1, 3, False)
            e_tile2(B - 1, 2)
            e_tile2(B - 1, 3)

        @block.gpsimd
        def _(pool):
            def sub(out_, a, b_, s):
                pool.tensor_tensor(out_, a, b_, ALU.subtract).then_inc(S[s], 1)

            def x_lo(b, h):
                pool.wait_ge(S["x_hi"], 2 * b + h + 1)
                sub(xl[:, :, :], xf[:, :, :], f(xh[:, :, :]), "x_lo")

            def o1_lo(b, p):
                h, m = p // 4, p % 4
                pool.wait_ge(S["o1_hi"], 8 * b + p + 1)
                sub(o1l[:, m, :], o1f[:, m, h * HALF:(h + 1) * HALF], f(o1h[:, m, :]), "o1_lo")

            def all_max(b):
                if isinstance(b, int) and b == 0:
                    pool.wait_ge(S["col_max"], 1)
                pool.partition_all_reduce(fall[:, :], fmx[:, :], P, RMAX).then_inc(S["all_max"], 1)

            def p1_low(b, n):
                pool.wait_ge(S["p1_hi"], NP_ * b + n + 1)
                sub(pl[:, n % RING, :], pf[:, n % 2, :], f(ph[:, n % RING, :]), "p1_lo")

            def acc1(b, n, first):
                h, j = n // NT, n % NT
                if j == 0:
                    return
                pool.wait_ge(S["p1_f"], NP_ * b + n + 1)
                a = acc[:, h, :]
                if j == 1:
                    if not first:
                        pool.wait_ge(S["pe_zc"], 4 * b - 1 + h)
                    pool.tensor_tensor(a, pf[:, 0, :], pf[:, 1, :], ALU.add).then_inc(S["acc1"], 2)
                else:
                    pool.wait_ge(S["acc1"], NP_ * b + n)
                    pool.tensor_tensor(a, a, pf[:, n % 2, :], ALU.add).then_inc(S["acc1"], 1)

            def g_lo(b, p):
                m = p % 4
                pool.wait_ge(S["g1_hi"], 8 * b + p + 1)
                sub(gview_l[:, m, :], yb[:, p % 2, :], f(gview_h[:, m, :]), "g1_lo")

            def o2_lo(b, p):
                h, m = p // 2, p % 2
                pool.wait_ge(S["o2_hi"], 4 * b + p + 1)
                n = slice(h * HALF, (h + 1) * HALF)
                sub(o2l[:, m, n], o2f[:, m, n], f(o2h[:, m, n]), "o2_lo")

            def acc2(b, n, last):
                h, j = n // NT, n % NT
                if j == 0:
                    return
                pool.wait_ge(S["p2_f"], NP_ * b + n + 1)
                a = acc[:, h, :]
                if j == 1:
                    pool.wait_ge(S["pe_zc"], 4 * b + 1 + h)
                    if h == 0 and not last:
                        pool.wait_ge(S["col_max"], b + 2)
                    pool.tensor_tensor(a, pf[:, 0, :], pf[:, 1, :], ALU.add).then_inc(S["acc2"], 2)
                else:
                    pool.wait_ge(S["acc2"], NP_ * b + n)
                    pool.tensor_tensor(a, a, pf[:, n % 2, :], ALU.add).then_inc(S["acc2"], 1)

            def p2_low(b, n):
                pool.wait_ge(S["p2_hi"], NP_ * b + n + 1)
                sub(pl[:, n % RING, :], pf[:, n % 2, :], f(ph[:, n % RING, :]), "p2_lo2")

            def rstd(b, c):
                pool.wait_ge(S["mv_ready"], 8 * b + 2 * c + 2)
                pool.tensor_tensor(rst[:, :], bmv[:, :, 1], epsc[:, :], ALU.add).then_inc(S["ve_ready"], 1)
                pool.wait_ge(S["ve_ready"], 4 * b + c + 1)
                pool.tensor_tensor(rsd[:, :], rst[:, :], powh[:, 0:2], ALU.pow).then_inc(S["rs_ready"], 1)

            def body(b, first, last):
                for n in range(RING, 6):
                    p1_low(b, n)
                    acc1(b, n, first)
                for n in range(6, 10):
                    if not first:
                        rstd(b - 1, n - 6)
                    if n < 8:
                        p1_low(b, n)
                    acc1(b, n, first)
                for n in range(10, NP_):
                    acc1(b, n, first)
                    if n == 11:
                        g_lo(b, 0)
                        g_lo(b, 1)
                    if n == 13:
                        g_lo(b, 2)
                        g_lo(b, 3)
                if not last:
                    x_lo(b + 1, 0)
                    for m in range(4):
                        o1_lo(b + 1, m)
                for p in range(4, 8):
                    g_lo(b, p)
                if not last:
                    x_lo(b + 1, 1)
                for p in range(4):
                    o2_lo(b, p)
                if not last:
                    for m in range(4, 8):
                        o1_lo(b + 1, m)
                for n in range(NP_):
                    if n % 2 == 1:
                        p2_low(b, n)
                    acc2(b, n, last)
                    if n == 1 and not last:
                        all_max(b + 1)
                if not last:
                    for n in range(RING):
                        p1_low(b + 1, n)
                        acc1(b + 1, n, False)

            pool.memset(ident[:, :], 0.0).then_inc(S["ident0"], 1)
            pool.wait_ge(S["ident0"], 1)
            pool.affine_select(out=ident[:, :], in_=ident[:, :], compare_op=ALU.not_equal, fill=1.0, base=0,
                               pattern=[[-1, P]], channel_multiplier=1).then_inc(S["ident0"], 1)
            pool.memset(epsc[:, :], EPS).then_inc(S["const_ready"], 1)
            pool.wait_ge(S["const_ready"], 5)
            x_lo(0, 0)
            for m in range(4):
                o1_lo(0, m)
            x_lo(0, 1)
            for m in range(4, 8):
                o1_lo(0, m)
            all_max(0)
            for n in range(RING):
                p1_low(0, n)
                acc1(0, n, True)
            body(0, True, False)
            with pool.Fori(1, B - 1) as b:
                body(b, False, False)
            body(B - 1, False, True)
            for c in range(4):
                rstd(B - 1, c)


def kernel(x, adj, L0_gnn_mlp1_w, L0_gnn_mlp1_b, L0_gnn_mlp2_w, L0_gnn_mlp2_b, L0_gnn_W_fc, L0_gnn_a_fc,
           L0_gnn_W_hand, L0_gnn_a_hand):
    import numpy as np
    import concourse.bacc as bacc
    from concourse.bass_utils import run_bass_kernel_spmd as run

    x = np.asarray(x)
    B, N, F = x.shape
    H, O = L0_gnn_mlp1_w.shape[1], L0_gnn_mlp2_w.shape[1]
    half, p = N // 2, 128
    c = np.ascontiguousarray
    arrays = {
        "xT": c(x.reshape(B, 2, half, F // p, p).transpose(0, 1, 4, 3, 2).reshape(B * 2 * p, -1)),
        "x": c(x.reshape(B, 4, 2, p, F).transpose(0, 1, 3, 2, 4).reshape(B * 4 * p, -1)),
        "adj": c(np.asarray(adj)),
        "adjT": c(np.asarray(adj).T),
        "w1": c(np.asarray(L0_gnn_mlp1_w)),
        "b1": c(np.asarray(L0_gnn_mlp1_b).reshape(H // p, p).T),
        "w2": c(np.asarray(L0_gnn_mlp2_w)),
        "b2": c(np.asarray(L0_gnn_mlp2_b).reshape(O // p, p).T),
        "wf": c(np.asarray(L0_gnn_W_fc)),
        "af": c(np.asarray(L0_gnn_a_fc).reshape(-1)),
        "wh": c(np.asarray(L0_gnn_W_hand)),
        "ah": c(np.asarray(L0_gnn_a_hand).reshape(-1)),
    }
    nc = bacc.Bacc("TRN2", target_bir_lowering=False, num_devices=1)
    aps = {n: nc.dram_tensor(f"in_{n}", a.shape, mybir.dt.from_np(a.dtype), kind="ExternalInput").ap()
           for n, a in arrays.items()}
    keep = nc.dram_tensor("no_edge", (N, N), U8).ap()
    out = nc.dram_tensor("out", (B * 4 * p, 2 * F), F32, kind="ExternalOutput").ap()
    gnn_layer_kernel(nc, aps["xT"], aps["x"], aps["adj"], aps["adjT"], aps["w1"], aps["b1"], aps["w2"], aps["b2"],
                     aps["wf"], aps["af"], aps["wh"], aps["ah"], keep, out)
    r = run(nc, [{f"in_{n}": a for n, a in arrays.items()}], core_ids=[0])
    return r.results[0]["out"].reshape(B, 4, p, 2, F).transpose(0, 1, 3, 2, 4).reshape(B, N, F)
```

```python
from contextlib import ExitStack

import concourse.bass as bass
from concourse import mybir

ALU = mybir.AluOpType
ACT = mybir.ActivationFunctionType
AX_X = mybir.AxisListType.X
F32 = mybir.dt.float32
F32R = mybir.dt.float32r
BF16 = mybir.dt.bfloat16
U8 = mybir.dt.uint8
I32 = mybir.dt.int32
RMAX = bass.bass_isa.ReduceOp.max

P = 128
HALF = 512
ALPHA = 0.2
EPS = 1e-5
SHRINK = 2.0 ** -60
GROW = 2.0 ** 60
NO_NEIGHBOUR = -1e17


def gnn_layer_kernel(nc, xT, x, adj, adjT, w1, b1, w2, b2, wf, af, wh, ah, keep_dram, out):
    B = xT.shape[0] // (2 * P)
    H = w1.shape[1]
    F = w1.shape[0]
    O = w2.shape[1]
    N = adj.shape[0]
    NT = N // P
    KF, KH, KO = F // P, H // P, O // P
    TH = NT // 2
    NP_ = 2 * NT
    LO = 32
    RING = 4
    WORK = 6
    WPARTS = 7

    with ExitStack() as ctx:
        def sb(name, shape, dt):
            return ctx.enter_context(nc.sbuf_tensor(name, shape, dt))

        def sem(name):
            return ctx.enter_context(nc.semaphore(name))

        w1h = sb("w1h", [P, KF, H], F32R)
        w1l = sb("w1l", [P, KF, H], F32R)
        wfh = sb("wfh", [P, KH, H + 2], F32R)
        wfl = sb("wfl", [P, KH, H + 2], F32R)
        w2h = sb("w2h", [P, KH, O], F32R)
        w2l = sb("w2l", [P, KH, O], F32R)
        whh = sb("whh", [P, KO, O + 2], F32R)
        whl = sb("whl", [P, KO, O + 2], F32R)
        b1c = sb("b1c", [P, KH], F32)
        b2c = sb("b2c", [P, KO], F32)
        wa = sb("wa", [P, KH, 2], F32)
        noT = sb("noT", [P, NT, N], U8)
        noD = sb("noD", [P, 2, N], U8)
        ident = sb("ident", [P, P], F32)
        pick = sb("pick", [LO + NT, NT], F32R)
        ones = sb("ones", [P, 1], F32)
        minus1 = sb("minus1", [P, 1], F32)
        powh = sb("powh", [P, 2], F32)
        epsc = sb("epsc", [P, 2], F32)
        xf = sb("xf", [P, KF, HALF], F32)
        xh = sb("xh", [P, KF, HALF], F32R)
        xl = sb("xl", [P, KF, HALF], F32R)
        o1f = sb("o1f", [P, KH, N], F32)
        o1h = sb("o1h", [P, KH, HALF], F32R)
        o1l = sb("o1l", [P, KH, HALF], F32R)
        gh = sb("gh", [P, KH * HALF], F32R)
        gl = sb("gl", [P, KH * HALF], F32R)
        h1h = sb("h1h", [P, NT, H], F32R)
        h1l = sb("h1l", [P, NT, H], F32R)
        ph = sb("ph", [P, RING, HALF], F32R)
        pl = sb("pl", [P, RING, HALF], F32R)
        o2f = sb("o2f", [P, KO, N], F32)
        wk = sb("wk", [P, WORK, HALF], F32)
        acc = sb("acc", [P, 2, HALF], F32)
        rz = sb("rz", [P, HALF], F32)
        yb = sb("yb", [P, 2, HALF], F32)
        eb = sb("eb", [P, 2, HALF], F32)
        vb = sb("vb", [P, 3, 2 * F], F32)
        brow = sb("brow", [P, N], F32)
        r1row = sb("r1row", [P, HALF], F32)
        r2row = sb("r2row", [P, HALF], F32)
        fc = sb("fc", [P, 2, NT], F32)
        f1c, f2c = fc[:, 0, :], fc[:, 1, :]
        fmx = sb("fmx", [P, 1], F32)
        fall = sb("fall", [P, 1], F32)
        nfa = sb("nfa", [P, 1], F32)
        nfb = sb("nfb", [P, 1], F32)
        sc = sb("sc", [P, NT], F32)
        uc = sb("uc", [P, NT], F32)
        vc = sb("vc", [P, NT], F32)
        bc = sb("bc", [P, NT], F32)
        gc = sb("gc", [P, 2, NT], F32)
        g1c, g2c = gc[:, 0, :], gc[:, 1, :]
        g2s = sb("g2s", [P, NT], F32)
        g2a = sb("g2a", [P, NT], F32)
        mx = sb("mx", [P, NT], F32)
        mxc = sb("mxc", [P, NT], F32)
        emp = sb("emp", [P, NT], F32)
        lg = sb("lg", [P, NT], F32)
        mc = sb("mc", [P, NT], F32)
        r1t = sb("r1t", [P, NT], F32)
        r2t = sb("r2t", [P, NT], F32)
        rc = sb("rc", [P, 2 * NT], F32)
        rT = sb("rT", [LO + NT, P], F32R)
        rTh, rTl = rT[0:NT, :], rT[LO:LO + NT, :]
        f2Th, bTh, bTl = rTh, rTh, rTl
        rzc = sb("rzc", [P, 4], F32)
        zT = sb("zT", [LO + 4, P], F32R)
        zTh, zTl = zT[0:4, :], zT[LO:LO + 4, :]
        bst = sb("bst", [P, 2, 2, 6], F32)
        bmv = sb("bmv", [P, 2, 2, 2], F32)
        rst = sb("rst", [P, 2, 2], F32)
        rsd = sb("rsd", [P, 2, 2], F32)

        gview_h = gh[:, :].rearrange("p (k n) -> p k n", k=KH)
        gview_l = gl[:, :].rearrange("p (k n) -> p k n", k=KH)
        h2h = gh[:, :].rearrange("p (t n) -> p t n", t=NT)
        h2l = gl[:, :].rearrange("p (t n) -> p t n", t=NT)
        o2h = ph[:, :, :].rearrange("p (k a) n -> p k (a n)", k=KO)
        o2l = pl[:, :, :].rearrange("p (k a) n -> p k (a n)", k=KO)
        afr = wk[:, 0:2, :]
        ahr = wk[:, 2, :].rearrange("p (a n) -> p a n", a=2)
        junk = [brow[:, h * HALF:(h + 1) * HALF].bitcast(BF16) for h in range(2)]
        wst = o1f[:, :, :].rearrange("p k n -> p (k n)")
        ast = o2f[:, :, :].bitcast(I32)

        pair = [ctx.enter_context(nc.psum_tensor(f"pair{i}", [P, 2, HALF], F32)) for i in range(4)]
        bank = [pair[i // 2][:, i % 2, :] for i in range(8)]
        row2 = pair[0]

        def pool_lows(n):
            return n - (n + 2) // 3

        def on_pool(n):
            return n % 3 != 0

        def low2(n, b):
            if on_pool(n):
                return S["p2_lo2"], pool_lows(NP_) * b + pool_lows(n + 1)
            return S["p2_lo"], (NP_ - pool_lows(NP_)) * b + n + 1 - pool_lows(n + 1)

        h2_bank = (2, 3, 0, 1)

        def slot1(n):
            return (n + 10) % WORK

        def slot2(n):
            return n % WORK

        names = """
        ld_w ld_b ld_a ld_adj0 ld_adj1 st_keep ld_x0 ld_keep0 ld_keep1 ld_xn0 ld_xn1 ld_xn2 ld_xn3 st_out0 st_out1 st_out2 st_out3
        const_ready ident0 wh_ready wl_ready wa_ready noT_ready noD_ready
        x_hi x_lo o1_f o1_hi o1_lo o1_lo2 h1_hi h1_lo h1_f
        col_max all_max shift_ready uvb_ready bT_hi bT_lo brow_ready
        p1_f p1_hi p1_lo p1_lo2 acc1 y1 m1 e1a e1 r1 g1 g1_hi g1_lo g1_lo2
        z_rec z_hi z_lo rz_ready pe_zc pe_zT pe_zr
        o2_f o2_hi o2_lo o2_lo2 h2_hi h2_lo h2_f g2s_ready f2T_ready row_max
        rstep rT_hi rT_lo rrow_ready
        a2 t2 t2m p2_f p2_hi p2_lo p2_lo2 acc2 y2 m2 e2a e2 r2 w2_done
        v_ready st_ready mv_ready ve_ready rs_ready o_ready
        pe_mlp1 pe_h1 pe_p1 pe_mlp2 pe_h2 pe_f2T pe_f2row pe_rT pe_rrow pe_p2 pe_bT pe_brow pe_tr
        """.split()
        S = {n: sem(n) for n in names}

        block = ctx.enter_context(nc.Block())

        def f(ap):
            return ap.bitcast(F32)

        @block.sync
        def _(sp):
            rows = [(w1, KF * H), (wf, KH * H), (w2, KH * O), (wh, KO * O)]
            sp.dma_start(b1c[:, :], b1).then_inc(S["ld_b"], 16)
            sp.dma_start(b2c[:, :], b2).then_inc(S["ld_b"], 16)
            sp.dma_start(wk[:, 0:2, :].rearrange("p a n -> p (a n)"), af.partition_broadcast(P)).then_inc(S["ld_a"], 16)
            sp.dma_start(wk[:, 2, :], ah.partition_broadcast(P)).then_inc(S["ld_a"], 16)
            for n, (w, size) in enumerate(rows):
                k = size // (HALF * (w.shape[1] // HALF if w.shape[1] >= HALF else 1))
                if n >= 1:
                    sp.wait_ge(S["wl_ready"], (1, 4, 5)[n - 1])
                kk = w.shape[0] // P
                sp.dma_start(wst[:, 0:size].rearrange("p (k n) -> p k n", k=kk),
                             w.rearrange("(k p) n -> p k n", p=P)).then_inc(S["ld_w"], 16)
            for t in range(2 * NT):
                if t >= 2:
                    sp.wait_ge(S["noT_ready"] if t % 2 == 0 else S["noD_ready"], t // 2)
                src = adjT if t % 2 == 0 else adj
                sp.dma_start(ast[:, t % 2, :], src[(t // 2) * P:(t // 2 + 1) * P, :])\
                    .then_inc(S["ld_adj0"] if t % 2 == 0 else S["ld_adj1"], 16)
                if t % 2 == 1:
                    sp.wait_ge(S["noD_ready"], t // 2 + 1)
                    sp.dma_start(keep_dram[(t // 2) * P:(t // 2 + 1) * P, :], noD[:, (t // 2) % 2, :])\
                        .then_inc(S["st_keep"], 16)
            sp.wait_ge(S["st_keep"], 16 * NT)

            def load_x(b, h, first):
                if not first:
                    sp.wait_ge(S["x_lo"], 2 * b + h)
                    sp.wait_ge(S["x_hi"], 2 * b + h)
                sp.dma_start(xf[:, :, :].rearrange("p k n -> p (k n)"), xT[bass.ts(2 * b + h, P), :])\
                    .then_inc(S["ld_x0"], 16)

            def load_masks(b, first):
                for t in range(NT):
                    if not (first and t < 2):
                        sp.wait_ge(S["row_max"], NT * b + t - 1)
                    sp.dma_start(noD[:, t % 2, :], keep_dram[t * P:(t + 1) * P, :])\
                        .then_inc(S["ld_keep0"] if t % 2 == 0 else S["ld_keep1"], 16)

            def load_chunk(b, c, first):
                if c == 3:
                    sp.wait_ge(S["st_out0"], 16 * b + 16)
                elif not first:
                    sp.wait_ge(S[("st_out3", "st_out1", "st_out2")[c]], 16 * b)
                sp.dma_start(vb[:, c % 3, :], x[bass.ts(4 * b + c, P), :]).then_inc(S[f"ld_xn{c}"], 16)

            def store_chunk(b, c):
                sp.wait_ge(S["o_ready"], 8 * b + 2 * c + 2)
                sp.dma_start(out[bass.ts(4 * b + c, P), :], vb[:, c % 3, :]).then_inc(S[f"st_out{c}"], 16)

            def chunks(b, first):
                for c in range(3):
                    load_chunk(b, c, first)
                store_chunk(b, 0)
                load_chunk(b, 3, first)
                for c in range(1, 4):
                    store_chunk(b, c)

            def body(b, first, last):
                if not first:
                    chunks(b - 1, isinstance(b, int) and b == 1)
                if not last:
                    load_x(b + 1, 1, False)
                load_masks(b, first)
                if not last and not (isinstance(b, int) and b == B - 2):
                    load_x(b + 2, 0, False)

            load_x(0, 0, True)
            load_x(0, 1, False)
            load_x(1, 0, False)
            body(0, True, False)
            body(1, False, False)
            with sp.Fori(2, B - 2) as b:
                body(b, False, False)
            body(B - 2, False, False)
            body(B - 1, False, True)
            chunks(B - 1, False)
            for c in range(4):
                sp.wait_ge(S[f"st_out{c}"], 16 * B)

        @block.tensor
        def _(pe):
            def mm3(dst, ah_, al_, bh_, bl_, start, stop):
                nc.tensor.matmul(dst, ah_, bh_, start=start, stop=False)
                nc.tensor.matmul(dst, ah_, bl_, start=False, stop=False)
                return nc.tensor.matmul(dst, al_, bh_, start=False, stop=stop)

            def mlp1(b, h, first, ms=range(4)):
                if 0 in ms:
                    pe.wait_ge(S["x_hi"], 2 * b + h + 1)
                    pe.wait_ge(S["x_lo"], 2 * b + h + 1)
                for m in ms:
                    if m >= 2:
                        pe.wait_ge(S["o1_hi"], 8 * b + 4 * h + m - 1)
                    elif not first:
                        if h == 0 and m == 0:
                            pe.wait_ge(S["y1"], 8 * b - 6)
                        if h == 0 and m == 1:
                            pe.wait_ge(S["o2_f"], 4 * b - 3)
                        if h == 1 and m == 1:
                            pe.wait_ge(S["y1"], 8 * b)
                    dst = bank[((1, 2), (1, 0))[h][m % 2]]
                    w = slice(m * P, (m + 1) * P)
                    for k in range(KF):
                        mm = mm3(dst, w1h[:, k, w], w1l[:, k, w], xh[:, k, :], xl[:, k, :], k == 0, k == KF - 1)
                    mm.then_inc(S["pe_mlp1"], 1)

            def proj1(b, h, first, qs, parts=(0, 1)):
                for q in qs:
                    if parts[0] == 1:
                        pass
                    elif q == 0:
                        pe.wait_ge(S["o1_hi"], 8 * b + 4 * h + 4)
                        pe.wait_ge(S["o1_lo"], 4 * b + 2 * h + 2)
                        pe.wait_ge(S["o1_lo2"], 4 * b + 2 * h + 2)
                        if h == 0 and not first:
                            pe.wait_ge(S["y1"], 8 * b - 3)
                            pe.wait_ge(S["rz_ready"], 4 * b - 2)
                        if h == 1:
                            pe.wait_ge(S["h1_f"], 8 * b + 4)
                    elif q == 1:
                        if h == 0 and not first:
                            pe.wait_ge(S["o2_f"], 4 * b - 2)
                    else:
                        pe.wait_ge(S["h1_f"], 8 * b + 4 * h + q - 1)
                    pr = pair[((3, 1), (3, 2))[h][q % 2]]
                    n = slice(q * P, (q + 1) * P)
                    for a in parts:
                        part, dst = ((slice(0, O + 2), pr[:, 0, 0:O + 2]), (slice(O + 2, H + 2), pr[:, 1, 0:O]))[a]
                        for k in range(KH):
                            mm = mm3(dst, o1h[:, k, n], o1l[:, k, n], wfh[:, k, part], wfl[:, k, part],
                                     k == 0, k == KH - 1)
                    if 1 in parts:
                        mm.then_inc(S["pe_h1"], 1)

            def agg1(b, h, j, ms, first):
                n = NT * h + j
                if 0 in ms:
                    pe.wait_ge(S["p1_hi"], NP_ * b + n + 1)
                    pe.wait_ge(S["p1_lo"] if h == 0 else S["p1_lo2"], NT * b + j + 1)
                for m in ms:
                    if j == 0 and h == 0 and m == 0:
                        pe.wait_ge(S["brow_ready"], 2 * b + 2)
                        pe.wait_ge(S["h1_f"], 8 * b + 8)
                        if not first:
                            pe.wait_ge(S["rz_ready"], 4 * b - 1)
                    if j == 0 and h == 1 and m == 0 and not first:
                        pe.wait_ge(S["v_ready"], 8 * b)
                    if j == 0 and h == 1 and m == 3:
                        pe.wait_ge(S["y1"], 8 * b + 1)
                    w = slice(m * P, (m + 1) * P)
                    mm = mm3(bank[((0, 1, 2, 3), (6, 4, 5, 0))[h][m]], h1h[:, j, w], h1l[:, j, w],
                             ph[:, n % RING, :], pl[:, n % RING, :], j == 0, j == NT - 1)
                if 3 in ms:
                    mm.then_inc(S["pe_p1"], 1)

            def z_columns(b, i):
                n = NP_ * b + NT * (i % 2) + NT
                pe.wait_ge(S["acc1"] if i < 2 else S["acc2"], n)
                if i == 1:
                    pe.wait_ge(S["rz_ready"], 4 * b + 1)
                if i == 0 and not (isinstance(b, int) and b == 0):
                    pe.wait_ge(S["rz_ready"], 4 * b)
                if i == 2:
                    pe.wait_ge(S["rrow_ready"], 4 * b + 4)
                if i == 3:
                    pe.wait_ge(S["y2"], 4 * b + 2)
                for q in range(4):
                    mm = nc.tensor.matmul(bank[(7, 7, 2, 7)[i]][:, q:q + 1], acc[:, i % 2, q * P:(q + 1) * P],
                                          ones[:, :], start=True, stop=True)
                mm.then_inc(S["pe_zc"], 1)

            def z_transpose(b, i):
                pe.wait_ge(S["z_rec"], 4 * b + i + 1)
                nc.tensor.transpose(bank[(7, 7, 2, 7)[i]][0:4, 0:P], rzc[:, :], ident[:, :]).then_inc(S["pe_zT"], 1)

            def z_spread(b, i):
                pe.wait_ge(S["z_hi"], 4 * b + i + 1)
                pe.wait_ge(S["z_lo"], 4 * b + i + 1)
                spread(bank[(7, 7, 2, 7)[i]], zT[:, :], 0).then_inc(S["pe_zr"], 1)

            def mlp2(b, h, last):
                pe.wait_ge(S["g1_hi"], 8 * b + 4 * h + 4)
                if h == 0:
                    pe.wait_ge(S["g1_lo"], 2 * b + 2)
                pe.wait_ge(S["g1_lo2"], 6 * b + 4 * h + 2)
                if h == 0:
                    pe.wait_ge(S["y1"], 8 * b + 4)
                for m in range(KO):
                    w = slice(m * P, (m + 1) * P)
                    for k in range(KH):
                        mm = mm3(bank[(2, 4)[h] + m], w2h[:, k, w], w2l[:, k, w], gview_h[:, k, :], gview_l[:, k, :],
                                 k == 0, k == KH - 1)
                    mm.then_inc(S["pe_mlp2"], 1)

            def proj2(b, last):
                pe.wait_ge(S["o2_hi"], 4 * b + 4)
                pe.wait_ge(S["o2_lo"], 3 * b + 3)
                pe.wait_ge(S["o2_lo2"], b + 1)
                pe.wait_ge(S["y1"], 8 * b + 8)
                if not last:
                    pe.wait_ge(S["h1_f"], 8 * b + 12)
                for t in range(NT):
                    if t == 2 and not last:
                        pe.wait_ge(S["o1_hi"], 8 * b + 16)
                    if t >= 4:
                        pe.wait_ge(S["h2_f"], NT * b + t - 3)
                    n = slice(t * P, (t + 1) * P)
                    for k in range(KO):
                        mm = mm3(bank[h2_bank[t % 4]][:, 0:O + 2], o2h[:, k, n], o2l[:, k, n], whh[:, k, :], whl[:, k, :],
                                 k == 0, k == KO - 1)
                    mm.then_inc(S["pe_h2"], 1)

            def spread(dst, rows, c0):
                K = rows.shape[0]
                for q in range(4):
                    mm = nc.tensor.matmul(dst[:, q * P:(q + 1) * P], pick[0:K, c0 + q:c0 + q + 1].to_broadcast([K, P]),
                                          rows, start=True, stop=True)
                return mm

            def f2_transpose(b):
                pe.wait_ge(S["h2_f"], NT * b + NT)
                nc.tensor.transpose(bank[0][0:NT, 0:P], g2c, ident[:, :]).then_inc(S["pe_f2T"], 1)

            def f2_spread(b):
                pe.wait_ge(S["f2T_ready"], b + 1)
                spread(bank[0], f2Th[:, :], 0)
                spread(bank[1], f2Th[:, :], 4).then_inc(S["pe_f2row"], 1)

            def r_transpose(b, h):
                pe.wait_ge(S["rstep"], 16 * b + 8 * h + 8)
                if h == 1:
                    pe.wait_ge(S["rrow_ready"], 4 * b + 2)
                nc.tensor.transpose(bank[2][0:NT, 0:P], rc[:, NT * h:NT * h + NT], ident[:, :])\
                    .then_inc(S["pe_rT"], 1)

            def r_spread(b, h):
                pe.wait_ge(S["rT_hi"], 2 * b + h + 1)
                pe.wait_ge(S["rT_lo"], 2 * b + h + 1)
                spread(bank[2], rT[:, :], 0)
                spread(bank[3], rT[:, :], 4).then_inc(S["pe_rrow"], 1)

            def agg2(b, h, js, last):
                for j in js:
                    n = NT * h + j
                    pe.wait_ge(S["p2_hi"], NP_ * b + n + 1)
                    pe.wait_ge(*low2(n, b))
                    if j == 0 and not last:
                        pe.wait_ge(S["h1_f"], 8 * b + (15, 16)[h])
                    if j == 0 and last:
                        pe.wait_ge(S["y1"], 8 * b + 8)
                    for m in range(KO):
                        w = slice(m * P, (m + 1) * P)
                        mm = mm3(bank[(6, 4)[h] + m], h2h[:, j, w], h2l[:, j, w],
                                 ph[:, n % RING, :], pl[:, n % RING, :], j == 0, j == NT - 1)
                    mm.then_inc(S["pe_p2"], 1)

            def b_transpose(b, first):
                pe.wait_ge(S["uvb_ready"], b + 1)
                if not first:
                    pe.wait_ge(S["row_max"], NT * b)
                nc.tensor.transpose(bank[0][0:NT, 0:P], bc[:, :], ident[:, :]).then_inc(S["pe_bT"], 1)

            def b_spread(b):
                pe.wait_ge(S["bT_hi"], b + 1)
                pe.wait_ge(S["bT_lo"], b + 1)
                spread(bank[0], rT[:, :], 0)
                spread(bank[1], rT[:, :], 4).then_inc(S["pe_brow"], 1)

            def transpose_chunk(b, c):
                pe.wait_ge(S["w2_done"], 4 * b + 2 * (c // 2) + 2)
                if c == 1:
                    pe.wait_ge(S["v_ready"], 8 * b + 2)
                for q in range(2):
                    t = 2 * c + q
                    for m in range(KO):
                        mm = nc.tensor.transpose(bank[(6, 6, 4, 5)[c]][:, q * O + m * P:q * O + (m + 1) * P],
                                                 o2f[:, m, t * P:(t + 1) * P], ident[:, :])
                mm.then_inc(S["pe_tr"], 1)

            def body(b, first, last):
                for j in range(NT):
                    agg1(b, 0, j, (0, 1), first)
                    if not first and j == 1:
                        z_transpose(b - 1, 3)
                    if j == NT - 1:
                        z_columns(b, 0)
                    agg1(b, 0, j, (2, 3), first)
                    if not first:
                        if j == 0:
                            z_columns(b - 1, 3)
                        if j == 1:
                            z_spread(b - 1, 3)
                        if j in (0, 2, 4, 5):
                            transpose_chunk(b - 1, (0, 2, 4, 5).index(j))
                z_transpose(b, 0)
                agg1(b, 1, 0, (0, 1, 2), first)
                z_spread(b, 0)
                agg1(b, 1, 1, (0, 1, 2), first)
                agg1(b, 1, 2, (0, 1, 2), first)
                for j in range(3):
                    agg1(b, 1, j, (3,), first)
                for j in range(3, 6):
                    agg1(b, 1, j, (0, 1, 2, 3), first)
                if not last:
                    mlp1(b + 1, 0, False, (0,))
                agg1(b, 1, 6, (0, 1, 2, 3), first)
                mlp2(b, 0, last)
                if not last:
                    mlp1(b + 1, 0, False, (1,))
                z_columns(b, 1)
                if not last:
                    mlp1(b + 1, 0, False, (2,))
                z_transpose(b, 1)
                if not last:
                    mlp1(b + 1, 0, False, (3,))
                z_spread(b, 1)
                agg1(b, 1, 7, (0, 1, 2, 3), first)
                if not last:
                    proj1(b + 1, 0, False, range(4))
                    mlp1(b + 1, 1, False, (0, 1))
                mlp2(b, 1, last)
                if not last:
                    mlp1(b + 1, 1, False, (2, 3))
                proj2(b, last)
                if not last:
                    proj1(b + 1, 1, False, (0,), (0,))
                f2_transpose(b)
                if not last:
                    proj1(b + 1, 1, False, (0,), (1,))
                f2_spread(b)
                if not last:
                    proj1(b + 1, 1, False, (1, 2))
                    proj1(b + 1, 1, False, (3,), (0,))
                r_transpose(b, 0)
                r_spread(b, 0)
                if not last:
                    proj1(b + 1, 1, False, (3,), (1,))
                agg2(b, 0, (0, 1), last)
                r_transpose(b, 1)
                agg2(b, 0, (2,), last)
                r_spread(b, 1)
                agg2(b, 0, (3, 4), last)
                if not last:
                    b_transpose(b + 1, False)
                agg2(b, 0, (5, 6, 7), last)
                if not last:
                    b_spread(b + 1)
                agg2(b, 1, (0,), last)
                z_columns(b, 2)
                agg2(b, 1, (1, 2), last)
                z_transpose(b, 2)
                agg2(b, 1, (3,), last)
                z_spread(b, 2)
                agg2(b, 1, range(4, NT), last)

            pe.wait_ge(S["const_ready"], 8)
            pe.wait_ge(S["wl_ready"], WPARTS)
            pe.wait_ge(S["wh_ready"], WPARTS)
            mlp1(0, 0, True)
            proj1(0, 0, True, range(4))
            mlp1(0, 1, True)
            proj1(0, 1, True, range(4))
            b_transpose(0, True)
            b_spread(0)
            body(0, True, False)
            with pe.Fori(1, B - 1) as b:
                body(b, False, False)
            body(B - 1, False, True)
            z_columns(B - 1, 3)
            z_transpose(B - 1, 3)
            z_spread(B - 1, 3)
            for c in range(4):
                transpose_chunk(B - 1, c)

        @block.vector
        def _(dve):
            def x_parts(b, h, first):
                dve.wait_ge(S["ld_x0"], 32 * b + 16 * h + 16)
                if not first:
                    dve.wait_ge(S["pe_mlp1"], 8 * b + 4 * h)
                dve.tensor_copy(xh[:, :, :], xf[:, :, :]).then_inc(S["x_hi"], 1)
                dve.wait_ge(S["x_hi"], 2 * b + h + 1)
                dve.tensor_tensor(xl[:, :, :], xf[:, :, :], f(xh[:, :, :]), ALU.subtract).then_inc(S["x_lo"], 1)

            def h1_evac(b, t):
                pr = pair[((3, 1), (3, 2))[t // 4][t % 2]]
                dve.wait_ge(S["h1_hi"], NT * b + t + 1)
                dve.tensor_tensor(h1l[:, t, :].rearrange("p (a n) -> p a n", a=2), pr[:, :, 0:O],
                                  f(h1h[:, t, :]).rearrange("p (a n) -> p a n", a=2), ALU.subtract)\
                    .then_inc(S["h1_lo"], 1)
                dve.tensor_copy(fc[:, :, t], pr[:, 0, O:O + 2]).then_inc(S["h1_f"], 1)

            def o1_low(b, p):
                h, m = p // 4, p % 4
                dve.wait_ge(S["o1_hi"], 8 * b + p + 1)
                dve.tensor_tensor(o1l[:, m, :], o1f[:, m, h * HALF:(h + 1) * HALF], f(o1h[:, m, :]), ALU.subtract)\
                    .then_inc(S["o1_lo2"], 1)

            def shifts(b):
                dve.wait_ge(S["h1_f"], NT * b + NT)
                dve.reduce_max(fmx[:, :], f2c, AX_X).then_inc(S["col_max"], 1)

            def shifts_rest(b):
                dve.wait_ge(S["all_max"], b + 1)
                dve.tensor_scalar(nfa[:, :], fall[:, :], -1.0, None, ALU.mult).then_inc(S["shift_ready"], 1)
                dve.tensor_scalar(nfb[:, :], fall[:, :], -ALPHA, None, ALU.mult).then_inc(S["shift_ready"], 1)
                dve.tensor_scalar(sc[:, :], f1c, fall[:, 0:1], 0.0, ALU.add, ALU.max)\
                    .then_inc(S["shift_ready"], 1)

            def b_parts(b):
                dve.wait_ge(S["pe_bT"], b + 1)
                dve.tensor_copy(bTh[:, :], bank[0][0:NT, 0:P]).then_inc(S["bT_hi"], 1)
                dve.wait_ge(S["bT_hi"], b + 1)
                dve.tensor_tensor(bTl[:, :], bank[0][0:NT, 0:P], f(bTh[:, :]), ALU.subtract)\
                    .then_inc(S["bT_lo"], 1)

            def p1_tile(b, n, first):
                j = n % NT
                if n == 0:
                    dve.wait_ge(S["brow_ready"], 2 * b + 2)
                if n >= WORK:
                    dve.wait_ge(S["p1_hi"], NP_ * b + n - WORK + 1)
                    dve.wait_ge(S["acc1"], NP_ * b + n - WORK + 1)
                    if n - WORK < NT:
                        dve.wait_ge(S["p1_lo"], NT * b + n - WORK + 1)
                    else:
                        dve.wait_ge(S["p1_lo2"], NT * b + n - WORK + 1 - NT)
                elif not first:
                    m = n + 10
                    dve.wait_ge(S["p2_hi"], NP_ * b - NP_ + m + 1)
                    dve.wait_ge(S["acc2"], NP_ * b - NP_ + m + 1)
                    dve.wait_ge(*low2(m, b - 1))
                h = n // NT
                dve.tensor_scalar(wk[:, slot1(n), :], brow[:, h * HALF:(h + 1) * HALF], vc[:, j:j + 1], uc[:, j:j + 1],
                                  ALU.mult, ALU.max).then_inc(S["p1_f"], 1)

            def p1_low(b, n):
                dve.wait_ge(S["p1_hi"], NP_ * b + n + 1)
                dve.wait_ge(S["pe_p1"], NP_ * b + n - RING + 1)
                dve.tensor_tensor(pl[:, n % RING, :], wk[:, slot1(n), :], f(ph[:, n % RING, :]), ALU.subtract)\
                    .then_inc(S["p1_lo2"], 1)

            def z_recip(b, i, first):
                dve.wait_ge(S["pe_zc"], 4 * b + i + 1)
                if not (first and i == 0):
                    dve.wait_ge(S["pe_zT"], 4 * b + i)
                dve.reciprocal(rzc[:, :], bank[(7, 7, 2, 7)[i]][:, 0:4]).then_inc(S["z_rec"], 1)

            def z_parts(b, i, first):
                src = bank[(7, 7, 2, 7)[i]][0:4, 0:P]
                dve.wait_ge(S["pe_zT"], 4 * b + i + 1)
                if not (first and i == 0):
                    dve.wait_ge(S["pe_zr"], 4 * b + i)
                dve.tensor_copy(zTh[:, :], src).then_inc(S["z_hi"], 1)
                dve.wait_ge(S["z_hi"], 4 * b + i + 1)
                dve.tensor_tensor(zTl[:, :], src, f(zTh[:, :]), ALU.subtract).then_inc(S["z_lo"], 1)

            def y_tile1(b, p, first):
                h, m = p // 4, p % 4
                if m == 0:
                    dve.wait_ge(S["rz_ready"], 4 * b + h + 1)
                    dve.wait_ge(S["pe_p1"], NP_ * b + NT * h + NT)
                if p in (2, 3):
                    dve.wait_ge(S["g1_lo"], 2 * b + p - 1)
                elif p >= 4:
                    dve.wait_ge(S["g1_lo2"], 6 * b + p - 3)
                elif not first:
                    dve.wait_ge(S["w2_done"], 4 * b)
                dve.tensor_tensor(yb[:, p % 2, :], bank[((0, 1, 2, 3), (6, 4, 5, 0))[h][m]], rz[:, :], ALU.mult)\
                    .then_inc(S["y1"], 1)
                dve.wait_ge(S["y1"], 8 * b + p + 1)
                dve.tensor_scalar(eb[:, p % 2, :], yb[:, p % 2, :], 0.0, None, ALU.min).then_inc(S["m1"], 1)

            def g_tile1(b, p):
                h, m = p // 4, p % 4
                dve.scalar_tensor_tensor(yb[:, p % 2, :], yb[:, p % 2, :], 0.0, o1f[:, m, h * HALF:(h + 1) * HALF],
                                         ALU.max, ALU.add).then_inc(S["r1"], 1)
                dve.wait_ge(S["r1"], 8 * b + p + 1)
                dve.wait_ge(S["e1"], 8 * b + p + 1)
                dve.scalar_tensor_tensor(yb[:, p % 2, :], eb[:, p % 2, :], -1.0, yb[:, p % 2, :],
                                         ALU.add, ALU.add).then_inc(S["g1"], 1)

            def g_low(b, p):
                m = p % 4
                dve.wait_ge(S["g1_hi"], 8 * b + p + 1)
                dve.tensor_tensor(gview_l[:, m, :], yb[:, p % 2, :], f(gview_h[:, m, :]), ALU.subtract)\
                    .then_inc(S["g1_lo2"], 1)

            def o2_low(b, p):
                h, m = p // 2, p % 2
                n = slice(h * HALF, (h + 1) * HALF)
                dve.wait_ge(S["o2_hi"], 4 * b + p + 1)
                dve.tensor_tensor(o2l[:, m, n], o2f[:, m, n], f(o2h[:, m, n]), ALU.subtract).then_inc(S["o2_lo2"], 1)

            def h2_evac(b, t):
                src = bank[h2_bank[t % 4]]
                dve.wait_ge(S["h2_hi"], NT * b + t + 1)
                dve.tensor_tensor(h2l[:, t, :], src[:, 0:O], f(h2h[:, t, :]), ALU.subtract).then_inc(S["h2_lo"], 1)
                dve.tensor_copy(gc[:, :, t], src[:, O:O + 2]).then_inc(S["h2_f"], 1)

            def f2_parts(b):
                dve.wait_ge(S["h2_f"], NT * b + NT)
                dve.tensor_scalar(g2a[:, :], g2c, SHRINK * ALPHA, None, ALU.mult).then_inc(S["g2s_ready"], 1)
                dve.wait_ge(S["pe_f2T"], b + 1)
                dve.tensor_scalar(f2Th[:, :], bank[0][0:NT, 0:P], SHRINK, None, ALU.mult).then_inc(S["f2T_ready"], 1)

            def max_tile(b, t):
                if t == 0:
                    dve.wait_ge(S["pe_f2row"], b + 1)
                dve.wait_ge(S["ld_keep0"] if t % 2 == 0 else S["ld_keep1"], 16 * (NT // 2) * b + 16 * (t // 2) + 16)
                if t >= 1:
                    dve.wait_ge(S["row_max"], NT * b + t - 1)
                dve.tensor_scalar(g2s[:, t:t + 1], g2c[:, t:t + 1], SHRINK, None, ALU.mult)\
                    .then_inc(S["g2s_ready"], 1)
                dve.tensor_tensor_reduce(junk[t % 2], row2[:, :, :].rearrange("p a n -> p (a n)"), noD[:, t % 2, :],
                                         GROW, -3e38, ALU.subtract, ALU.max, mx[:, t:t + 1]).then_inc(S["row_max"], 1)

            def r_columns(b, h):
                R = S["rstep"]
                done = 16 * b + 8 * h
                c = slice(TH * h, TH * h + TH)
                dve.wait_ge(S["row_max"], NT * b + TH * h + TH)
                dve.tensor_scalar(emp[:, c], mx[:, c], NO_NEIGHBOUR, None, ALU.is_lt).then_inc(R, 1)
                dve.scalar_tensor_tensor(mxc[:, c], mx[:, c], NO_NEIGHBOUR, mx[:, c], ALU.is_ge, ALU.mult)\
                    .then_inc(R, 1)
                dve.wait_ge(R, done + 2)
                dve.tensor_tensor(lg[:, c], gc[:, 0, c], mxc[:, c], ALU.add).then_inc(R, 1)
                dve.wait_ge(R, done + 3)
                dve.scalar_tensor_tensor(mc[:, c], lg[:, c], ALPHA, lg[:, c], ALU.mult, ALU.max).then_inc(R, 1)
                dve.wait_ge(R, done + 4)
                dve.tensor_tensor(r1t[:, c], gc[:, 0, c], mc[:, c], ALU.subtract).then_inc(R, 1)
                dve.scalar_tensor_tensor(r2t[:, c], gc[:, 0, c], ALPHA, mc[:, c], ALU.mult, ALU.subtract)\
                    .then_inc(R, 1)
                dve.wait_ge(R, done + 6)
                dve.scalar_tensor_tensor(rc[:, NT * h:NT * h + TH], r1t[:, c], SHRINK, emp[:, c],
                                         ALU.mult, ALU.add).then_inc(R, 1)
                dve.scalar_tensor_tensor(rc[:, NT * h + TH:NT * h + NT], r2t[:, c], SHRINK, emp[:, c],
                                         ALU.mult, ALU.add).then_inc(R, 1)

            def r_parts(b, h):
                dve.wait_ge(S["pe_rT"], 2 * b + h + 1)
                if h == 1:
                    dve.wait_ge(S["pe_rrow"], 2 * b + 1)
                src = bank[2][0:NT, 0:P]
                dve.tensor_copy(rTh[:, :], src).then_inc(S["rT_hi"], 1)
                dve.wait_ge(S["rT_hi"], 2 * b + h + 1)
                dve.tensor_tensor(rTl[:, :], src, f(rTh[:, :]), ALU.subtract).then_inc(S["rT_lo"], 1)

            def t_tile(b, n):
                h, j = n // NT, n % NT
                t = wk[:, slot2(n), :]
                dve.wait_ge(S["a2"], NP_ * b + n + 1)
                if j == 0:
                    dve.wait_ge(S["rrow_ready"], 4 * b + 2 * h + 2)
                if h == 0:
                    dve.wait_ge(S["g2s_ready"], 9 * b + j + 2)
                dve.scalar_tensor_tensor(t, r1row[:, :], g2s[:, j:j + 1], t, ALU.add, ALU.max).then_inc(S["t2"], 1)

            def mask_tile(b, n):
                h, j = n // NT, n % NT
                t = wk[:, slot2(n), :]
                dve.wait_ge(S["t2"], NP_ * b + n + 1)
                dve.tensor_tensor(t, t, noT[:, j, h * HALF:(h + 1) * HALF], ALU.subtract).then_inc(S["t2m"], 1)

            def p2_low(b, n):
                if on_pool(n):
                    return
                dve.wait_ge(S["p2_hi"], NP_ * b + n + 1)
                dve.tensor_tensor(pl[:, n % RING, :], wk[:, slot2(n), :], f(ph[:, n % RING, :]), ALU.subtract)\
                    .then_inc(S["p2_lo"], 1)

            def p2_step(b, n):
                t_tile(b, n)
                if n >= 3:
                    p2_low(b, n - 2)
                mask_tile(b, n)

            def y_tile2(b, p):
                h, m = p // 2, p % 2
                if m == 0:
                    dve.wait_ge(S["rz_ready"], 4 * b + 3 + h)
                    dve.wait_ge(S["pe_p2"], NP_ * b + NT * h + NT)
                if p == 0:
                    dve.wait_ge(S["g1_lo2"], 6 * b + 6)
                    dve.wait_ge(S["g1_hi"], 8 * b + 8)
                elif p >= 2:
                    dve.wait_ge(S["w2_done"], 4 * b + p - 1)
                dve.tensor_tensor(yb[:, p % 2, :], bank[(6, 4)[h] + m], rz[:, :], ALU.mult)\
                    .then_inc(S["y2"], 1)
                dve.wait_ge(S["y2"], 4 * b + p + 1)
                dve.tensor_scalar(eb[:, p % 2, :], yb[:, p % 2, :], 0.0, None, ALU.min).then_inc(S["m2"], 1)

            def w_tile2(b, p):
                h, m = p // 2, p % 2
                o2 = o2f[:, m, h * HALF:(h + 1) * HALF]
                dve.scalar_tensor_tensor(yb[:, p % 2, :], yb[:, p % 2, :], 0.0, o2,
                                         ALU.max, ALU.add).then_inc(S["r2"], 1)
                dve.wait_ge(S["r2"], 4 * b + p + 1)
                dve.wait_ge(S["e2"], 4 * b + p + 1)
                dve.scalar_tensor_tensor(o2, eb[:, p % 2, :], -1.0, yb[:, p % 2, :],
                                         ALU.add, ALU.add).then_inc(S["w2_done"], 1)

            def norm_in(b, c, first):
                dve.wait_ge(S["pe_tr"], 4 * b + c + 1)
                dve.wait_ge(S[f"ld_xn{c}"], 16 * b + 16)
                v = [vb[:, c % 3, q * F:(q + 1) * F] for q in range(2)]
                src = bank[(6, 6, 4, 5)[c]]
                for q in range(2):
                    dve.scalar_tensor_tensor(v[q], src[:, q * O:(q + 1) * O], 0.0, v[q], ALU.max, ALU.add)\
                        .then_inc(S["v_ready"], 1)
                for q in range(2):
                    dve.wait_ge(S["v_ready"], 8 * b + 2 * c + q + 1)
                    if not (first and c == 0):
                        dve.wait_ge(S["mv_ready"], 8 * b + 2 * c)
                    dve.bn_stats(bst[:, c % 2, q, :], v[q]).then_inc(S["st_ready"], 1)
                for q in range(2):
                    dve.wait_ge(S["const_ready"], 8)
                    dve.wait_ge(S["st_ready"], 8 * b + 2 * c + q + 1)
                    dve.bn_aggr(bmv[:, c % 2, q, :], bst[:, c % 2, q, :]).then_inc(S["mv_ready"], 1)

            def norm_out(b, c):
                dve.wait_ge(S["rs_ready"], 4 * b + c + 1)
                for q in range(2):
                    v = vb[:, c % 3, q * F:(q + 1) * F]
                    dve.tensor_scalar(v, v, bmv[:, c % 2, q, 0:1], rsd[:, c % 2, q:q + 1], ALU.subtract, ALU.mult)\
                        .then_inc(S["o_ready"], 1)

            def body(b, first, last):
                if first:
                    for n in range(RING, 11):
                        p1_tile(b, n, first)
                    p1_low(b, 8)
                    p1_low(b, 9)
                else:
                    second = isinstance(b, int) and b == 1
                    z_recip(b - 1, 3, False)
                    p1_tile(b, 4, first)
                    norm_in(b - 1, 0, second)
                    z_parts(b - 1, 3, False)
                    p1_tile(b, 5, first)
                    norm_out(b - 1, 0)
                    y_tile2(b - 1, 2)
                    y_tile2(b - 1, 3)
                    norm_in(b - 1, 1, second)
                    w_tile2(b - 1, 2)
                    w_tile2(b - 1, 3)
                    p1_tile(b, 6, first)
                    norm_out(b - 1, 1)
                    norm_in(b - 1, 2, second)
                    p1_tile(b, 7, first)
                    p1_tile(b, 8, first)
                    norm_in(b - 1, 3, second)
                    norm_out(b - 1, 2)
                    p1_tile(b, 9, first)
                    p1_low(b, 8)
                    p1_tile(b, 10, first)
                    z_recip(b, 0, first)
                    p1_low(b, 9)
                    z_parts(b, 0, first)
                    norm_out(b - 1, 3)
                if first:
                    z_recip(b, 0, first)
                    z_parts(b, 0, first)
                p1_tile(b, 11, first)
                p1_low(b, 10)
                p1_tile(b, 12, first)
                if not last:
                    x_parts(b + 1, 0, False)
                y_tile1(b, 0, first)
                y_tile1(b, 1, first)
                p1_low(b, 11)
                g_tile1(b, 0)
                p1_tile(b, 13, first)
                g_tile1(b, 1)
                p1_low(b, 12)
                p1_low(b, 13)
                y_tile1(b, 2, first)
                y_tile1(b, 3, first)
                p1_tile(b, 14, first)
                g_tile1(b, 2)
                g_tile1(b, 3)
                p1_low(b, 14)
                g_low(b, 2)
                g_low(b, 3)
                p1_tile(b, 15, first)
                p1_low(b, 15)
                z_recip(b, 1, first)
                z_parts(b, 1, first)
                if not last:
                    o1_low(b + 1, 2)
                    o1_low(b + 1, 3)
                    x_parts(b + 1, 1, False)
                y_tile1(b, 4, first)
                y_tile1(b, 5, first)
                g_tile1(b, 4)
                g_tile1(b, 5)
                if not last:
                    h1_evac(b + 1, 0)
                g_low(b, 4)
                y_tile1(b, 6, first)
                if not last:
                    h1_evac(b + 1, 1)
                g_low(b, 5)
                y_tile1(b, 7, first)
                g_tile1(b, 6)
                g_tile1(b, 7)
                if not last:
                    h1_evac(b + 1, 2)
                g_low(b, 6)
                g_low(b, 7)
                if not last:
                    h1_evac(b + 1, 3)
                o2_low(b, 3)
                if not last:
                    o1_low(b + 1, 6)
                    o1_low(b + 1, 7)
                for t in range(NT):
                    h2_evac(b, t)
                f2_parts(b)
                max_tile(b, 0)
                if not last:
                    h1_evac(b + 1, 4)
                max_tile(b, 1)
                max_tile(b, 2)
                if not last:
                    h1_evac(b + 1, 5)
                max_tile(b, 3)
                r_columns(b, 0)
                r_parts(b, 0)
                max_tile(b, 4)
                if not last:
                    h1_evac(b + 1, 6)
                max_tile(b, 5)
                p2_step(b, 0)
                p2_step(b, 1)
                p2_low(b, 0)
                max_tile(b, 6)
                if not last:
                    h1_evac(b + 1, 7)
                    shifts(b + 1)
                p2_step(b, 2)
                max_tile(b, 7)
                r_columns(b, 1)
                p2_step(b, 3)
                r_parts(b, 1)
                p2_step(b, 4)
                if not last:
                    shifts_rest(b + 1)
                p2_step(b, 5)
                for n in range(6, 8):
                    p2_step(b, n)
                p2_step(b, 8)
                p2_step(b, 9)
                if not last:
                    b_parts(b + 1)
                p2_step(b, 10)
                p2_step(b, 11)
                z_recip(b, 2, first)
                p2_step(b, 12)
                if not last:
                    p1_tile(b + 1, 0, False)
                p2_step(b, 13)
                z_parts(b, 2, first)
                if not last:
                    p1_tile(b + 1, 1, False)
                p2_step(b, 14)
                if not last:
                    p1_tile(b + 1, 2, False)
                p2_step(b, 15)
                p2_low(b, 14)
                if not last:
                    p1_tile(b + 1, 3, False)
                p2_low(b, 15)
                y_tile2(b, 0)
                y_tile2(b, 1)
                w_tile2(b, 0)
                w_tile2(b, 1)

            dve.memset(minus1[:, :], -1.0).then_inc(S["const_ready"], 1)
            dve.memset(ones[:, :], 1.0).then_inc(S["const_ready"], 1)
            dve.memset(powh[:, :], -0.5).then_inc(S["const_ready"], 1)
            dve.wait_ge(S["ld_a"], 32)
            halves = {1: [(slice(0, O), slice(0, O)), (slice(O + 2, H + 2), slice(O, H))],
                      3: [(slice(0, O), slice(0, O))]}
            made = 0
            parts = 0
            for n, (hi, lo, K, W) in enumerate(((w1h, w1l, KF, H), (wfh, wfl, KH, H), (w2h, w2l, KH, O),
                                                (whh, whl, KO, O))):
                src = wst[:, 0:K * W].rearrange("p (k n) -> p k n", k=K)
                dve.wait_ge(S["ld_w"], 16 * n + 16)
                if n in (1, 3):
                    row = (afr, ahr)[n // 2]
                    for k in range(K):
                        for a in range(2):
                            if made >= 1:
                                dve.wait_ge(S["wa_ready"], made)
                            dve.tensor_tensor_reduce(junk[0][:, 0:W], src[:, k, :], row[:, a, :], 1.0, 0.0, ALU.mult,
                                                     ALU.add, wa[:, k, a:a + 1]).then_inc(S["wa_ready"], 1)
                            made += 1
                    dve.wait_ge(S["wa_ready"], made)
                    parts += 1
                    dve.tensor_copy(hi[:, :, O:O + 2], wa[:, 0:K, :]).then_inc(S["wh_ready"], 1)
                    dve.wait_ge(S["wh_ready"], parts)
                    dve.tensor_tensor(lo[:, :, O:O + 2], wa[:, 0:K, :], f(hi[:, :, O:O + 2]), ALU.subtract)\
                        .then_inc(S["wl_ready"], 1)
                    dve.wait_ge(S["wl_ready"], parts)
                for to, of in halves.get(n, [(slice(0, W), slice(0, W))]):
                    parts += 1
                    dve.tensor_copy(hi[:, :, to], src[:, :, of]).then_inc(S["wh_ready"], 1)
                    dve.wait_ge(S["wh_ready"], parts)
                    dve.tensor_tensor(lo[:, :, to], src[:, :, of], f(hi[:, :, to]), ALU.subtract)\
                        .then_inc(S["wl_ready"], 1)
            dve.wait_ge(S["ident0"], 2)
            dve.tensor_copy(pick[:, :], ident[0:LO + NT, 0:NT]).then_inc(S["const_ready"], 1)
            dve.tensor_scalar(rT[:, :], ident[0:LO + NT, :], 0.0, None, ALU.mult).then_inc(S["const_ready"], 1)
            dve.tensor_scalar(zT[:, :], ident[0:LO + 4, :], 0.0, None, ALU.mult).then_inc(S["const_ready"], 1)
            dve.wait_ge(S["const_ready"], 7)
            dve.tensor_copy(pick[LO:LO + NT, :], ident[LO:LO + NT, LO:LO + NT]).then_inc(S["const_ready"], 1)
            dve.wait_ge(S["const_ready"], 8)
            for t in range(NT):
                dve.wait_ge(S["ld_adj0"], 16 * t + 16)
                dve.tensor_scalar(noT[:, t, :], ast[:, 0, :], 0, None, ALU.is_le).then_inc(S["noT_ready"], 1)
                dve.wait_ge(S["ld_adj1"], 16 * t + 16)
                if t >= 2:
                    dve.wait_ge(S["st_keep"], 16 * (t - 1))
                dve.tensor_scalar(noD[:, t % 2, :], ast[:, 1, :], 0, None, ALU.is_le).then_inc(S["noD_ready"], 1)
            x_parts(0, 0, True)
            o1_low(0, 2)
            o1_low(0, 3)
            x_parts(0, 1, False)
            for t in range(4):
                h1_evac(0, t)
            o1_low(0, 6)
            o1_low(0, 7)
            for t in range(4, 8):
                h1_evac(0, t)
            shifts(0)
            shifts_rest(0)
            b_parts(0)
            for n in range(RING):
                p1_tile(0, n, True)
            body(0, True, False)
            body(1, False, False)
            with dve.Fori(2, B - 1) as b:
                body(b, False, False)
            body(B - 1, False, True)
            z_recip(B - 1, 3, False)
            z_parts(B - 1, 3, False)
            y_tile2(B - 1, 2)
            y_tile2(B - 1, 3)
            w_tile2(B - 1, 2)
            w_tile2(B - 1, 3)
            for c in range(4):
                norm_in(B - 1, c, False)
                if c >= 1:
                    norm_out(B - 1, c - 1)
            norm_out(B - 1, 3)

        @block.scalar
        def _(act):
            def o1_evac(b, p, first):
                h, m = p // 4, p % 4
                src = bank[((1, 2), (1, 0))[h][m % 2]]
                act.wait_ge(S["pe_mlp1"], 8 * b + p + 1)
                if m == 0 and not first:
                    act.wait_ge(S["g1"], 8 * b - 4 + 4 * h)
                act.activation(o1f[:, m, h * HALF:(h + 1) * HALF], src, ACT.Relu, bias=b1c[:, m:m + 1])\
                    .then_inc(S["o1_f"], 1)
                if m == 0 and not (first and h == 0):
                    act.wait_ge(S["pe_h1"], 8 * b + 4 * h)
                act.activation(o1h[:, m, :], src, ACT.Relu, bias=b1c[:, m:m + 1]).then_inc(S["o1_hi"], 1)

            def h1_hi(b, t, first):
                pr = pair[((3, 1), (3, 2))[t // 4][t % 2]]
                act.wait_ge(S["pe_h1"], NT * b + t + 1)
                if t == 0 and not first:
                    act.wait_ge(S["pe_p1"], NP_ * b)
                act.activation(h1h[:, t, :].rearrange("p (a n) -> p a n", a=2), pr[:, :, 0:O], ACT.Copy)\
                    .then_inc(S["h1_hi"], 1)

            def uvb(b, first):
                act.wait_ge(S["shift_ready"], 3 * b + 3)
                if not first:
                    act.wait_ge(S["p1_f"], NP_ * b)
                    act.wait_ge(S["pe_bT"], b)
                act.activation(uc[:, :], f2c, ACT.Exp, bias=nfa[:, 0:1])
                act.activation(vc[:, :], f2c, ACT.Exp, bias=nfb[:, 0:1], scale=ALPHA)
                act.activation(bc[:, :], sc[:, :], ACT.Exp, scale=ALPHA - 1.0).then_inc(S["uvb_ready"], 1)

            def brow_evac(b):
                act.wait_ge(S["pe_brow"], b + 1)
                act.activation(brow[:, 0:HALF], bank[0], ACT.Copy).then_inc(S["brow_ready"], 1)
                act.activation(brow[:, HALF:N], bank[1], ACT.Copy).then_inc(S["brow_ready"], 1)

            def p1_hi(b, n, first):
                act.wait_ge(S["p1_f"], NP_ * b + n + 1)
                if n >= RING:
                    act.wait_ge(S["pe_p1"], NP_ * b + n - RING + 1)
                elif not first:
                    act.wait_ge(S["pe_p2"], NP_ * b - RING + n + 1)
                act.activation(ph[:, n % RING, :], wk[:, slot1(n), :], ACT.Copy).then_inc(S["p1_hi"], 1)

            def rz_evac(b, i, first):
                act.wait_ge(S["pe_zr"], 4 * b + i + 1)
                if i == 0 and not first:
                    act.wait_ge(S["y2"], 4 * b)
                elif i == 1:
                    act.wait_ge(S["y1"], 8 * b + 4)
                elif i == 2:
                    act.wait_ge(S["y1"], 8 * b + 8)
                elif i == 3:
                    act.wait_ge(S["y2"], 4 * b + 2)
                act.activation(rz[:, :], bank[(7, 7, 2, 7)[i]], ACT.Copy).then_inc(S["rz_ready"], 1)

            def e_tile1(b, p):
                act.wait_ge(S["m1"], 8 * b + p + 1)
                act.activation(eb[:, p % 2, :], eb[:, p % 2, :], ACT.Exp).then_inc(S["e1a"], 1)
                act.wait_ge(S["e1a"], 8 * b + p + 1)
                act.activation(eb[:, p % 2, :], eb[:, p % 2, :], ACT.Exp, bias=minus1[:, 0:1]).then_inc(S["e1"], 1)

            def g_hi(b, p, first):
                h, m = p // 4, p % 4
                act.wait_ge(S["g1"], 8 * b + p + 1)
                if p == 0 and not first:
                    act.wait_ge(S["pe_p2"], NP_ * b)
                if p == 4:
                    act.wait_ge(S["pe_mlp2"], 4 * b + 2)
                act.activation(gview_h[:, m, :], yb[:, p % 2, :], ACT.Copy).then_inc(S["g1_hi"], 1)

            def o2_f(b, p, first):
                h, m = p // 2, p % 2
                act.wait_ge(S["pe_mlp2"], 4 * b + p + 1)
                if p == 0 and not first:
                    act.wait_ge(S["pe_tr"], 4 * b)
                act.activation(o2f[:, m, h * HALF:(h + 1) * HALF], bank[(2, 4)[h] + m], ACT.Relu,
                               bias=b2c[:, m:m + 1]).then_inc(S["o2_f"], 1)

            def o2_hi(b, p):
                h, m = p // 2, p % 2
                act.wait_ge(S["o2_f"], 4 * b + p + 1)
                act.wait_ge(S["pe_p1"], NP_ * b + NP_)
                n = slice(h * HALF, (h + 1) * HALF)
                act.activation(o2h[:, m, n], o2f[:, m, n], ACT.Copy).then_inc(S["o2_hi"], 1)

            def h2_hi(b, t):
                act.wait_ge(S["pe_h2"], NT * b + t + 1)
                if t == 0:
                    act.wait_ge(S["pe_mlp2"], 4 * b + 4)
                act.activation(h2h[:, t, :], bank[h2_bank[t % 4]][:, 0:O], ACT.Copy).then_inc(S["h2_hi"], 1)

            def r2(b, h, first):
                act.wait_ge(S["pe_rrow"], 2 * b + h + 1)
                if h == 1 or not first:
                    act.wait_ge(S["a2"], NP_ * b + NT * h)
                act.activation(r2row[:, :], bank[3], ACT.Copy).then_inc(S["rrow_ready"], 1)

            def r1(b, h, first):
                if h == 1 or not first:
                    act.wait_ge(S["t2"], NP_ * b + NT * h)
                act.activation(r1row[:, :], bank[2], ACT.Copy).then_inc(S["rrow_ready"], 1)

            def a_tile(b, n):
                h, j = n // NT, n % NT
                if n == 0:
                    act.wait_ge(S["g2s_ready"], 9 * b + 1)
                if j == 0:
                    act.wait_ge(S["rrow_ready"], 4 * b + 2 * h + 1)
                if n < WORK:
                    act.wait_ge(S["acc1"], NP_ * b + NP_)
                    act.wait_ge(S["p1_lo2"], NT * b + NT)
                else:
                    act.wait_ge(S["acc2"], NP_ * b + n - WORK + 1)
                    act.wait_ge(*low2(n - WORK, b))
                act.activation(wk[:, slot2(n), :], r2row[:, :], ACT.Identity, bias=g2a[:, j:j + 1])\
                    .then_inc(S["a2"], 1)

            def p2_hi(b, n):
                if n < RING:
                    act.wait_ge(S["pe_h2"], NT * b + NT)
                else:
                    act.wait_ge(S["pe_p2"], NP_ * b + n - RING + 1)
                act.wait_ge(S["p2_f"], NP_ * b + n + 1)
                act.activation(ph[:, n % RING, :], wk[:, slot2(n), :], ACT.Copy).then_inc(S["p2_hi"], 1)

            def p2_step(b, n):
                act.wait_ge(S["t2m"], NP_ * b + n + 1)
                act.activation(wk[:, slot2(n), :], wk[:, slot2(n), :], ACT.Exp, scale=GROW).then_inc(S["p2_f"], 1)
                if n + 2 == NT:
                    r2(b, 1, False)
                if n + 2 < NP_:
                    a_tile(b, n + 2)
                if n + 2 == NT:
                    r1(b, 1, False)
                p2_hi(b, n)

            def e_tile2(b, p):
                act.wait_ge(S["m2"], 4 * b + p + 1)
                act.activation(eb[:, p % 2, :], eb[:, p % 2, :], ACT.Exp).then_inc(S["e2a"], 1)
                act.wait_ge(S["e2a"], 4 * b + p + 1)
                act.activation(eb[:, p % 2, :], eb[:, p % 2, :], ACT.Exp, bias=minus1[:, 0:1]).then_inc(S["e2"], 1)

            def body(b, first, last):
                p1_hi(b, 4, first)
                if not first:
                    rz_evac(b - 1, 3, False)
                    e_tile2(b - 1, 2)
                    e_tile2(b - 1, 3)
                for n in range(5, 10):
                    p1_hi(b, n, first)
                p1_hi(b, 10, first)
                p1_hi(b, 11, first)
                rz_evac(b, 0, first)
                e_tile1(b, 0)
                e_tile1(b, 1)
                g_hi(b, 0, first)
                g_hi(b, 1, first)
                p1_hi(b, 12, first)
                p1_hi(b, 13, first)
                e_tile1(b, 2)
                e_tile1(b, 3)
                p1_hi(b, 14, first)
                g_hi(b, 2, first)
                g_hi(b, 3, first)
                p1_hi(b, 15, first)
                o2_f(b, 0, first)
                o2_f(b, 1, first)
                if not last:
                    for m in range(4):
                        o1_evac(b + 1, m, False)
                rz_evac(b, 1, first)
                e_tile1(b, 4)
                e_tile1(b, 5)
                if not last:
                    h1_hi(b + 1, 0, False)
                g_hi(b, 4, first)
                g_hi(b, 5, first)
                if not last:
                    h1_hi(b + 1, 1, False)
                e_tile1(b, 6)
                e_tile1(b, 7)
                if not last:
                    h1_hi(b + 1, 2, False)
                g_hi(b, 6, first)
                g_hi(b, 7, first)
                if not last:
                    h1_hi(b + 1, 3, False)
                o2_hi(b, 0)
                o2_hi(b, 1)
                if not last:
                    o1_evac(b + 1, 4, False)
                    o1_evac(b + 1, 5, False)
                for p in (2, 3):
                    o2_f(b, p, first)
                    o2_hi(b, p)
                if not last:
                    o1_evac(b + 1, 6, False)
                    o1_evac(b + 1, 7, False)
                for t in range(NT):
                    h2_hi(b, t)
                if not last:
                    for t in range(4, 7):
                        h1_hi(b + 1, t, False)
                r2(b, 0, first)
                r1(b, 0, first)
                a_tile(b, 0)
                a_tile(b, 1)
                if not last:
                    h1_hi(b + 1, 7, False)
                for n in range(NP_):
                    p2_step(b, n)
                    if n == 4 and not last:
                        uvb(b + 1, False)
                    if n == 10 and not last:
                        brow_evac(b + 1)
                    if n == 15:
                        rz_evac(b, 2, first)
                if not last:
                    p1_hi(b + 1, 0, False)
                    p1_hi(b + 1, 1, False)
                e_tile2(b, 0)
                e_tile2(b, 1)
                if not last:
                    p1_hi(b + 1, 2, False)
                    p1_hi(b + 1, 3, False)

            act.wait_ge(S["ld_b"], 32)
            act.wait_ge(S["const_ready"], 8)
            act.wait_ge(S["wl_ready"], WPARTS)
            for m in range(4):
                o1_evac(0, m, True)
            for t in range(4):
                h1_hi(0, t, True)
            for m in range(4, 8):
                o1_evac(0, m, True)
            for t in range(4, 8):
                h1_hi(0, t, True)
            uvb(0, True)
            brow_evac(0)
            for n in range(RING):
                p1_hi(0, n, True)
            act.wait_ge(S["noT_ready"], NT)
            act.wait_ge(S["noD_ready"], NT)
            body(0, True, False)
            with act.Fori(1, B - 1) as b:
                body(b, False, False)
            body(B - 1, False, True)
            rz_evac(B - 1, 3, False)
            e_tile2(B - 1, 2)
            e_tile2(B - 1, 3)

        @block.gpsimd
        def _(pool):
            def sub(out_, a, b_, s):
                pool.tensor_tensor(out_, a, b_, ALU.subtract).then_inc(S[s], 1)

            def o1_lo(b, p):
                h, m = p // 4, p % 4
                pool.wait_ge(S["o1_hi"], 8 * b + p + 1)
                sub(o1l[:, m, :], o1f[:, m, h * HALF:(h + 1) * HALF], f(o1h[:, m, :]), "o1_lo")

            def all_max(b):
                if isinstance(b, int) and b == 0:
                    pool.wait_ge(S["col_max"], 1)
                pool.partition_all_reduce(fall[:, :], fmx[:, :], P, RMAX).then_inc(S["all_max"], 1)

            def p1_low(b, n):
                pool.wait_ge(S["p1_hi"], NP_ * b + n + 1)
                sub(pl[:, n % RING, :], wk[:, slot1(n), :], f(ph[:, n % RING, :]), "p1_lo")

            def acc1(b, n, first):
                h, j = n // NT, n % NT
                if j == 0:
                    return
                pool.wait_ge(S["p1_f"], NP_ * b + n + 1)
                a = acc[:, h, :]
                if j == 1:
                    if not first:
                        pool.wait_ge(S["pe_zc"], 4 * b - 1 + h)
                    pool.tensor_tensor(a, wk[:, slot1(n - 1), :], wk[:, slot1(n), :], ALU.add).then_inc(S["acc1"], 2)
                else:
                    pool.wait_ge(S["acc1"], NP_ * b + n)
                    pool.tensor_tensor(a, a, wk[:, slot1(n), :], ALU.add).then_inc(S["acc1"], 1)

            def g_lo(b, p):
                m = p % 4
                pool.wait_ge(S["g1_hi"], 8 * b + p + 1)
                sub(gview_l[:, m, :], yb[:, p % 2, :], f(gview_h[:, m, :]), "g1_lo")

            def o2_lo(b, p):
                h, m = p // 2, p % 2
                pool.wait_ge(S["o2_hi"], 4 * b + p + 1)
                n = slice(h * HALF, (h + 1) * HALF)
                sub(o2l[:, m, n], o2f[:, m, n], f(o2h[:, m, n]), "o2_lo")

            def acc2(b, n, last):
                h, j = n // NT, n % NT
                if j == 0:
                    return
                pool.wait_ge(S["p2_f"], NP_ * b + n + 1)
                a = acc[:, h, :]
                if j == 1:
                    pool.wait_ge(S["pe_zc"], 4 * b + 1 + h)
                    if h == 0 and not last:
                        pool.wait_ge(S["col_max"], b + 2)
                    pool.tensor_tensor(a, wk[:, slot2(n - 1), :], wk[:, slot2(n), :], ALU.add).then_inc(S["acc2"], 2)
                else:
                    pool.wait_ge(S["acc2"], NP_ * b + n)
                    pool.tensor_tensor(a, a, wk[:, slot2(n), :], ALU.add).then_inc(S["acc2"], 1)

            def p2_low(b, n):
                pool.wait_ge(S["p2_hi"], NP_ * b + n + 1)
                sub(pl[:, n % RING, :], wk[:, slot2(n), :], f(ph[:, n % RING, :]), "p2_lo2")

            def rstd(b, c):
                pool.wait_ge(S["mv_ready"], 8 * b + 2 * c + 2)
                pool.tensor_tensor(rst[:, c % 2, :], bmv[:, c % 2, :, 1], epsc[:, :], ALU.add).then_inc(S["ve_ready"], 1)
                pool.wait_ge(S["ve_ready"], 4 * b + c + 1)
                pool.tensor_tensor(rsd[:, c % 2, :], rst[:, c % 2, :], powh[:, 0:2], ALU.pow).then_inc(S["rs_ready"], 1)

            def body(b, first, last):
                for n in range(RING, 10):
                    if not first and n in (5, 6, 7, 8):
                        rstd(b - 1, n - 5)
                    if n < 8:
                        p1_low(b, n)
                    acc1(b, n, first)
                for n in range(10, NP_):
                    acc1(b, n, first)
                    if n == 11:
                        g_lo(b, 0)
                        g_lo(b, 1)
                if not last:
                    for m in range(2):
                        o1_lo(b + 1, m)
                o2_lo(b, 0)
                o2_lo(b, 1)
                if not last:
                    for m in range(4, 6):
                        o1_lo(b + 1, m)
                o2_lo(b, 2)
                for n in range(NP_):
                    if on_pool(n):
                        p2_low(b, n)
                    acc2(b, n, last)
                    if n == 1 and not last:
                        all_max(b + 1)
                if not last:
                    for n in range(RING):
                        p1_low(b + 1, n)
                        acc1(b + 1, n, False)

            pool.memset(ident[:, :], 0.0).then_inc(S["ident0"], 1)
            pool.wait_ge(S["ident0"], 1)
            pool.affine_select(out=ident[:, :], in_=ident[:, :], compare_op=ALU.not_equal, fill=1.0, base=0,
                               pattern=[[-1, P]], channel_multiplier=1).then_inc(S["ident0"], 1)
            pool.memset(epsc[:, :], EPS).then_inc(S["const_ready"], 1)
            pool.wait_ge(S["const_ready"], 8)
            for m in range(2):
                o1_lo(0, m)
            for m in range(4, 6):
                o1_lo(0, m)
            all_max(0)
            for n in range(RING):
                p1_low(0, n)
                acc1(0, n, True)
            body(0, True, False)
            with pool.Fori(1, B - 1) as b:
                body(b, False, False)
            body(B - 1, False, True)
            for c in range(4):
                rstd(B - 1, c)


def kernel(x, adj, L0_gnn_mlp1_w, L0_gnn_mlp1_b, L0_gnn_mlp2_w, L0_gnn_mlp2_b, L0_gnn_W_fc, L0_gnn_a_fc,
           L0_gnn_W_hand, L0_gnn_a_hand):
    import numpy as np
    import concourse.bacc as bacc
    from concourse.bass_utils import run_bass_kernel_spmd as run

    x = np.asarray(x)
    B, N, F = x.shape
    H, O = L0_gnn_mlp1_w.shape[1], L0_gnn_mlp2_w.shape[1]
    half, p = N // 2, 128
    c = np.ascontiguousarray
    arrays = {
        "xT": c(x.reshape(B, 2, half, F // p, p).transpose(0, 1, 4, 3, 2).reshape(B * 2 * p, -1)),
        "x": c(x.reshape(B, 4, 2, p, F).transpose(0, 1, 3, 2, 4).reshape(B * 4 * p, -1)),
        "adj": c(np.asarray(adj)),
        "adjT": c(np.asarray(adj).T),
        "w1": c(np.asarray(L0_gnn_mlp1_w)),
        "b1": c(np.asarray(L0_gnn_mlp1_b).reshape(H // p, p).T),
        "w2": c(np.asarray(L0_gnn_mlp2_w)),
        "b2": c(np.asarray(L0_gnn_mlp2_b).reshape(O // p, p).T),
        "wf": c(np.asarray(L0_gnn_W_fc)),
        "af": c(np.asarray(L0_gnn_a_fc).reshape(-1)),
        "wh": c(np.asarray(L0_gnn_W_hand)),
        "ah": c(np.asarray(L0_gnn_a_hand).reshape(-1)),
    }
    nc = bacc.Bacc("TRN2", target_bir_lowering=False, num_devices=1)
    aps = {n: nc.dram_tensor(f"in_{n}", a.shape, mybir.dt.from_np(a.dtype), kind="ExternalInput").ap()
           for n, a in arrays.items()}
    keep = nc.dram_tensor("no_edge", (N, N), U8).ap()
    out = nc.dram_tensor("out", (B * 4 * p, 2 * F), F32, kind="ExternalOutput").ap()
    gnn_layer_kernel(nc, aps["xT"], aps["x"], aps["adj"], aps["adjT"], aps["w1"], aps["b1"], aps["w2"], aps["b2"],
                     aps["wf"], aps["af"], aps["wh"], aps["ah"], keep, out)
    r = run(nc, [{f"in_{n}": a for n, a in arrays.items()}], core_ids=[0])
    return r.results[0]["out"].reshape(B, 4, p, 2, F).transpose(0, 1, 3, 2, 4).reshape(B, N, F)
```
